# Optimizing a Trainium2 kernel written in Bass

```python
import numpy as np
import jax
import jax.numpy as jnp

def _softmax(x, axis=-1):
    return jax.nn.softmax(x, axis=axis)

def _gelu(x):
    return jax.nn.gelu(x, approximate=True)

def _silu(x):
    return jax.nn.silu(x)

def _sigmoid(x):
    return jax.nn.sigmoid(x)

def _layernorm(x, axis=-1, eps=1e-05):
    m = jnp.mean(x, axis=axis, keepdims=True)
    v = jnp.var(x, axis=axis, keepdims=True)
    return (x - m) / jnp.sqrt(v + eps)

def _scatter_add(tgt, idx, src, axis=0):
    return tgt.at[idx].add(src)

def _segment_sum(src, seg, n):
    return jax.ops.segment_sum(src, seg, n)
kernel_name = 'mk_adaln_d1_jaxref_r4_10b095'

def setup_inputs(seed: int=0):
    np.random.seed(seed)
    _w = jnp.asarray

    def _L0_attn_setup():
        import jax, jax.numpy as jnp
        import numpy as np
        D_MODEL = 512
        N_HEADS = 16
        D_K = D_MODEL // N_HEADS
        key = jax.random.key(seed)
        ks = jax.random.split(key, 9)
        B, S = (2, 512)
        s = 1.0 / np.sqrt(D_MODEL)
        inp = {'x': jax.random.normal(ks[0], (B, S, D_MODEL), dtype=jnp.float32), 'w_q': jax.random.uniform(ks[1], (D_MODEL, D_MODEL), jnp.float32, -s, s), 'b_q': jax.random.uniform(ks[2], (D_MODEL,), jnp.float32, -s, s), 'w_k': jax.random.uniform(ks[3], (D_MODEL, D_MODEL), jnp.float32, -s, s), 'b_k': jax.random.uniform(ks[4], (D_MODEL,), jnp.float32, -s, s), 'w_v': jax.random.uniform(ks[5], (D_MODEL, D_MODEL), jnp.float32, -s, s), 'b_v': jax.random.uniform(ks[6], (D_MODEL,), jnp.float32, -s, s), 'w_o': jax.random.uniform(ks[7], (D_MODEL, D_MODEL), jnp.float32, -s, s), 'b_o': jax.random.uniform(ks[8], (D_MODEL,), jnp.float32, -s, s)}
        return inp
    _L0_attn_in = _L0_attn_setup()

    def _L0_ffn_setup():
        import jax, jax.numpy as jnp
        import numpy as np
        E = 32
        G = 8
        TKG = 4
        K = 4
        D = 512
        H = 256
        HS = 1024
        SCALE = 2.5
        CAP = 256

        def relu2(x):
            r = jnp.maximum(x, 0.0)
            return r * r

        def route_tokens(scores, bias_corr):
            T = scores.shape[0]
            scores_c = scores + bias_corr
            group_scores = jax.lax.top_k(scores_c.reshape(T, G, E // G), 2)[0].sum(-1)
            _, group_idx = jax.lax.top_k(group_scores, TKG)
            group_mask = jnp.zeros((T, G), scores.dtype).at[jnp.arange(T)[:, None], group_idx].set(1.0)
            score_mask = jnp.repeat(group_mask, E // G, axis=1)
            masked = jnp.where(score_mask > 0, scores_c, 0.0)
            _, topk_idx = jax.lax.top_k(masked, K)
            topk_w = jnp.take_along_axis(scores, topk_idx, axis=1)
            topk_w = topk_w / (topk_w.sum(-1, keepdims=True) + 1e-20)
            return (topk_idx, topk_w * SCALE)
        key = jax.random.key(seed)
        ks = jax.random.split(key, 6)
        B, S = (2, 512)
        return dict(hidden_states=jax.random.normal(ks[0], (B, S, D), jnp.float32), gate_w=jax.random.normal(ks[1], (E, D), jnp.float32) * 0.02, bias_corr=jnp.zeros((E,), jnp.float32), up_w=jax.random.normal(ks[2], (E, H, D), jnp.float32) * 0.02, down_w=jax.random.normal(ks[3], (E, D, H), jnp.float32) * 0.02, shared_up_w=jax.random.normal(ks[4], (HS, D), jnp.float32) * 0.02, shared_down_w=jax.random.normal(ks[5], (D, HS), jnp.float32) * 0.02)
    _L0_ffn_in = _L0_ffn_setup()
    _L0_c = _w((lambda *s: np.random.randn(*s).astype(np.float32) * 0.05)(8, 512))
    _L0_wmod = _w((lambda *s: np.random.randn(*s).astype(np.float32) * 0.05)(512, 6 * 512) * 512 ** (-0.5))
    _d = {'L0_attn_x': _L0_attn_in['x'], 'L0_attn_w_q': _L0_attn_in['w_q'], 'L0_attn_b_q': _L0_attn_in['b_q'], 'L0_attn_w_k': _L0_attn_in['w_k'], 'L0_attn_b_k': _L0_attn_in['b_k'], 'L0_attn_w_v': _L0_attn_in['w_v'], 'L0_attn_b_v': _L0_attn_in['b_v'], 'L0_attn_w_o': _L0_attn_in['w_o'], 'L0_attn_b_o': _L0_attn_in['b_o'], 'L0_ffn_gate_w': _L0_ffn_in['gate_w'], 'L0_ffn_bias_corr': _L0_ffn_in['bias_corr'], 'L0_ffn_up_w': _L0_ffn_in['up_w'], 'L0_ffn_down_w': _L0_ffn_in['down_w'], 'L0_ffn_shared_up_w': _L0_ffn_in['shared_up_w'], 'L0_ffn_shared_down_w': _L0_ffn_in['shared_down_w'], 'L0_c': _L0_c, 'L0_wmod': _L0_wmod}
    _x0 = _d['L0_attn_x']
    _d['L0_attn_x'] = jax.random.normal(jax.random.fold_in(jax.random.key(seed), 1), (8, 1024, 512), dtype=_x0.dtype)
    del _x0
    return _d

def reference(L0_attn_x, L0_attn_w_q, L0_attn_b_q, L0_attn_w_k, L0_attn_b_k, L0_attn_w_v, L0_attn_b_v, L0_attn_w_o, L0_attn_b_o, L0_ffn_gate_w, L0_ffn_bias_corr, L0_ffn_up_w, L0_ffn_down_w, L0_ffn_shared_up_w, L0_ffn_shared_down_w, L0_c, L0_wmod):

    def _L0_attn_ref(x, w_q, b_q, w_k, b_k, w_v, b_v, w_o, b_o):
        import jax, jax.numpy as jnp
        import numpy as np
        D_MODEL = 512
        N_HEADS = 16
        D_K = D_MODEL // N_HEADS
        B, S, _ = x.shape

        def proj(w, b):
            return (x @ w.T + b).reshape(B, S, N_HEADS, D_K).transpose(0, 2, 1, 3)
        q = proj(w_q, b_q)
        k = proj(w_k, b_k)
        v = proj(w_v, b_v)
        scores = jnp.einsum('bhqd,bhkd->bhqk', q, k) / np.sqrt(D_K).astype(np.float32)
        causal = jnp.tril(jnp.ones((S, S), dtype=bool))
        scores = jnp.where(causal, scores, -jnp.inf)
        attn = jax.nn.softmax(scores, axis=-1)
        out = jnp.einsum('bhqk,bhkd->bqhd', attn, v).reshape(B, S, D_MODEL)
        return out @ w_o.T + b_o

    def _L0_ffn_ref(hidden_states, gate_w, bias_corr, up_w, down_w, shared_up_w, shared_down_w):
        import jax, jax.numpy as jnp
        import numpy as np
        E = 32
        G = 8
        TKG = 4
        K = 4
        D = 512
        H = 256
        HS = 1024
        SCALE = 2.5
        CAP = 256

        def relu2(x):
            r = jnp.maximum(x, 0.0)
            return r * r

        def route_tokens(scores, bias_corr):
            T = scores.shape[0]
            scores_c = scores + bias_corr
            group_scores = jax.lax.top_k(scores_c.reshape(T, G, E // G), 2)[0].sum(-1)
            _, group_idx = jax.lax.top_k(group_scores, TKG)
            group_mask = jnp.zeros((T, G), scores.dtype).at[jnp.arange(T)[:, None], group_idx].set(1.0)
            score_mask = jnp.repeat(group_mask, E // G, axis=1)
            masked = jnp.where(score_mask > 0, scores_c, 0.0)
            _, topk_idx = jax.lax.top_k(masked, K)
            topk_w = jnp.take_along_axis(scores, topk_idx, axis=1)
            topk_w = topk_w / (topk_w.sum(-1, keepdims=True) + 1e-20)
            return (topk_idx, topk_w * SCALE)
        B, S, _ = hidden_states.shape
        T = B * S
        flat = hidden_states.reshape(T, D)
        logits = flat @ gate_w.T
        scores = jax.nn.sigmoid(logits)
        topk_idx, topk_w = route_tokens(scores, bias_corr)
        e_flat = topk_idx.reshape(-1)
        oh = jax.nn.one_hot(e_flat, E, dtype=jnp.int32)
        pos = jnp.take_along_axis(jnp.cumsum(oh, axis=0) - 1, e_flat[:, None], axis=1)[:, 0]
        tok = jnp.repeat(jnp.arange(T), K)
        valid = pos < CAP
        xe = jnp.zeros((E, CAP, D), flat.dtype).at[e_flat, pos].set(flat[tok], mode='drop')
        h = relu2(jnp.einsum('ecd,ehd->ech', xe, up_w))
        ye = jnp.einsum('ech,edh->ecd', h, down_w)
        gathered = ye[e_flat, jnp.minimum(pos, CAP - 1)]
        gathered = jnp.where(valid[:, None], gathered, 0.0) * topk_w.reshape(-1)[:, None]
        routed = gathered.reshape(T, K, D).sum(axis=1).reshape(B, S, D)
        shared = relu2(hidden_states @ shared_up_w.T) @ shared_down_w.T
        return routed + shared
    x = L0_attn_x
    mod = (_silu(L0_c) @ L0_wmod).reshape(L0_c.shape[0], 6, 1, -1)
    sa, ca, ga, sb, cb, gb = (mod[:, 0], mod[:, 1], mod[:, 2], mod[:, 3], mod[:, 4], mod[:, 5])
    ga = (2 * (ga >= 0) - 1) * jnp.maximum(jnp.abs(ga), 0.25)
    gb = (2 * (gb >= 0) - 1) * jnp.maximum(jnp.abs(gb), 0.25)
    h = _layernorm(x, axis=-1) * (1 + ca) + sa
    x = x + ga * _L0_attn_ref(h, L0_attn_w_q, L0_attn_b_q, L0_attn_w_k, L0_attn_b_k, L0_attn_w_v, L0_attn_b_v, L0_attn_w_o, L0_attn_b_o)
    h = _layernorm(x, axis=-1) * (1 + cb) + sb
    x = x + gb * _L0_ffn_ref(h, L0_ffn_gate_w, L0_ffn_bias_corr, L0_ffn_up_w, L0_ffn_down_w, L0_ffn_shared_up_w, L0_ffn_shared_down_w)
    return x

_drawn_inputs = setup_inputs


def setup_inputs(seed=0):
    import zlib

    import numpy as np

    out = dict(_drawn_inputs(seed))
    spreads = {'L0_ffn_bias_corr': (0.0, 0.593)}
    factors = {'L0_attn_w_q': 8.0,
     'L0_attn_b_q': 8.0,
     'L0_attn_w_k': 8.0,
     'L0_attn_b_k': 64.0,
     'L0_attn_w_v': 7.307,
     'L0_attn_b_v': 8.0,
     'L0_attn_w_o': 6.573,
     'L0_attn_b_o': 8.0,
     'L0_ffn_gate_w': 5.004,
     'L0_ffn_up_w': 5.108,
     'L0_ffn_down_w': 4.659,
     'L0_ffn_shared_up_w': 6.233,
     'L0_ffn_shared_down_w': 5.704}
    for name, (base, spread) in spreads.items():
        noise = np.random.default_rng([zlib.crc32(name.encode()), seed]).standard_normal(out[name].shape)
        drawn = base * np.exp(spread * noise) if base else spread * noise
        out[name] = jnp.asarray(drawn.astype(out[name].dtype))
    for name, factor in factors.items():
        out[name] = (out[name] * factor).astype(out[name].dtype)
    return out
```

```python
import numpy as np
import concourse.bass as bass
from concourse import mybir
from contextlib import ExitStack

FP32 = mybir.dt.float32
F32R = mybir.dt.float32r
BF16 = mybir.dt.bfloat16
I32 = mybir.dt.int32
U32 = mybir.dt.uint32
ALU = mybir.AluOpType
ACT = mybir.ActivationFunctionType
AX = mybir.AxisListType

P = 128
NB, S, D = 8, 1024, 512
T = NB * S
DK = D // P
HD = 32
NG = D // P
GH = P // HD
UNIT = 512
UT = UNIT // P
HALVES = S // UNIT
NE, NGR, EPG = 32, 8, 4
TOPG, TOPK = 4, 4
HID, HS, CAP = 256, 1024, 256
ROUTE_SCALE = 2.5
EPS = 1e-5
MASKED = -1.0e30
QHI, QLO, KHI, KLO = range(4)
SLOTS = NE * CAP
M_SA, M_CA, M_GA, M_SB, M_CB, M_GB = range(6)


def raw(ap):
    return ap.bitcast(FP32)


class Chain:

    def __init__(self, eng, sem, base):
        self.eng, self.sem, self.base, self.n = eng, sem, base, 0

    def done(self, ins):
        self.n += 1
        ins.then_inc(self.sem, 1)

    def wait(self):
        self.eng.wait_ge(self.sem, self.base + self.n)


class Credited:

    def __init__(self, sem, credit):
        self.sem, self.credit = sem, credit

    def open(self, eng):
        eng.sem_inc(self.sem, self.credit)

    def wait(self, eng, value):
        eng.wait_ge(self.sem, value + self.credit)


def hold(eng, sem, value, mark):
    eng.wait_ge(sem, value)
    eng.sem_inc(mark, 1)


class Scope:

    def __init__(self, nc, ctx, prefix):
        self.nc, self.ctx, self.prefix = nc, ctx, prefix

    def sb(self, name, shape, dt):
        return self.ctx.enter_context(self.nc.sbuf_tensor(self.prefix + name, shape, dt))

    def ps(self, name, shape=(P, 512), dt=FP32):
        return self.ctx.enter_context(self.nc.psum_tensor(self.prefix + name, list(shape), dt))

    def sem(self, name):
        return self.ctx.enter_context(self.nc.semaphore(self.prefix + name))

    def sems(self, name, n):
        return [self.sem(f"{name}{i}") for i in range(n)]


STAT_LINKS, ROOT_LINKS = 2, 5


def combine_stats(chain, stats, mv, tmp):
    dve = chain.eng
    total, diff, m2 = tmp[:, :, 0], tmp[:, :, 1], tmp[:, :, 2]
    dve.tensor_tensor(total, stats[:, :, 1], stats[:, :, 4], ALU.add)
    dve.tensor_tensor(diff, stats[:, :, 1], stats[:, :, 4], ALU.subtract)
    chain.done(dve.tensor_tensor(m2, stats[:, :, 2], stats[:, :, 5], ALU.add))
    chain.wait()
    dve.tensor_scalar_mul(mv[:, :, 0], total, 0.5)
    dve.tensor_scalar(m2, m2, 1.0 / D, EPS, ALU.mult, ALU.add)
    chain.done(dve.scalar_tensor_tensor(diff, diff, 0.25, diff, op0=ALU.mult, op1=ALU.mult))
    chain.wait()
    return dve.tensor_tensor(mv[:, :, 1], m2, diff, ALU.add)


def inverse_root(chain, rstd, std, var, y):
    dve = chain.eng
    r = rstd[:, :]
    for op in (lambda: dve.reciprocal(r, std[:, :]),
               lambda: dve.tensor_tensor(y, r, r, ALU.mult),
               lambda: dve.tensor_tensor(y, y, var, ALU.mult),
               lambda: dve.tensor_scalar(y, y, -0.5, 1.5, ALU.mult, ALU.add),
               lambda: dve.tensor_tensor(r, r, y, ALU.mult)):
        chain.done(op())
        chain.wait()


def stage_modulation(nc, cT, wmod, mod_dram, h2_dram, info_dram, out):
    with ExitStack() as ctx:
        s = Scope(nc, ctx, "mod_")
        c_sb = s.sb("c", [P, DK, NB], FP32)
        sig = s.sb("sig", [P, DK, NB], FP32)
        silu = s.sb("silu", [P, DK, NB], FP32)
        w_sb = s.sb("w", [P, DK, 6 * D], FP32)
        res = s.sb("res", [NB, 6, D], FP32)
        sign = s.sb("sign", [NB, 2, D], FP32)
        mag = s.sb("mag", [NB, 2, D], FP32)
        ps = [s.ps(f"ps{j}", (NB, D)) for j in range(6)]
        SP_TILES = SLOTS // P
        zero = s.sb("zero", [P, D], FP32)
        pad_i = s.sb("pad_i", [P, SP_TILES], I32)
        info = s.sb("info", [P, SP_TILES, 2], FP32)
        pool_own, info_done = s.sem("pool_own"), s.sem("info")
        loaded, sig_done, silu_done = s.sem("loaded"), s.sem("sig"), s.sem("silu")
        mm, own, ready, stored = s.sem("mm"), s.sem("own"), s.sem("ready"), s.sem("stored")
        gates = (M_GA, M_GB)
        block = ctx.enter_context(nc.Block())

        @block.sync
        def _(sp):
            sp.dma_start(c_sb[:, :, :], cT.rearrange("(k p) b -> p k b", p=P)).then_inc(loaded, 16)
            sp.dma_start(w_sb[:, :, :], wmod.rearrange("(k p) n -> p k n", p=P)).then_inc(loaded, 16)
            sp.wait_ge(info_done, 1)
            for r in range(CAP // P):
                sp.dma_start(h2_dram[T + r * P:T + (r + 1) * P, :], zero[:, :]).then_inc(stored, 16)
                sp.dma_start(out[T + r * P:T + (r + 1) * P, :], zero[:, :]).then_inc(stored, 16)
            sp.dma_start(info_dram.rearrange("(n p) c -> p n c", p=P), info[:, :, :]).then_inc(stored, 16)
            sp.dma_start(mod_dram[NB:NB + 1, :, :].rearrange("b j d -> (b j) d"), zero[0:6, :]).then_inc(stored, 16)
            sp.wait_ge(ready, 1)
            sp.dma_start(mod_dram[0:NB, :, :], res[:, :, :]).then_inc(stored, 16)
            sp.wait_ge(stored, 16 * (2 * CAP // P + 3))

        @block.gpsimd
        def _(pool):
            pool.memset(zero[:, :], 0.0)
            pool.memset(info[:, :, :], 0.0)
            pool.iota(pad_i[:, :], pattern=[[0, NE], [P, CAP // P]], base=T, channel_multiplier=1).then_inc(pool_own, 1)
            pool.wait_ge(pool_own, 1)
            pool.tensor_copy(info[:, :, 0], pad_i[:, :]).then_inc(info_done, 1)

        @block.scalar
        def _(act):
            act.wait_ge(loaded, 32)
            act.activation(sig[:, :, :], c_sb[:, :, :], ACT.Sigmoid).then_inc(sig_done, 1)

        @block.tensor
        def _(pe):
            pe.wait_ge(silu_done, 1)
            for j in range(6):
                for k in range(DK):
                    last = pe.matmul(ps[j][:, :], silu[:, k, :], w_sb[:, k, j * D:(j + 1) * D],
                                     start=k == 0, stop=k == DK - 1)
                last.then_inc(mm, 1)

        @block.vector
        def _(dve):
            chain = Chain(dve, own, 0)
            dve.wait_ge(sig_done, 1)
            dve.tensor_tensor(silu[:, :, :], c_sb[:, :, :], sig[:, :, :], ALU.mult).then_inc(silu_done, 1)
            for j in range(6):
                dve.wait_ge(mm, j + 1)
                if j in (M_CA, M_CB):
                    last = dve.tensor_scalar_add(res[:, j, :], ps[j][:, :], 1.0)
                else:
                    last = dve.tensor_copy(res[:, j, :], ps[j][:, :])
            chain.done(last)
            chain.wait()
            for n, j in enumerate(gates):
                dve.tensor_scalar(sign[:, n, :], res[:, j, :], 0.0, 2.0, ALU.is_ge, ALU.mult)
                last = dve.tensor_scalar(mag[:, n, :], res[:, j, :], -1.0, 0.25, ALU.mult, ALU.max)
            chain.done(last)
            chain.wait()
            for n, j in enumerate(gates):
                last = dve.tensor_tensor(mag[:, n, :], mag[:, n, :], res[:, j, :], ALU.max)
            chain.done(last)
            chain.wait()
            for n, j in enumerate(gates):
                last = dve.scalar_tensor_tensor(res[:, j, :], sign[:, n, :], -1.0, mag[:, n, :],
                                                op0=ALU.add, op1=ALU.mult)
            last.then_inc(ready, 1)


def make_identity(pool, tile, own, n):
    pool.memset(tile[:, :], 0.0).then_inc(own, 1)
    pool.wait_ge(own, n + 1)
    pool.affine_select(out=tile[:, :], in_=tile[:, :], compare_op=ALU.not_equal, fill=1.0, base=0,
                       pattern=[[-1, tile.shape[1]]], channel_multiplier=1).then_inc(own, 1)
    return n + 2


def stage_qkv(nc, x, wqkvT, bqk, bv, mod_dram, qk_dram, v_dram):
    with ExitStack() as ctx:
        s = Scope(nc, ctx, "qkv_")
        x_sb = [s.sb(f"x{p}", [P, UT, D], FP32) for p in range(2)]
        wraw = s.sb("wraw", [P, DK, D], FP32)
        w_hi = [s.sb(f"w_hi{j}", [P, DK, D], F32R) for j in range(3)]
        w_lo = [s.sb(f"w_lo{j}", [P, DK, D], F32R) for j in range(3)]
        hT_hi = [s.sb(f"hT_hi{p}", [P, DK, UNIT], F32R) for p in range(2)]
        hT_lo = [s.sb(f"hT_lo{p}", [P, DK, UNIT], F32R) for p in range(2)]
        mod = s.sb("mod", [P, 2, D], FP32)
        bqk_sb = s.sb("bqk", [P, 2 * NG], FP32)
        bv_sb = s.sb("bv", [P, D], FP32)
        ident = s.sb("ident", [P, P], FP32)
        stats = s.sb("stats", [P, UT, 6], FP32)
        mv = s.sb("mv", [P, UT, 2], FP32)
        std = s.sb("std", [P, UT], FP32)
        rstd = s.sb("rstd", [P, UT], FP32)
        tmp = s.sb("tmp", [P, UT, 3], FP32)
        RING, BANKS = 4, 6
        out_hi = [s.sb(f"out_hi{n}", [P, UNIT], F32R) for n in range(RING)]
        out_lo = [s.sb(f"out_lo{n}", [P, UNIT], F32R) for n in range(RING)]
        out_v = [s.sb(f"out_v{n}", [P, D], FP32) for n in range(UT)]
        ps_t = [s.ps(f"ps_t{n}") for n in range(2)]
        ps_m = [s.ps(f"ps_m{n}") for n in range(BANKS)]

        w_loaded, w_hi_done, w_lo_done = s.sem("w_loaded"), s.sem("w_hi_done"), s.sem("w_lo_done")
        consts, pool_own, dve_own = s.sem("consts"), s.sem("pool_own"), s.sem("dve_own")
        x_in, mod_in = s.sems("x_in", 2), s.sem("mod_in")
        var_done, std_done, norm_done, h_done = s.sem("var"), s.sem("std"), s.sem("norm"), s.sem("h")
        mul_done = s.sem("mul")
        tr_done, hi_done, lo_done = s.sem("tr"), s.sem("hi"), s.sem("lo")
        mm_done, ehi_done, elo_done, ev_done = s.sem("mm"), s.sem("ehi"), s.sem("elo"), s.sem("ev")
        qk_out, v_out = s.sems("qk_out", RING), s.sems("v_out", UT)
        NQK = 2 * NG
        NM = NQK + UT
        mm_done, lo_done = Credited(mm_done, NM), Credited(lo_done, 1)
        elo_done, ev_done = Credited(elo_done, 1), Credited(ev_done, UT)
        block = ctx.enter_context(nc.Block())
        LAST = NB - 1

        def steps(eng, body):
            with eng.Fori(0, LAST) as b:
                for half in range(HALVES):
                    body(b, half, True)
            for half in range(HALVES):
                body(LAST, half, half + 1 < HALVES)

        @block.sync
        def _(sp):
            def load_x(b, half):
                src = x[bass.ds(b, 1), half * UNIT:(half + 1) * UNIT, :]
                sp.dma_start(x_sb[half][:, :, :], src.rearrange("o (t p) d -> p (o t) d", p=P)).then_inc(x_in[half], 16)

            def load_mod(b):
                for m, j in enumerate((M_SA, M_CA)):
                    sp.dma_start(mod[:, m, :], mod_dram[bass.ds(b, 1), j, :].broadcast_to([P, D])).then_inc(mod_in, 16)

            load_x(0, 0)
            load_mod(0)
            for j in range(3):
                if j:
                    sp.wait_ge(w_lo_done, j)
                sp.dma_start(wraw[:, :, :], wqkvT[j].rearrange("(k p) n -> p k n", p=P)).then_inc(w_loaded, 16)
            sp.dma_start(bqk_sb[:, :], bqk[:, :]).then_inc(consts, 16)
            sp.dma_start(bv_sb[:, :], bv[:, :].broadcast_to([P, D])).then_inc(consts, 16)
            load_x(0, 1)

            def body(b, half, more):
                u = b * HALVES + half
                if more or half == 0:
                    if not isinstance(b, int) or b < LAST:
                        sp.wait_ge(tr_done, DK * (u + 1))
                        load_x(b + 1, half)
                        if half == 0:
                            sp.wait_ge(h_done, UT * (u + 2))
                            load_mod(b + 1)
                for n in range(NQK):
                    elo_done.wait(sp, NQK * u + n + 1)
                    which, g = (QHI, n) if n < NG else (KHI, n - NG)
                    for part, tile in ((0, out_hi), (1, out_lo)):
                        dst = qk_dram[which + part, bass.ds(b * NG + g, 1), :, half * UNIT:(half + 1) * UNIT]
                        sp.dma_start(dst.rearrange("o p t -> (o p) t"), raw(tile[n % RING][:, :])).then_inc(qk_out[n % RING], 16)
                for t in range(UT):
                    ev_done.wait(sp, UT * u + t + 1)
                    tok = half * UNIT + t * P
                    dst = v_dram[bass.ds(b * NG, NG), tok:tok + P, :]
                    sp.dma_start(dst.rearrange("g t j -> t g j"),
                                 out_v[t][:, :].rearrange("p (g j) -> p g j", g=NG)).then_inc(v_out[t], 16)

            steps(sp, body)
            units = NB * HALVES
            for n in range(RING):
                sp.wait_ge(qk_out[n], 32 * (NQK // RING) * units)
            for t in range(UT):
                sp.wait_ge(v_out[t], 16 * units)

        @block.gpsimd
        def _(pool):
            make_identity(pool, ident, pool_own, 0)

            def modulate(u, half, b):
                pool.wait_ge(mod_in, 32 * (b + 1))
                for t in range(UT):
                    pool.wait_ge(norm_done, UT * u + t + 1)
                    xt = x_sb[half][:, t, :]
                    pool.tensor_tensor(xt, xt, mod[:, 1, :], ALU.mult).then_inc(mul_done, 1)
                    pool.wait_ge(mul_done, UT * u + t + 1)
                    pool.tensor_tensor(xt, xt, mod[:, 0, :], ALU.add).then_inc(h_done, 1)

            modulate(0, 0, 0)

            def body(b, half, more):
                if more:
                    u = b * HALVES + half
                    modulate(u + 1, 1 - half, b + half)

            steps(pool, body)

        @block.scalar
        def _(act):
            for j in range(3):
                act.wait_ge(w_loaded, 16 * (j + 1))
                act.activation(w_hi[j][:, :, :], wraw[:, :, :], ACT.Copy).then_inc(w_hi_done, 1)
            act.wait_ge(consts, 32)

            def root(u):
                act.wait_ge(var_done, u + 1)
                act.activation(std[:, :], mv[:, :, 1], ACT.Sqrt).then_inc(std_done, 1)

            root(0)

            def body(b, half, more):
                u = b * HALVES + half
                mm_done.wait(act, NM * (u - 1))
                for k in range(DK):
                    act.wait_ge(tr_done, DK * u + k + 1)
                    act.activation(hT_hi[half][:, k, :], ps_t[k % 2][:, :], ACT.Copy).then_inc(hi_done, 1)
                if more:
                    root(u + 1)
                for n in range(NQK):
                    mm_done.wait(act, NM * u + n + 1)
                    use = (NQK // RING) * u + n // RING
                    act.wait_ge(qk_out[n % RING], 32 * use)
                    act.activation(out_hi[n % RING][:, :], ps_m[n % BANKS][:, :], ACT.Identity,
                                   bias=bqk_sb[:, n:n + 1]).then_inc(ehi_done, 1)

            steps(act, body)

        @block.vector
        def _(dve):
            for free in (lo_done, elo_done, ev_done):
                free.open(dve)
            for j in range(3):
                dve.wait_ge(w_hi_done, j + 1)
                dve.tensor_tensor(w_lo[j][:, :, :], wraw[:, :, :], raw(w_hi[j][:, :, :]), ALU.subtract).then_inc(w_lo_done, 1)
            dve.wait_ge(consts, 32)
            LINKS = 1 + STAT_LINKS + ROOT_LINKS

            def layernorm(u, half, b):
                chain = Chain(dve, dve_own, LINKS * u)
                dve.wait_ge(x_in[half], 16 * (b + 1))
                for t in range(UT):
                    last = dve.bn_stats(stats[:, t, :], x_sb[half][:, t, :])
                chain.done(last)
                chain.wait()
                combine_stats(chain, stats, mv, tmp).then_inc(var_done, 1)
                dve.wait_ge(std_done, u + 1)
                dve.wait_ge(var_done, u + 1)
                inverse_root(chain, rstd, std, mv[:, :, 1], tmp[:, :, 0])
                assert chain.n == LINKS
                for t in range(UT):
                    dve.tensor_scalar(x_sb[half][:, t, :], x_sb[half][:, t, :], mv[:, t, 0:1], rstd[:, t:t + 1],
                                      ALU.subtract, ALU.mult).then_inc(norm_done, 1)

            layernorm(0, 0, 0)

            def body(b, half, more):
                u = b * HALVES + half
                for k in range(DK):
                    dve.wait_ge(hi_done, DK * u + k + 1)
                    dve.tensor_tensor(hT_lo[half][:, k, :], ps_t[k % 2][:, :], raw(hT_hi[half][:, k, :]),
                                      ALU.subtract).then_inc(lo_done.sem, 1)
                if more:
                    layernorm(u + 1, 1 - half, b + half)
                for n in range(NQK):
                    dve.wait_ge(ehi_done, NQK * u + n + 1)
                    dve.scalar_tensor_tensor(out_lo[n % RING][:, :], ps_m[n % BANKS][:, :], bqk_sb[:, n:n + 1],
                                             raw(out_hi[n % RING][:, :]), op0=ALU.add, op1=ALU.subtract).then_inc(elo_done.sem, 1)
                for t in range(UT):
                    mm_done.wait(dve, NM * u + NQK + t + 1)
                    dve.wait_ge(v_out[t], 16 * u)
                    dve.tensor_tensor(out_v[t][:, :], ps_m[(NQK + t) % BANKS][:, :], bv_sb[:, :], ALU.add).then_inc(ev_done.sem, 1)

            steps(dve, body)

        @block.tensor
        def _(pe):
            mm_done.open(pe)
            pe.wait_ge(pool_own, 2)

            def body(b, half, more):
                u = b * HALVES + half
                pe.wait_ge(h_done, UT * (u + 1))
                for k in range(DK):
                    lo_done.wait(pe, DK * u + k - 1)
                    for t in range(UT):
                        last = pe.transpose(ps_t[k % 2][:, t * P:(t + 1) * P], x_sb[half][:, t, k * P:(k + 1) * P], ident[:, :])
                    last.then_inc(tr_done, 1)
                pe.wait_ge(w_lo_done, 3)
                lo_done.wait(pe, DK * (u + 1))
                for n in range(NM):
                    if n < BANKS:
                        if n < BANKS - UT:
                            elo_done.wait(pe, NQK * u - (BANKS - UT) + n + 1)
                        else:
                            ev_done.wait(pe, UT * u - UT + (n - (BANKS - UT)) + 1)
                    else:
                        elo_done.wait(pe, NQK * u + n - BANKS + 1)
                    for k in range(DK):
                        for a, c in ((0, 0), (0, 1), (1, 0)):
                            h_part = (hT_hi, hT_lo)[a][half]
                            if n < NQK:
                                w_part = (w_hi, w_lo)[c][n // NG]
                                last = pe.matmul(ps_m[n % BANKS][:, :], w_part[:, k, (n % NG) * P:(n % NG + 1) * P],
                                                 h_part[:, k, :], start=k == 0 and a + c == 0, stop=k == DK - 1 and a == 1)
                            else:
                                t = n - NQK
                                last = pe.matmul(ps_m[n % BANKS][:, :], h_part[:, k, t * P:(t + 1) * P],
                                                 (w_hi, w_lo)[c][2][:, k, :], start=k == 0 and a + c == 0, stop=k == DK - 1 and a == 1)
                    last.then_inc(mm_done.sem, 1)

            steps(pe, body)


def stage_attention(nc, qk_dram, v_dram, o_dram):
    STACK = 3 * HD
    ROWS = STACK + 2
    KT = S // P
    QH = S // UNIT
    GROUPS = NB * NG
    SLOT = 3
    NPT = 2 * GH
    with ExitStack() as ctx:
        s = Scope(nc, ctx, "att_")
        qs = [s.sb(f"qs{i}", [ROWS, GH, S], F32R) for i in range(SLOT)]
        ks = [s.sb(f"ks{i}", [ROWS, GH, S], F32R) for i in range(SLOT)]
        vs = [s.sb(f"vs{i}", [P, KT, P], FP32) for i in range(SLOT)]
        pt = [s.sb(f"pt{i}", [P, UNIT], FP32) for i in range(NPT)]
        rsum = s.sb("rsum", [P, UNIT], FP32)
        o32 = [s.sb(f"o32_{i}", [P, UNIT], FP32) for i in range(QH)]
        oT_hi = [s.sb(f"oT_hi{i}", [P, UNIT], F32R) for i in range(QH)]
        oT_lo = [s.sb(f"oT_lo{i}", [P, UNIT], F32R) for i in range(QH)]
        rowmax = s.sb("rowmax", [P, GH * KT], FP32)
        m_hi = s.sb("m_hi", [GH * KT, P], F32R)
        m_lo = s.sb("m_lo", [GH * KT, P], F32R)
        ones = s.sb("ones", [P, HD], FP32)
        ident = s.sb("ident", [P, P], FP32)
        ident16 = s.sb("ident16", [P, P], BF16)
        mask_q = s.sb("mask_q", [P, P], BF16)
        mask_k = s.sb("mask_k", [P, P], BF16)
        ps_s = [s.ps(f"ps_s{i}", (P, 2 * 512)) for i in range(2)]
        ps_p = [s.ps(f"ps_p{i}") for i in range(2)]
        ps_o, ps_sum = s.ps("ps_o"), s.ps("ps_sum")

        q_in, v_in, m_in = s.sems("q_in", SLOT), s.sems("v_in", SLOT), s.sems("m_in", SLOT)
        pool_own, consts, dve_own = s.sem("pool_own"), s.sem("consts"), s.sem("dve_own")
        s_done, max_done = s.sem("s"), Credited(s.sem("max"), 2)
        mt_done, mhi_done, mlo_done = s.sem("mt"), s.sem("mhi"), s.sem("mlo")
        p_done, exp_done, pv_done = s.sem("p"), Credited(s.sem("exp"), 2), Credited(s.sem("pv"), 2)
        o_free, ohi_done, olo_done = s.sem("o_free"), s.sem("ohi"), s.sem("olo")
        o_out = s.sems("o_out", QH)
        block = ctx.enter_context(nc.Block())

        order1 = [(h, t) for a in range(KT // 2) for t in (KT - 1 - a, a) for h in range(GH)]
        chunks = [(qh, kt) for qh in range(QH) for kt in range((qh + 1) * UNIT // P)]
        N1, NC = len(order1), len(chunks)
        NP = NC * GH
        TURN = NC - 2
        share = [min(N1, N1 * c // TURN) for c in range(1, NC + 1)]
        BEFORE = [(share[c - 1] if c else 0, share[c]) for c in range(NC)]

        class Group:
            def __init__(self, g, slot, use):
                self.g, self.slot, self.use = g, slot, use

            def ahead(self, n):
                slot = self.slot + n
                return Group(self.g + n, slot % SLOT, self.use + slot // SLOT)

        def steps(step):
            FULL = (GROUPS - 3) // SLOT

            def run(eng):
                first = Group(0, 0, 0)
                step(first, None)
                with eng.Fori(0, FULL) as i:
                    for j in range(SLOT):
                        prev = Group(i * SLOT + j, j, i)
                        step(prev.ahead(1), prev)
                for g in range(FULL * SLOT, GROUPS):
                    prev = first.ahead(g)
                    step(prev.ahead(1) if g + 1 < GROUPS else None, prev)
            return run

        @block.sync
        def _(sp):
            def load(G):
                for tile, parts in ((qs, (QHI, QHI, QLO)), (ks, (KHI, KLO, KHI))):
                    for r, part in enumerate(parts):
                        src = qk_dram[part, bass.ds(G.g, 1), :, :].rearrange("o (h d) t -> d (o h) t", d=HD)
                        sp.dma_start(raw(tile[G.slot][r * HD:(r + 1) * HD, :, :]), src).then_inc(q_in[G.slot], 16)
                src = v_dram[bass.ds(G.g, 1), :, :].rearrange("o (k p) j -> p (o k) j", p=P)
                sp.dma_start(vs[G.slot][:, :, :], src).then_inc(v_in[G.slot], 16)

            def step(cur, prev):
                if prev and cur is not None and (not isinstance(cur.g, int) or cur.g + 1 < GROUPS):
                    pv_done.wait(sp, NC * prev.g)
                    load(cur.ahead(1))
                if cur:
                    sp.wait_ge(mlo_done, cur.g + 1)
                    for row, part in ((STACK, m_hi), (STACK + 1, m_lo)):
                        sp.dma_start(raw(qs[cur.slot][row:row + 1, :, :]).rearrange("o h (q t) -> o (h q) t", q=KT),
                                     raw(part[:, :])).then_inc(m_in[cur.slot], 16)
                if prev:
                    for qh in range(QH):
                        sp.wait_ge(olo_done, QH * prev.g + qh + 1)
                        for part, tile in ((0, oT_hi), (1, oT_lo)):
                            dst = o_dram[part, bass.ds(prev.g, 1), :, qh * UNIT:(qh + 1) * UNIT]
                            sp.dma_start(dst.rearrange("o p t -> (o p) t"), raw(tile[qh][:, :])).then_inc(o_out[qh], 16)

            load(Group(0, 0, 0))
            load(Group(1, 1, 0))
            steps(step)(sp)
            for qh in range(QH):
                sp.wait_ge(o_out[qh], 32 * GROUPS)

        @block.gpsimd
        def _(pool):
            n = make_identity(pool, ident, pool_own, 0)
            n = make_identity(pool, ident16, pool_own, n)
            pool.memset(mask_q[:, :], 0.0).then_inc(pool_own, 1)
            pool.memset(mask_k[:, :], 0.0).then_inc(pool_own, 1)
            pool.memset(ones[:, :], 1.0).then_inc(pool_own, 1)
            pool.wait_ge(pool_own, n + 3)
            pool.affine_select(out=mask_q[:, :], in_=mask_q[:, :], compare_op=ALU.is_ge, fill=MASKED, base=0,
                               pattern=[[-1, P]], channel_multiplier=1).then_inc(pool_own, 1)
            pool.affine_select(out=mask_k[:, :], in_=mask_k[:, :], compare_op=ALU.is_ge, fill=MASKED, base=0,
                               pattern=[[1, P]], channel_multiplier=-1).then_inc(pool_own, 1)
            for i in range(SLOT):
                pool.wait_ge(pool_own, n + 5 + i)
                pool.memset(raw(ks[i][STACK:ROWS, :, :]), 1.0).then_inc(pool_own, 1)
            pool.wait_ge(pool_own, n + 5 + SLOT)
            pool.sem_inc(consts, 1)

            def step(cur, prev):
                if prev:
                    for qh in range(QH):
                        pool.wait_ge(ohi_done, QH * prev.g + qh + 1)
                        pool.tensor_tensor(oT_lo[qh][:, :], o32[qh][:, :], raw(oT_hi[qh][:, :]),
                                           ALU.subtract).then_inc(olo_done, 1)

            steps(step)(pool)

        @block.scalar
        def _(act):
            exp_done.open(act)

            def step(cur, prev):
                if not prev:
                    return
                for c, (qh, kt) in enumerate(chunks):
                    col = max(kt * P - qh * UNIT, 0)
                    for h in range(GH):
                        n = c * GH + h
                        if h == 0:
                            pv_done.wait(act, NC * prev.g + c - 1)
                        act.wait_ge(p_done, NP * prev.g + n + 1)
                        act.activation(pt[n % NPT][:, col:UNIT], ps_p[n % 2][:, col:UNIT], ACT.Exp,
                                       scale=float(HD) ** -0.5).then_inc(exp_done.sem, 1)

            steps(step)(act)

        @block.vector
        def _(dve):
            max_done.open(dve)

            def step(cur, prev):
                def maxima(lo, hi):
                    for i in range(lo, hi):
                        h, t = order1[i]
                        dve.wait_ge(s_done, N1 * cur.g + i + 1)
                        dve.reduce_max(rowmax[:, h * KT + t:h * KT + t + 1], ps_s[i % 2][:, 0:(t + 1) * P],
                                       axis=AX.X).then_inc(max_done.sem, 1)

                def negate():
                    dve.wait_ge(mt_done, cur.g + 1)
                    if prev:
                        dve.wait_ge(m_in[prev.slot], 32 * (prev.use + 1))
                    top = ps_s[0][0:GH * KT, 0:P]
                    dve.tensor_scalar_mul(m_hi[:, :], top, -1.0).then_inc(mhi_done, 1)
                    dve.wait_ge(mhi_done, cur.g + 1)
                    dve.scalar_tensor_tensor(m_lo[:, :], top, -1.0, raw(m_hi[:, :]),
                                             op0=ALU.mult, op1=ALU.subtract).then_inc(mlo_done, 1)

                if not prev:
                    maxima(0, N1)
                    negate()
                    return
                def normalise(qh, c):
                    pv_done.wait(dve, NC * prev.g + c + 1)
                    dve.wait_ge(olo_done, QH * prev.g)
                    dve.wait_ge(o_out[qh], 32 * prev.g)
                    dve.reciprocal(rsum[:, :], ps_sum[:, :]).then_inc(dve_own, 1)
                    dve.wait_ge(dve_own, QH * prev.g + qh + 1)
                    dve.tensor_tensor(o32[qh][:, :], ps_o[:, :], rsum[:, :], ALU.mult).then_inc(o_free, 1)
                    dve.wait_ge(o_free, QH * prev.g + qh + 1)
                    dve.tensor_copy(oT_hi[qh][:, :], o32[qh][:, :]).then_inc(ohi_done, 1)

                for c, (qh, kt) in enumerate(chunks):
                    if cur:
                        maxima(*BEFORE[c])
                        if c == TURN:
                            negate()
                    if kt == 0 and qh:
                        normalise(qh - 1, c - 1)
                normalise(QH - 1, NC - 1)

            steps(step)(dve)

        @block.tensor
        def _(pe):
            pv_done.open(pe)
            pe.wait_ge(consts, 1)

            def step(cur, prev):
                def scores(lo, hi):
                    for i in range(lo, hi):
                        h, t = order1[i]
                        max_done.wait(pe, N1 * cur.g + i - 1)
                        if i == 0 and prev:
                            pe.wait_ge(mlo_done, cur.g)
                        top, bank = (t + 1) * P, ps_s[i % 2]
                        for c0 in range(0, top, 512):
                            c1 = min(c0 + 512, top)
                            pe.matmul(bank[:, c0:c1], qs[cur.slot][0:STACK, h, t * P:top],
                                      ks[cur.slot][0:STACK, h, c0:c1], start=True, stop=c1 < top)
                        pe.matmul(bank[:, t * P:top], ident16[:, :], mask_q[:, :], start=False, stop=True).then_inc(s_done, 1)

                def accumulate(c, acc, lhs):
                    qh, kt = chunks[c]
                    col = max(kt * P - qh * UNIT, 0)
                    for h in range(GH):
                        last = pe.matmul(acc[h * HD:(h + 1) * HD, col:UNIT], lhs(h), pt[(c * GH + h) % NPT][:, col:UNIT],
                                         start=kt == 0, stop=kt == (qh + 1) * UNIT // P - 1)
                    return last

                def weigh(c):
                    qh, kt = chunks[c]
                    if kt == 0:
                        pe.wait_ge(o_free, QH * prev.g + qh)
                    exp_done.wait(pe, NP * prev.g + (c + 1) * GH)
                    accumulate(c, ps_o, lambda h: vs[prev.slot][:, kt, h * HD:(h + 1) * HD])

                def total(c):
                    accumulate(c, ps_sum, lambda h: ones[:, :]).then_inc(pv_done.sem, 1)

                def turn():
                    max_done.wait(pe, N1 * (cur.g + 1))
                    pe.transpose(ps_s[0][0:GH * KT, 0:P], rowmax[:, :], ident[:, :]).then_inc(mt_done, 1)

                if cur:
                    pe.wait_ge(q_in[cur.slot], 96 * (cur.use + 1))
                if not prev:
                    scores(0, N1)
                    turn()
                    return
                for c, (qh, kt) in enumerate(chunks):
                    col = max(kt * P - qh * UNIT, 0)
                    q0 = qh * UNIT + col
                    diag = kt * P >= qh * UNIT
                    if cur:
                        scores(*BEFORE[c])
                        if c == TURN:
                            turn()
                    if c == 0:
                        pe.wait_ge(m_in[prev.slot], 32 * (prev.use + 1))
                        pe.wait_ge(v_in[prev.slot], 16 * (prev.use + 1))
                    for h in range(GH):
                        n = c * GH + h
                        exp_done.wait(pe, NP * prev.g + n - 1)
                        last = pe.matmul(ps_p[n % 2][:, col:UNIT], ks[prev.slot][:, h, kt * P:(kt + 1) * P],
                                         qs[prev.slot][:, h, q0:(qh + 1) * UNIT], start=True, stop=not diag)
                        if diag:
                            last = pe.matmul(ps_p[n % 2][:, col:col + P], ident16[:, :], mask_k[:, :], start=False, stop=True)
                        last.then_inc(p_done, 1)
                        if c and h == 1:
                            weigh(c - 1)
                        if c and h == 2:
                            total(c - 1)
                weigh(NC - 1)
                total(NC - 1)

            steps(step)(pe)


def stage_project_route_shared(nc, x, o_dram, mod_dram, woT, bo, gateT, bias, upT, downT, h2_dram, info_dram, out):
    UP = HS // P
    RING = 4
    with ExitStack() as ctx:
        s = Scope(nc, ctx, "ffn_")
        wo_hi, wo_lo = s.sb("wo_hi", [P, DK, D], F32R), s.sb("wo_lo", [P, DK, D], F32R)
        up_hi, up_lo = s.sb("up_hi", [P, DK, HS], F32R), s.sb("up_lo", [P, DK, HS], F32R)
        dn_hi, dn_lo = s.sb("dn_hi", [P, UP, D], F32R), s.sb("dn_lo", [P, UP, D], F32R)
        gt_hi, gt_lo = s.sb("gt_hi", [P, DK, NE], F32R), s.sb("gt_lo", [P, DK, NE], F32R)
        o_hi, o_lo = s.sb("o_hi", [P, NG, UNIT], F32R), s.sb("o_lo", [P, NG, UNIT], F32R)
        x_sb = [s.sb(f"x{p}", [P, UT, D], FP32) for p in range(2)]
        h2 = s.sb("h2", [P, UT, D], FP32)
        hT_hi, hT_lo = s.sb("hT_hi", [P, DK, UNIT], F32R), s.sb("hT_lo", [P, DK, UNIT], F32R)
        a_hi, a_lo = s.sb("a_hi", [P, UP, UNIT], F32R), s.sb("a_lo", [P, UP, UNIT], F32R)
        relu = [s.sb(f"relu{i}", [P, UNIT], FP32) for i in range(2)]
        att = s.sb("att", [P, D], FP32)
        mod = s.sb("mod", [P, 3, D], FP32)
        gb = s.sb("gb", [P, D], FP32)
        bo_sb = s.sb("bo", [P, D], FP32)
        bias_sb = s.sb("bias", [P, NE], FP32)
        ident = s.sb("ident", [P, P], FP32)
        before = s.sb("before", [P, P], BF16)
        ones = s.sb("ones", [P, P], BF16)
        stats, tmp = s.sb("stats", [P, UT, 6], FP32), s.sb("tmp", [P, UT, 3], FP32)
        mv, std, rstd = s.sb("mv", [P, UT, 2], FP32), s.sb("std", [P, UT], FP32), s.sb("rstd", [P, UT], FP32)
        UG = UT * NGR
        score, biased = s.sb("score", [P, UT, NE], FP32), s.sb("biased", [P, UT, NE], FP32)
        masked = s.sb("masked", [P, UT, NE], FP32)
        pair_hi, pair_lo = s.sb("pair_hi", [P, UG, 2], FP32), s.sb("pair_lo", [P, UG, 2], FP32)
        grp = s.sb("grp", [P, 3, UG], FP32)
        ahead, ties = s.sb("ahead", [P, UG, NGR], FP32), s.sb("ties", [P, UG, NGR], FP32)
        earlier_i, earlier = s.sb("earlier_i", [P, NGR, NGR], I32), s.sb("earlier", [P, NGR, NGR], FP32)
        chosen = s.sb("chosen", [P, UG], I32)
        top, top_idx = s.sb("top", [P, UT, 8], FP32), s.sb("top_idx", [P, UT, 8], U32)
        expert = s.sb("expert", [P, UT, TOPK], FP32)
        iota_i, iota = s.sb("iota_i", [P, NE], I32), s.sb("iota", [P, NE], FP32)
        onehot, picked = s.sb("onehot", [P, UT, TOPK, NE], FP32), s.sb("picked", [P, UT, TOPK, NE], FP32)
        weight, den = s.sb("weight", [P, UT, TOPK], FP32), s.sb("den", [P, UT], FP32)
        sel, sel_acc = s.sb("sel", [P, UT, NE], BF16), s.sb("sel_acc", [P, NE], BF16)
        sel_sum = s.sb("sel_sum", [P, NE], FP32)
        place, over = s.sb("place", [P, UT, TOPK], FP32), s.sb("over", [P, UT, TOPK], FP32)
        tok_i, tok = s.sb("tok_i", [P, UT], I32), s.sb("tok", [P, UT], FP32)
        slot = [s.sb(f"slot{p}", [P, UT * TOPK], I32) for p in range(2)]
        info = [s.sb(f"info{p}", [P, UT * TOPK, 2], FP32) for p in range(2)]

        ps_t = [s.ps(f"ps_t{n}") for n in range(2)]
        ps_m = [s.ps(f"ps_m{n}") for n in range(RING)]
        ps_g, ps_pos = s.ps("ps_g"), s.ps("ps_pos")

        wraw = (h2, x_sb[1])
        w_in, w_hi_done, w_lo_done = s.sems("w_in", 2), s.sem("w_hi"), s.sem("w_lo")
        consts, pool_own, iotas, mark = s.sem("consts"), s.sem("pool_own"), s.sem("iotas"), s.sem("mark")
        o_in, x_in, mod_in, gb_in = s.sem("o_in"), s.sems("x_in", 2), s.sem("mod_in"), s.sem("gb_in")
        dve_own, var_done, std_done, norm_done = s.sem("dve_own"), s.sem("var"), s.sem("std"), s.sem("norm")
        mul_done, h_done = s.sem("mul"), s.sem("h")
        tr_done, hi_done, lo_done = s.sem("tr"), s.sem("hi"), Credited(s.sem("lo"), 1)
        gate_done, score_done, sel_done, pos_done = s.sem("gate"), s.sem("score"), s.sem("sel"), s.sem("pos")
        up_done, relu_done = Credited(s.sem("up"), UP), s.sem("relu")
        sq_done, ahi_done, alo_done = s.sem("sq"), s.sem("ahi"), Credited(s.sem("alo"), 2)
        proj_done, att_done = s.sem("proj"), s.sem("att")
        down_done, fin_done, out_done = Credited(s.sem("down"), UT), Credited(s.sem("fin"), UT), s.sem("out")
        slot_done = s.sem("slot")
        h2_out, x_out, scattered = s.sem("h2_out"), s.sems("x_out", 2), s.sems("scattered", 2)
        block = ctx.enter_context(nc.Block())
        LAST = NB - 1

        def steps(eng, body):
            with eng.Fori(0, LAST) as b:
                for half in range(HALVES):
                    body(b, half, True)
            for half in range(HALVES):
                body(LAST, half, half + 1 < HALVES)

        def piece(src, hi, lo, k0, k1):
            return src.rearrange("(k p) n -> p k n", p=P)[:, k0:k1, :], hi[:, k0:k1, :], lo[:, k0:k1, :]
        pieces = [piece(woT, wo_hi, wo_lo, 0, DK), piece(gateT, gt_hi, gt_lo, 0, DK)]
        pieces += [piece(upT, up_hi, up_lo, k, k + 2) for k in range(0, DK, 2)]
        pieces += [piece(downT, dn_hi, dn_lo, k, k + 4) for k in range(0, UP, 4)]
        NW = len(pieces)

        def raw_piece(n):
            k, w = pieces[n][1].shape[1:]
            return wraw[n % 2][:, :, :].rearrange("p a b -> p (a b)")[:, 0:k * w].rearrange("p (a b) -> p a b", a=k)

        @block.sync
        def _(sp):
            def load_o(b, half):
                for part, tile in ((0, o_hi), (1, o_lo)):
                    src = o_dram[part, bass.ds(b * NG, NG), :, half * UNIT:(half + 1) * UNIT]
                    sp.dma_start(raw(tile[:, :, :]), src.rearrange("g p t -> p g t")).then_inc(o_in, 16)

            def load_x(b, half):
                src = x[bass.ds(b, 1), half * UNIT:(half + 1) * UNIT, :]
                sp.dma_start(x_sb[half][:, :, :], src.rearrange("o (t p) d -> p (o t) d", p=P)).then_inc(x_in[half], 16)

            def load_mod(b):
                for m, j in enumerate((M_GA, M_CB, M_SB)):
                    sp.dma_start(mod[:, m, :], mod_dram[bass.ds(b, 1), j, :].broadcast_to([P, D])).then_inc(mod_in, 16)

            def load_gb(b):
                sp.dma_start(gb[:, :], mod_dram[bass.ds(b, 1), M_GB, :].broadcast_to([P, D])).then_inc(gb_in, 16)

            def store_h2(b, half):
                u = b * HALVES + half
                sp.wait_ge(h_done, UT * (u + 1))
                dst = h2_dram[bass.ds(u * UNIT, UNIT), :]
                sp.dma_start(dst.rearrange("(t p) d -> p t d", p=P), h2[:, :, :]).then_inc(h2_out, 16)

            load_o(0, 0)
            load_x(0, 0)
            load_mod(0)
            load_gb(0)
            sp.dma_start(bo_sb[:, :], bo[:, :].broadcast_to([P, D])).then_inc(consts, 16)
            sp.dma_start(bias_sb[:, :], bias[:, :].broadcast_to([P, NE])).then_inc(consts, 16)
            for n in range(NW):
                if n >= 2:
                    sp.wait_ge(w_lo_done, n - 1)
                sp.dma_start(raw_piece(n), pieces[n][0]).then_inc(w_in[n % 2], 16)
            sp.wait_ge(w_lo_done, NW)
            load_x(0, 1)
            sp.wait_ge(proj_done, UT)
            load_o(0, 1)
            store_h2(0, 0)

            def body(b, half, more):
                u = b * HALVES + half
                if more:
                    nb, nhalf = (b, 1) if half == 0 else (b + 1, 0)
                    if half == 0:
                        has_next2 = not (isinstance(b, int) and b == LAST)
                    else:
                        has_next2 = True
                    if has_next2:
                        sp.wait_ge(proj_done, UT * (u + 2))
                        load_o(b + 1, half)
                    store_h2(nb, nhalf)
                    if half == 0 and has_next2:
                        load_mod(b + 1)
                sp.wait_ge(out_done, UT * (u + 1))
                dst = out[bass.ds(u * UNIT, UNIT), :]
                sp.dma_start(dst.rearrange("(t p) d -> p t d", p=P), x_sb[half][:, :, :]).then_inc(x_out[half], 16)
                if not (isinstance(b, int) and b == LAST):
                    sp.wait_ge(x_out[half], 16 * (b + 1))
                    load_x(b + 1, half)
                    if half == 1:
                        load_gb(b + 1)

            steps(sp, body)
            sp.wait_ge(h2_out, 16 * NB * HALVES)
            for p in range(2):
                sp.wait_ge(x_out[p], 16 * NB)
                sp.wait_ge(scattered[p], 16 * UT * TOPK * NB)

        @block.gpsimd
        def _(pool):
            n = make_identity(pool, ident, pool_own, 0)
            pool.memset(ones[:, :], 1.0).then_inc(pool_own, 1)
            pool.memset(before[:, :], 1.0).then_inc(pool_own, 1)
            pool.wait_ge(pool_own, n + 2)
            pool.affine_select(out=before[:, :], in_=before[:, :], compare_op=ALU.is_gt, fill=0.0, base=0,
                               pattern=[[1, P]], channel_multiplier=-1).then_inc(pool_own, 1)
            pool.iota(earlier_i[:, :, :], pattern=[[1, NGR], [-1, NGR]], base=0, channel_multiplier=0)
            pool.iota(iota_i[:, :], pattern=[[1, NE]], base=0, channel_multiplier=0)
            pool.iota(tok_i[:, :], pattern=[[P, UT]], base=0, channel_multiplier=1).then_inc(iotas, 1)

            def modulate(b, half):
                u = b * HALVES + half
                for t in range(UT):
                    pool.wait_ge(norm_done, UT * u + t + 1)
                    ht = h2[:, t, :]
                    pool.tensor_tensor(ht, ht, mod[:, 1, :], ALU.mult).then_inc(mul_done, 1)
                    pool.wait_ge(mul_done, UT * u + t + 1)
                    pool.tensor_tensor(ht, ht, mod[:, 2, :], ALU.add).then_inc(h_done, 1)

            modulate(0, 0)

            def body(b, half, more):
                u = b * HALVES + half
                if more:
                    modulate(*((b, 1) if half == 0 else (b + 1, 0)))
                hold(pool, slot_done, u + 1, mark)
                for j in range(UT * TOPK):
                    pool.indirect_dma_start(
                        info_dram[:, :], bass.IndirectOffsetOnAxis(slot[half][:, j:j + 1].bitcast(U32), 0),
                        info[half][:, j, :], None, bounds_check=SLOTS - 1, oob_is_err=False).then_inc(scattered[half], 16)

            steps(pool, body)

        @block.scalar
        def _(act):
            up_free = down_done
            for n in range(NW):
                act.wait_ge(w_in[n % 2], 16 * (n // 2 + 1))
                act.activation(pieces[n][1], raw_piece(n), ACT.Copy).then_inc(w_hi_done, 1)

            def root(u):
                act.wait_ge(var_done, u + 1)
                act.activation(std[:, :], mv[:, :, 1], ACT.Sqrt).then_inc(std_done, 1)

            root(0)

            def body(b, half, more):
                u = b * HALVES + half
                up_done.wait(act, UP * u)
                for k in range(DK):
                    act.wait_ge(tr_done, DK * u + k + 1)
                    act.activation(hT_hi[:, k, :], ps_t[k % 2][:, :], ACT.Copy).then_inc(hi_done, 1)
                down_done.wait(act, UT * u)

                def high(n):
                    act.wait_ge(sq_done, UP * u + n + 1)
                    act.activation(a_hi[:, n, :], relu[n % 2][:, :], ACT.Copy).then_inc(ahi_done, 1)

                for n in range(UP):
                    up_done.wait(act, UP * u + n + 1)
                    alo_done.wait(act, UP * u + n - 1)
                    act.activation(relu[n % 2][:, :], ps_m[n % RING][:, :], ACT.Relu).then_inc(relu_done, 1)
                    if n:
                        high(n - 1)
                high(UP - 1)
                if more:
                    root(u + 1)
                act.wait_ge(gate_done, u + 1)
                act.activation(score[:, :, :].rearrange("p t e -> p (t e)"), ps_g[:, 0:UT * NE], ACT.Sigmoid).then_inc(score_done, 1)

            steps(act, body)

        @block.vector
        def _(dve):
            for free in (lo_done, alo_done, fin_done):
                free.open(dve)
            dve.wait_ge(iotas, 1)
            dve.tensor_single_scalar(earlier[:, :, :], earlier_i[:, :, :], 0, op=ALU.is_gt)
            dve.tensor_copy(iota[:, :], iota_i[:, :])
            dve.tensor_copy(tok[:, :], tok_i[:, :])
            dve.memset(sel_acc[:, :], 0.0)
            dve.memset(sel_sum[:, :], 0.0)
            for n in range(NW):
                dve.wait_ge(w_hi_done, n + 1)
                dve.tensor_tensor(pieces[n][2], raw_piece(n), raw(pieces[n][1]), ALU.subtract).then_inc(w_lo_done, 1)
            dve.wait_ge(consts, 32)
            LINKS = 2 * UT + 1 + STAT_LINKS + ROOT_LINKS

            def attend(b, half):
                u = b * HALVES + half
                chain = Chain(dve, dve_own, LINKS * u)
                xs = x_sb[half]
                dve.wait_ge(x_in[half], 16 * (b + 1))
                dve.wait_ge(mod_in, 48 * (b + 1))
                for t in range(UT):
                    dve.wait_ge(proj_done, UT * u + t + 1)
                    dve.tensor_tensor(att[:, :], ps_m[t % RING][:, :], bo_sb[:, :], ALU.add).then_inc(att_done, 1)
                    dve.wait_ge(att_done, UT * u + t + 1)
                    chain.done(dve.tensor_tensor(att[:, :], att[:, :], mod[:, 0, :], ALU.mult))
                    chain.wait()
                    chain.done(dve.tensor_tensor(xs[:, t, :], xs[:, t, :], att[:, :], ALU.add))
                    chain.wait()
                    last = dve.bn_stats(stats[:, t, :], xs[:, t, :])
                chain.done(last)
                chain.wait()
                combine_stats(chain, stats, mv, tmp).then_inc(var_done, 1)
                dve.wait_ge(std_done, u + 1)
                dve.wait_ge(var_done, u + 1)
                inverse_root(chain, rstd, std, mv[:, :, 1], tmp[:, :, 0])
                assert chain.n == LINKS
                dve.wait_ge(tr_done, DK * u)
                dve.wait_ge(h2_out, 16 * u)
                for t in range(UT):
                    dve.tensor_scalar(h2[:, t, :], xs[:, t, :], mv[:, t, 0:1], rstd[:, t:t + 1],
                                      ALU.subtract, ALU.mult).then_inc(norm_done, 1)

            def groups(t):
                return t.rearrange("p (t g) -> p t g", t=UT)

            def choose(u):
                dve.wait_ge(score_done, u + 1)
                dve.tensor_tensor(biased[:, :, :], score[:, :, :], bias_sb[:, :].unsqueeze(1).broadcast_to([P, UT, NE]), ALU.add)
                dve.drain()
                pairs = biased[:, :, :].rearrange("p t (g r) -> p (t g) r", r=EPG)
                dve.tensor_tensor(pair_hi[:, :, :], pairs[:, :, 0::2], pairs[:, :, 1::2], ALU.max)
                dve.tensor_tensor(pair_lo[:, :, :], pairs[:, :, 0::2], pairs[:, :, 1::2], ALU.min)
                dve.drain()
                best, second, third = (grp[:, i, :] for i in range(3))
                dve.tensor_tensor(best, pair_hi[:, :, 0], pair_hi[:, :, 1], ALU.max)
                dve.tensor_tensor(second, pair_hi[:, :, 0], pair_hi[:, :, 1], ALU.min)
                dve.tensor_tensor(third, pair_lo[:, :, 0], pair_lo[:, :, 1], ALU.max)
                dve.drain()
                dve.tensor_tensor(second, second, third, ALU.max)
                dve.drain()
                dve.tensor_tensor(best, best, second, ALU.add)
                dve.drain()
                other = groups(best).unsqueeze(2).broadcast_to([P, UT, NGR, NGR])
                own = groups(best).unsqueeze(3).broadcast_to([P, UT, NGR, NGR])
                four = lambda t: t[:, :, :].rearrange("p (t g) h -> p t g h", t=UT)
                dve.tensor_tensor(four(ahead), other, own, ALU.is_gt)
                dve.tensor_tensor(four(ties), other, own, ALU.is_equal)
                dve.drain()
                dve.tensor_tensor(four(ties), four(ties), earlier[:, :, :].unsqueeze(1).broadcast_to([P, UT, NGR, NGR]), ALU.mult)
                dve.drain()
                dve.tensor_tensor(ahead[:, :, :], ahead[:, :, :], ties[:, :, :], ALU.add)
                dve.drain()
                dve.tensor_reduce(grp[:, 2, :], ahead[:, :, :], axis=AX.X, op=ALU.add)
                dve.memset(masked[:, :, :], 0.0)
                dve.drain()
                dve.tensor_single_scalar(chosen[:, :], grp[:, 2, :], float(TOPG), op=ALU.is_lt)
                dve.drain()
                dve.copy_predicated(masked[:, :, :].rearrange("p t (g r) -> p (t g) r", r=EPG),
                                    chosen[:, :].unsqueeze(2).broadcast_to([P, UG, EPG]), pairs)
                dve.drain()
                for t in range(UT):
                    dve.max(top[:, t, :], masked[:, t, :])
                dve.drain()
                for t in range(UT):
                    dve.max_index(top_idx[:, t, :], top[:, t, :], masked[:, t, :])
                dve.drain()
                dve.tensor_copy(expert[:, :, :], top_idx[:, :, 0:TOPK])
                dve.drain()
                flat = lambda t: t[:, :, :, :].rearrange("p t k e -> p (t k) e")
                dve.tensor_tensor(flat(onehot), iota[:, :].unsqueeze(1).broadcast_to([P, UT * TOPK, NE]),
                                  expert[:, :, :].rearrange("p t k -> p (t k)").unsqueeze(2).broadcast_to([P, UT * TOPK, NE]),
                                  ALU.is_equal)
                dve.drain()
                with nc.allow_low_precision("0 or 1"):
                    dve.tensor_reduce(sel[:, :, :], onehot[:, :, :, :].rearrange("p t k e -> p t e k"), axis=AX.X, op=ALU.add).then_inc(sel_done, 1)
                dve.tensor_tensor(picked[:, :, :, :], onehot[:, :, :, :], score[:, :, :].unsqueeze(2).broadcast_to([P, UT, TOPK, NE]), ALU.mult)
                dve.drain()
                dve.tensor_reduce(weight[:, :, :], picked[:, :, :, :], axis=AX.X, op=ALU.add)
                dve.drain()
                dve.tensor_reduce(den[:, :], weight[:, :, :], axis=AX.X, op=ALU.add)
                dve.drain()
                dve.tensor_scalar_add(den[:, :], den[:, :], 1e-20)
                dve.drain()
                dve.reciprocal(den[:, :], den[:, :])
                dve.drain()
                dve.tensor_scalar_mul(den[:, :], den[:, :], ROUTE_SCALE)

            def give_slots(u, b, half):
                dve.wait_ge(scattered[half], 16 * UT * TOPK * b)
                dve.wait_ge(pos_done, u + 1)
                dve.tensor_tensor(picked[:, :, :, :], onehot[:, :, :, :],
                                  ps_pos[:, 0:UT * NE].rearrange("p (t e) -> p t e", t=UT).unsqueeze(2).broadcast_to([P, UT, TOPK, NE]), ALU.mult)
                pairs = info[half][:, :, :].rearrange("p (t k) c -> p t k c", t=UT)
                dve.tensor_tensor(pairs[:, :, :, 1], weight[:, :, :], den[:, :].unsqueeze(2).broadcast_to([P, UT, TOPK]), ALU.mult)
                dve.tensor_copy(pairs[:, :, :, 0], tok[:, :].unsqueeze(2).broadcast_to([P, UT, TOPK]))
                dve.tensor_reduce(sel_sum[:, :], sel[:, :, :].rearrange("p t e -> p e t"), axis=AX.X, op=ALU.add)
                dve.drain()
                dve.tensor_tensor(sel_acc[:, :], sel_acc[:, :], sel_sum[:, :], ALU.add)
                dve.tensor_reduce(place[:, :, :], picked[:, :, :, :], axis=AX.X, op=ALU.add)
                dve.tensor_scalar_add(tok[:, :], tok[:, :], float(UNIT))
                dve.drain()
                dve.tensor_scalar(over[:, :, :], place[:, :, :], float(CAP), float(SLOTS), ALU.is_ge, ALU.mult)
                dve.scalar_tensor_tensor(place[:, :, :], expert[:, :, :], float(CAP), place[:, :, :], op0=ALU.mult, op1=ALU.add)
                dve.drain()
                dve.tensor_tensor(slot[half][:, :].rearrange("p (t k) -> p t k", t=UT), place[:, :, :], over[:, :, :], ALU.add).then_inc(slot_done, 1)

            attend(0, 0)

            def body(b, half, more):
                u = b * HALVES + half
                for k in range(DK):
                    dve.wait_ge(hi_done, DK * u + k + 1)
                    dve.tensor_tensor(hT_lo[:, k, :], ps_t[k % 2][:, :], raw(hT_hi[:, k, :]), ALU.subtract).then_inc(lo_done.sem, 1)

                def low(n):
                    dve.wait_ge(ahi_done, UP * u + n + 1)
                    dve.tensor_tensor(a_lo[:, n, :], relu[n % 2][:, :], raw(a_hi[:, n, :]), ALU.subtract).then_inc(alo_done.sem, 1)

                for n in range(UP):
                    dve.wait_ge(relu_done, UP * u + n + 1)
                    dve.tensor_tensor(relu[n % 2][:, :], relu[n % 2][:, :], relu[n % 2][:, :], ALU.mult).then_inc(sq_done, 1)
                    if n:
                        low(n - 1)
                low(UP - 1)
                if more:
                    attend(*((b, 1) if half == 0 else (b + 1, 0)))
                choose(u)
                dve.wait_ge(gb_in, 16 * (b + 1))
                for t in range(UT):
                    down_done.wait(dve, UT * u + t + 1)
                    if t:
                        dve.wait_ge(out_done, UT * u + t)
                    dve.tensor_tensor(att[:, :], ps_m[t % RING][:, :], gb[:, :], ALU.mult).then_inc(fin_done.sem, 1)
                    fin_done.wait(dve, UT * u + t + 1)
                    dve.tensor_tensor(x_sb[half][:, t, :], x_sb[half][:, t, :], att[:, :], ALU.add).then_inc(out_done, 1)
                give_slots(u, b, half)

            steps(dve, body)

        @block.tensor
        def _(pe):
            up_done.open(pe)
            down_done.open(pe)
            THREE = ((0, 0), (0, 1), (1, 0))

            def exact(bank, pairs):
                for i, (a, c) in enumerate(pairs):
                    for j, (m, n) in enumerate(THREE):
                        last = pe.matmul(bank, a[m], c[n], start=i + j == 0, stop=i + 1 == len(pairs) and j == 2)
                return last

            def project(b, half, free):
                u = b * HALVES + half
                pe.wait_ge(o_in, 32 * (u + 1))
                for t in range(UT):
                    free(t)
                    cols = slice(t * P, (t + 1) * P)
                    exact(ps_m[t % RING][:, :], [((o_hi[:, g, cols], o_lo[:, g, cols]), (wo_hi[:, g, :], wo_lo[:, g, :]))
                                                 for g in range(NG)]).then_inc(proj_done, 1)

            pe.wait_ge(pool_own, 5)
            pe.wait_ge(w_lo_done, 1)
            project(0, 0, lambda t: None)
            pe.wait_ge(w_lo_done, NW)

            def body(b, half, more):
                u = b * HALVES + half
                pe.wait_ge(h_done, UT * (u + 1))
                for k in range(DK):
                    lo_done.wait(pe, DK * u + k - 1)
                    for t in range(UT):
                        last = pe.transpose(ps_t[k % 2][:, t * P:(t + 1) * P], h2[:, t, k * P:(k + 1) * P], ident[:, :])
                    last.then_inc(tr_done, 1)
                lo_done.wait(pe, DK * (u + 1))
                pe.wait_ge(score_done, u)
                for t in range(UT):
                    cols = slice(t * P, (t + 1) * P)
                    last = exact(ps_g[:, t * NE:(t + 1) * NE], [((hT_hi[:, k, cols], hT_lo[:, k, cols]), (gt_hi[:, k, :], gt_lo[:, k, :]))
                                                               for k in range(DK)])
                last.then_inc(gate_done, 1)
                for n in range(UP):
                    if n < RING:
                        fin_done.wait(pe, UT * (u - 1) + n + 1)
                    else:
                        pe.wait_ge(relu_done, UP * u + n - RING + 1)
                    cols = slice(n * P, (n + 1) * P)
                    exact(ps_m[n % RING][:, :], [((up_hi[:, k, cols], up_lo[:, k, cols]), (hT_hi[:, k, :], hT_lo[:, k, :]))
                                                 for k in range(DK)]).then_inc(up_done.sem, 1)
                if more:
                    project(*((b, 1) if half == 0 else (b + 1, 0)), lambda t: pe.wait_ge(relu_done, UP * u + UP - RING + t + 1))
                alo_done.wait(pe, UP * (u + 1))
                for t in range(UT):
                    if more:
                        pe.wait_ge(att_done, UT * (u + 1) + t + 1)
                    else:
                        pe.wait_ge(relu_done, UP * (u + 1))
                    cols = slice(t * P, (t + 1) * P)
                    exact(ps_m[t % RING][:, :], [((a_hi[:, n, cols], a_lo[:, n, cols]), (dn_hi[:, n, :], dn_lo[:, n, :]))
                                                 for n in range(UP)]).then_inc(down_done.sem, 1)
                pe.wait_ge(sel_done, u + 1)
                pe.wait_ge(slot_done, u)
                for t in range(UT):
                    bank = ps_pos[:, t * NE:(t + 1) * NE]
                    pe.matmul(bank, before[:, :], sel[:, t, :], start=True, stop=False)
                    for t2 in range(t):
                        pe.matmul(bank, ones[:, :], sel[:, t2, :], start=False, stop=False)
                    last = pe.matmul(bank, ones[:, :], sel_acc[:, :], start=False, stop=True)
                last.then_inc(pos_done, 1)

            steps(pe, body)


def stage_experts(nc, e_upT, e_downT, h2_dram, mod_dram, info_dram, out):
    J, HT = CAP // P, HID // P
    with ExitStack() as ctx:
        s = Scope(nc, ctx, "exp_")
        two = range(2)
        upr, dnr = ([s.sb(f"{n}{p}", sh, FP32) for p in two] for n, sh in (("upr", [P, DK, HID]), ("dnr", [P, HT, D])))
        up_hi, up_lo = ([s.sb(f"{n}{p}", [P, DK, HID], F32R) for p in two] for n in ("up_hi", "up_lo"))
        dn_hi, dn_lo = ([s.sb(f"{n}{p}", [P, HT, D], F32R) for p in two] for n in ("dn_hi", "dn_lo"))
        info = [s.sb(f"info{p}", [P, J, 2], FP32) for p in two]
        tok = [s.sb(f"tok{p}", [P, J], I32) for p in two]
        row = [s.sb(f"row{p}", [P, J], I32) for p in two]
        xg = [s.sb(f"xg{p}", [P, J, D], FP32) for p in two]
        gbg = [s.sb(f"gbg{p}", [P, J, D], FP32) for p in two]
        xT_hi, xT_lo = ([s.sb(f"{n}{p}", [P, DK, CAP], F32R) for p in two] for n in ("xT_hi", "xT_lo"))
        relu = s.sb("relu", [P, HT, CAP], FP32)
        a_hi, a_lo = s.sb("a_hi", [P, HT, CAP], F32R), s.sb("a_lo", [P, HT, CAP], F32R)
        y = [s.sb(f"y{p}", [P, J, D], FP32) for p in two]
        ident = s.sb("ident", [P, P], FP32)
        ps_t = [s.ps(f"ps_t{n}") for n in range(2)]
        ps_u = [s.ps(f"ps_u{n}") for n in range(HT)]
        ps_y = [s.ps(f"ps_y{n}") for n in range(2 * J)]

        w_in, info_in = s.sems("w_in", 2), s.sems("info_in", 2)
        pool_own, mark = s.sem("pool_own"), s.sem("mark")
        tok_done, row_done = s.sem("tok"), s.sem("row")
        x_in, added = s.sems("x_in", 2), s.sem("added")
        whi_done, wlo_done, dlo_done = s.sem("whi"), Credited(s.sem("wlo"), 2), Credited(s.sem("dlo"), 2)
        tr_done, xhi_done, xlo_done = s.sem("tr"), s.sem("xhi"), Credited(s.sem("xlo"), 2)
        up_done, relu_done, sq_done = Credited(s.sem("up"), 2), s.sem("relu"), s.sem("sq")
        ahi_done, alo_done = s.sem("ahi"), s.sem("alo")
        dn_done, y_done = Credited(s.sem("dn"), 2 * J), Credited(s.sem("y"), 2 * J)
        block = ctx.enter_context(nc.Block())

        def steps(eng, body):
            with eng.Fori(0, NE // 2) as i:
                for p in two:
                    body(i * 2 + p, p, i)

        @block.sync
        def _(sp):
            def body(e, p, i):
                wlo_done.wait(sp, e - 1)
                dlo_done.wait(sp, e - 1)
                sp.dma_start(upr[p][:, :, :], e_upT[bass.ds(e, 1), :, :].rearrange("o (k p) n -> p (o k) n", p=P)).then_inc(w_in[p], 16)
                sp.dma_start(dnr[p][:, :, :], e_downT[bass.ds(e, 1), :, :].rearrange("o (k p) n -> p (o k) n", p=P)).then_inc(w_in[p], 16)
                y_done.wait(sp, J * (e - 1))
                sp.dma_start(info[p][:, :, :], info_dram[bass.ds(e * CAP, CAP), :].rearrange("(j p) c -> p j c", p=P)).then_inc(info_in[p], 16)

            steps(sp, body)
            sp.wait_ge(added, 16 * J * NE)

        @block.gpsimd
        def _(pool):
            dlo_done.open(pool)
            make_identity(pool, ident, pool_own, 0)

            def body(e, p, i):
                hold(pool, row_done, e + 1, mark)
                xlo_done_wait = 2 * (e - 1)
                xlo_done.wait(pool, xlo_done_wait)
                pool.sem_inc(mark, 1)
                y_done.wait(pool, J * (e - 1))
                pool.sem_inc(mark, 1)
                for j in range(J):
                    pool.indirect_dma_start(xg[p][:, j, :], None, h2_dram[:, :],
                                            bass.IndirectOffsetOnAxis(tok[p][:, j:j + 1].bitcast(U32), 0)).then_inc(x_in[p], 16)
                    pool.indirect_dma_start(gbg[p][:, j, :], None, mod_dram.rearrange("b m d -> (b m) d"),
                                            bass.IndirectOffsetOnAxis(row[p][:, j:j + 1].bitcast(U32), 0)).then_inc(x_in[p], 16)
                dn_done.wait(pool, J * (e - 1))
                pool.sem_inc(mark, 1)
                pool.wait_ge(whi_done, 2 * (e + 1))
                pool.tensor_tensor(dn_lo[p][:, :, :], dnr[p][:, :, :], raw(dn_hi[p][:, :, :]), ALU.subtract).then_inc(dlo_done.sem, 1)

            def add(e, p):
                y_done.wait(pool, J * (e + 1))
                pool.sem_inc(mark, 1)
                hold(pool, added, 16 * J * e, mark)
                for j in range(J):
                    pool.indirect_dma_start(out[:, :], bass.IndirectOffsetOnAxis(tok[p][:, j:j + 1].bitcast(U32), 0),
                                            y[p][:, j, :], None, compute_op=ALU.add).then_inc(added, 16)

            body(0, 0, 0)
            with pool.Fori(0, NE // 2 - 1) as i:
                for p in two:
                    body(i * 2 + p + 1, 1 - p, i + p)
                    add(i * 2 + p, p)
            body(NE - 1, 1, NE // 2 - 1)
            add(NE - 2, 0)
            add(NE - 1, 1)

        @block.scalar
        def _(act):
            def weights(e, p, i):
                act.wait_ge(w_in[p], 32 * (i + 1))
                dn_done.wait(act, J * (e - 1))
                act.activation(up_hi[p][:, :, :], upr[p][:, :, :], ACT.Copy).then_inc(whi_done, 1)
                act.activation(dn_hi[p][:, :, :], dnr[p][:, :, :], ACT.Copy).then_inc(whi_done, 1)

            def body(e, p, i, more=True):
                if more:
                    weights(e + 1, 1 - p, i + p)
                for n in range(2):
                    act.wait_ge(tr_done, 2 * e + n + 1)
                    act.activation(xT_hi[p][:, 2 * n:2 * n + 2, :].rearrange("p k c -> p (k c)"), ps_t[n][:, :], ACT.Copy).then_inc(xhi_done, 1)
                for n in range(HT):
                    up_done.wait(act, HT * e + n + 1)
                    if n == 0:
                        act.wait_ge(alo_done, e)
                    act.activation(relu[:, n, :], ps_u[n][:, 0:CAP], ACT.Relu).then_inc(relu_done, 1)
                act.wait_ge(sq_done, e + 1)
                act.activation(a_hi[:, :, :], relu[:, :, :], ACT.Copy).then_inc(ahi_done, 1)

            weights(0, 0, 0)
            with act.Fori(0, NE // 2 - 1) as i:
                for p in two:
                    body(i * 2 + p, p, i)
            body(NE - 2, 0, NE // 2 - 1)
            body(NE - 1, 1, NE // 2 - 1, more=False)

        @block.vector
        def _(dve):
            for free in (wlo_done, xlo_done, y_done):
                free.open(dve)

            def tokens(e, p, i):
                dve.wait_ge(info_in[p], 16 * (i + 1))
                dve.wait_ge(added, 16 * J * (e - 1)) if not isinstance(e, int) or e > 0 else None
                dve.tensor_copy(tok[p][:, :], info[p][:, :, 0]).then_inc(tok_done, 1)
                dve.wait_ge(tok_done, e + 1)
                dve.tensor_single_scalar(row[p][:, :], tok[p][:, :], S.bit_length() - 1, op=ALU.logical_shift_right)
                dve.drain()
                dve.tensor_scalar(row[p][:, :], row[p][:, :], 6.0, float(M_GB), ALU.mult, ALU.add).then_inc(row_done, 1)
                dve.wait_ge(whi_done, 2 * e + 1)
                dve.tensor_tensor(up_lo[p][:, :, :], upr[p][:, :, :], raw(up_hi[p][:, :, :]), ALU.subtract).then_inc(wlo_done.sem, 1)

            def body(e, p, i, more=True):
                if more:
                    tokens(e + 1, 1 - p, i + p)
                for n in range(2):
                    dve.wait_ge(xhi_done, 2 * e + n + 1)
                    dve.tensor_tensor(xT_lo[p][:, 2 * n:2 * n + 2, :].rearrange("p k c -> p (k c)"), ps_t[n][:, :],
                                      raw(xT_hi[p][:, 2 * n:2 * n + 2, :]).rearrange("p k c -> p (k c)"), ALU.subtract).then_inc(xlo_done.sem, 1)
                dve.wait_ge(relu_done, HT * (e + 1))
                dve.tensor_tensor(relu[:, :, :], relu[:, :, :], relu[:, :, :], ALU.mult).then_inc(sq_done, 1)
                dve.wait_ge(ahi_done, e + 1)
                dve.tensor_tensor(a_lo[:, :, :], relu[:, :, :], raw(a_hi[:, :, :]), ALU.subtract).then_inc(alo_done, 1)
                dve.wait_ge(x_in[p], 64 * (i + 1))
                for j in range(J):
                    dn_done.wait(dve, J * e + j + 1)
                    dve.scalar_tensor_tensor(y[p][:, j, :], ps_y[p * J + j][:, :], info[p][:, j, 1:2], gbg[p][:, j, :],
                                             op0=ALU.mult, op1=ALU.mult).then_inc(y_done.sem, 1)

            tokens(0, 0, 0)
            with dve.Fori(0, NE // 2 - 1) as i:
                for p in two:
                    body(i * 2 + p, p, i)
            body(NE - 2, 0, NE // 2 - 1)
            body(NE - 1, 1, NE // 2 - 1, more=False)

        @block.tensor
        def _(pe):
            up_done.open(pe)
            dn_done.open(pe)
            THREE = ((0, 0), (0, 1), (1, 0))
            pe.wait_ge(pool_own, 2)

            def body(e, p, i):
                pe.wait_ge(x_in[p], 64 * (i + 1))
                for n in range(2):
                    xlo_done.wait(pe, 2 * (e - 1) + n + 1)
                    for k in (2 * n, 2 * n + 1):
                        for j in range(J):
                            col = (k % 2) * CAP + j * P
                            last = pe.transpose(ps_t[n][:, col:col + P], xg[p][:, j, k * P:(k + 1) * P], ident[:, :])
                    last.then_inc(tr_done, 1)
                xlo_done.wait(pe, 2 * (e + 1))
                wlo_done.wait(pe, e + 1)
                pe.wait_ge(relu_done, HT * e)
                for n in range(HT):
                    for k in range(DK):
                        for a, c in THREE:
                            last = pe.matmul(ps_u[n][:, 0:CAP], (up_hi, up_lo)[a][p][:, k, n * P:(n + 1) * P],
                                             (xT_hi, xT_lo)[c][p][:, k, :], start=k + a + c == 0, stop=k == DK - 1 and a == 1)
                    last.then_inc(up_done.sem, 1)
                pe.wait_ge(alo_done, e + 1)
                dlo_done.wait(pe, e + 1)
                y_done.wait(pe, J * (e - 1))
                for j in range(J):
                    for n in range(HT):
                        for a, c in THREE:
                            last = pe.matmul(ps_y[p * J + j][:, :], (a_hi, a_lo)[a][:, n, j * P:(j + 1) * P],
                                             (dn_hi, dn_lo)[c][p][:, n, :], start=n + a + c == 0, stop=n == HT - 1 and a == 1)
                    last.then_inc(dn_done.sem, 1)

            steps(pe, body)


def build(nc, x, cT, wmod, wqkvT, bqk, bv, woT, bo, gateT, bias, sh_upT, sh_downT, e_upT, e_downT, out):
    mod_dram = nc.dram_tensor("mod_rows", [NB + 1, 6, D], FP32, kind="Internal").ap()
    qk_dram = nc.dram_tensor("qk_parts", [4, NB * NG, P, S], FP32, kind="Internal").ap()
    v_dram = nc.dram_tensor("v_rows", [NB * NG, S, P], FP32, kind="Internal").ap()
    o_dram = nc.dram_tensor("o_parts", [2, NB * NG, P, S], FP32, kind="Internal").ap()
    h2_dram = nc.dram_tensor("h2_rows", [T + CAP, D], FP32, kind="Internal").ap()
    info_dram = nc.dram_tensor("slot_info", [SLOTS, 2], FP32, kind="Internal").ap()
    stage_modulation(nc, cT, wmod, mod_dram, h2_dram, info_dram, out)
    stage_qkv(nc, x, wqkvT, bqk, bv, mod_dram, qk_dram, v_dram)
    stage_attention(nc, qk_dram, v_dram, o_dram)
    stage_project_route_shared(nc, x, o_dram, mod_dram, woT, bo, gateT, bias, sh_upT, sh_downT, h2_dram, info_dram, out)
    stage_experts(nc, e_upT, e_downT, h2_dram, mod_dram, info_dram, out)


def kernel(L0_attn_x, L0_attn_w_q, L0_attn_b_q, L0_attn_w_k, L0_attn_b_k, L0_attn_w_v, L0_attn_b_v, L0_attn_w_o,
           L0_attn_b_o, L0_ffn_gate_w, L0_ffn_bias_corr, L0_ffn_up_w, L0_ffn_down_w, L0_ffn_shared_up_w,
           L0_ffn_shared_down_w, L0_c, L0_wmod):
    import concourse.bacc as bacc
    from concourse.bass_utils import run_bass_kernel_spmd

    a = np.asarray
    arrays = {
        "x": a(L0_attn_x),
        "cT": a(L0_c).T,
        "wmod": a(L0_wmod),
        "wqkvT": np.stack([a(w).T for w in (L0_attn_w_q, L0_attn_w_k, L0_attn_w_v)]),
        "bqk": np.concatenate([a(b).reshape(NG, P).T for b in (L0_attn_b_q, L0_attn_b_k)], axis=1),
        "bv": a(L0_attn_b_v).reshape(1, D),
        "woT": a(L0_attn_w_o).T,
        "bo": a(L0_attn_b_o).reshape(1, D),
        "gateT": a(L0_ffn_gate_w).T,
        "bias": a(L0_ffn_bias_corr).reshape(1, NE),
        "sh_upT": a(L0_ffn_shared_up_w).T,
        "sh_downT": a(L0_ffn_shared_down_w).T,
        "e_upT": a(L0_ffn_up_w).transpose(0, 2, 1),
        "e_downT": a(L0_ffn_down_w).transpose(0, 2, 1),
    }
    arrays = {n: np.ascontiguousarray(v) for n, v in arrays.items()}
    nc = bacc.Bacc("TRN2", target_bir_lowering=False, num_devices=1)
    args = [nc.dram_tensor(n, v.shape, mybir.dt.from_np(v.dtype), kind="ExternalInput").ap() for n, v in arrays.items()]
    out = nc.dram_tensor("out", (T + CAP, D), FP32, kind="ExternalOutput").ap()
    build(nc, *args, out)
    r = run_bass_kernel_spmd(nc, [arrays], core_ids=[0])
    return r.results[0]["out"][:T].reshape(NB, S, D)
```

```python
import numpy as np
import concourse.bass as bass
from concourse import mybir
from contextlib import ExitStack

FP32 = mybir.dt.float32
F32R = mybir.dt.float32r
BF16 = mybir.dt.bfloat16
I32 = mybir.dt.int32
U32 = mybir.dt.uint32
ALU = mybir.AluOpType
ACT = mybir.ActivationFunctionType
AX = mybir.AxisListType

P = 128
NB, S, D = 8, 1024, 512
T = NB * S
DK = D // P
HD = 32
NG = D // P
GH = P // HD
UNIT = 512
UT = UNIT // P
HALVES = S // UNIT
NE, NGR, EPG = 32, 8, 4
TOPG, TOPK = 4, 4
HID, HS, CAP = 256, 1024, 256
ROUTE_SCALE = 2.5
EPS = 1e-5
MASKED = -1.0e30
QHI, QLO, KHI, KLO = range(4)
SLOTS = NE * CAP
M_SA, M_CA, M_GA, M_SB, M_CB, M_GB = range(6)


def raw(ap):
    return ap.bitcast(FP32)


class Chain:

    def __init__(self, eng, sem, base):
        self.eng, self.sem, self.base, self.n = eng, sem, base, 0

    def done(self, ins):
        self.n += 1
        ins.then_inc(self.sem.sem, 1)

    def wait(self):
        self.sem.wait(self.eng, self.base + self.n)


class Sem:

    def __init__(self, sem, credit):
        self.sem, self.credit = sem, credit

    def wait(self, eng, value):
        low = value if isinstance(value, int) else value.min_val
        if isinstance(value, int) and value <= 0:
            return
        assert isinstance(value, int) or low + self.credit > 0, (self.sem, low)
        eng.wait_ge(self.sem, value + self.credit)


def hold(eng, sem, value, mark):
    sem.wait(eng, value)
    eng.sem_inc(mark.sem, 1)


class Scope:

    def __init__(self, nc, ctx, prefix, credit=16):
        self.nc, self.ctx, self.prefix, self.credit, self.all = nc, ctx, prefix, credit, []

    def sb(self, name, shape, dt):
        return self.ctx.enter_context(self.nc.sbuf_tensor(self.prefix + name, shape, dt))

    def ps(self, name, shape=(P, 512), dt=FP32):
        return self.ctx.enter_context(self.nc.psum_tensor(self.prefix + name, list(shape), dt))

    def sem(self, name, credit=None):
        sem = Sem(self.ctx.enter_context(self.nc.semaphore(self.prefix + name)),
                  self.credit if credit is None else credit)
        self.all.append(sem)
        return sem

    def sems(self, name, n, credit=None):
        return [self.sem(f"{name}{i}", credit) for i in range(n)]

    def give_credit(self, eng):
        for sem in self.all:
            if sem.credit:
                eng.sem_inc(sem.sem, sem.credit)


STAT_LINKS, ROOT_LINKS = 2, 5


def combine_stats(chain, stats, mv, tmp):
    dve = chain.eng
    total, diff, m2 = tmp[:, :, 0], tmp[:, :, 1], tmp[:, :, 2]
    dve.tensor_tensor(total, stats[:, :, 1], stats[:, :, 4], ALU.add)
    dve.tensor_tensor(diff, stats[:, :, 1], stats[:, :, 4], ALU.subtract)
    chain.done(dve.tensor_tensor(m2, stats[:, :, 2], stats[:, :, 5], ALU.add))
    chain.wait()
    dve.tensor_scalar_mul(mv[:, :, 0], total, 0.5)
    dve.tensor_scalar(m2, m2, 1.0 / D, EPS, ALU.mult, ALU.add)
    chain.done(dve.scalar_tensor_tensor(diff, diff, 0.25, diff, op0=ALU.mult, op1=ALU.mult))
    chain.wait()
    return dve.tensor_tensor(mv[:, :, 1], m2, diff, ALU.add)


def inverse_root(chain, rstd, std, var, y):
    dve = chain.eng
    r = rstd[:, :]
    for op in (lambda: dve.reciprocal(r, std[:, :]),
               lambda: dve.tensor_tensor(y, r, r, ALU.mult),
               lambda: dve.tensor_tensor(y, y, var, ALU.mult),
               lambda: dve.tensor_scalar(y, y, -0.5, 1.5, ALU.mult, ALU.add),
               lambda: dve.tensor_tensor(r, r, y, ALU.mult)):
        chain.done(op())
        chain.wait()


def stage_modulation(nc, cT, wmod, mod_dram, h2_dram, info_dram, out):
    with ExitStack() as ctx:
        s = Scope(nc, ctx, "mod_", credit=0)
        c_sb = s.sb("c", [P, DK, NB], FP32)
        sig = s.sb("sig", [P, DK, NB], FP32)
        silu = s.sb("silu", [P, DK, NB], FP32)
        w_sb = s.sb("w", [P, DK, 6 * D], FP32)
        res = s.sb("res", [NB, 6, D], FP32)
        sign = s.sb("sign", [NB, 2, D], FP32)
        mag = s.sb("mag", [NB, 2, D], FP32)
        ps = [s.ps(f"ps{j}", (NB, D)) for j in range(6)]
        SP_TILES = SLOTS // P
        zero = s.sb("zero", [P, D], FP32)
        pad_i = s.sb("pad_i", [P, SP_TILES], I32)
        info = s.sb("info", [P, SP_TILES, 2], FP32)
        pool_own, info_done = s.sem("pool_own"), s.sem("info")
        loaded, sig_done, silu_done = s.sem("loaded"), s.sem("sig"), s.sem("silu")
        mm, own, ready, stored = s.sem("mm"), s.sem("own"), s.sem("ready"), s.sem("stored")
        gates = (M_GA, M_GB)
        block = ctx.enter_context(nc.Block())

        @block.sync
        def _(sp):
            sp.dma_start(c_sb[:, :, :], cT.rearrange("(k p) b -> p k b", p=P)).then_inc(loaded.sem, 16)
            sp.dma_start(w_sb[:, :, :], wmod.rearrange("(k p) n -> p k n", p=P)).then_inc(loaded.sem, 16)
            info_done.wait(sp, 1)
            for r in range(CAP // P):
                sp.dma_start(h2_dram[T + r * P:T + (r + 1) * P, :], zero[:, :]).then_inc(stored.sem, 16)
                sp.dma_start(out[T + r * P:T + (r + 1) * P, :], zero[:, :]).then_inc(stored.sem, 16)
            sp.dma_start(info_dram.rearrange("(n p) c -> p n c", p=P), info[:, :, :]).then_inc(stored.sem, 16)
            sp.dma_start(mod_dram[NB:NB + 1, :, :].rearrange("b j d -> (b j) d"), zero[0:6, :]).then_inc(stored.sem, 16)
            ready.wait(sp, 1)
            sp.dma_start(mod_dram[0:NB, :, :], res[:, :, :]).then_inc(stored.sem, 16)
            stored.wait(sp, 16 * (2 * CAP // P + 3))

        @block.gpsimd
        def _(pool):
            pool.memset(zero[:, :], 0.0)
            pool.memset(info[:, :, :], 0.0)
            pool.iota(pad_i[:, :], pattern=[[0, NE], [P, CAP // P]], base=T, channel_multiplier=1).then_inc(pool_own.sem, 1)
            pool_own.wait(pool, 1)
            pool.tensor_copy(info[:, :, 0], pad_i[:, :]).then_inc(info_done.sem, 1)

        @block.scalar
        def _(act):
            loaded.wait(act, 32)
            act.activation(sig[:, :, :], c_sb[:, :, :], ACT.Sigmoid).then_inc(sig_done.sem, 1)

        @block.tensor
        def _(pe):
            silu_done.wait(pe, 1)
            for j in range(6):
                for k in range(DK):
                    last = pe.matmul(ps[j][:, :], silu[:, k, :], w_sb[:, k, j * D:(j + 1) * D],
                                     start=k == 0, stop=k == DK - 1)
                last.then_inc(mm.sem, 1)

        @block.vector
        def _(dve):
            chain = Chain(dve, own, 0)
            sig_done.wait(dve, 1)
            dve.tensor_tensor(silu[:, :, :], c_sb[:, :, :], sig[:, :, :], ALU.mult).then_inc(silu_done.sem, 1)
            for j in range(6):
                mm.wait(dve, j + 1)
                if j in (M_CA, M_CB):
                    last = dve.tensor_scalar_add(res[:, j, :], ps[j][:, :], 1.0)
                else:
                    last = dve.tensor_copy(res[:, j, :], ps[j][:, :])
            chain.done(last)
            chain.wait()
            for n, j in enumerate(gates):
                dve.tensor_scalar(sign[:, n, :], res[:, j, :], 0.0, 2.0, ALU.is_ge, ALU.mult)
                last = dve.tensor_scalar(mag[:, n, :], res[:, j, :], -1.0, 0.25, ALU.mult, ALU.max)
            chain.done(last)
            chain.wait()
            for n, j in enumerate(gates):
                last = dve.tensor_tensor(mag[:, n, :], mag[:, n, :], res[:, j, :], ALU.max)
            chain.done(last)
            chain.wait()
            for n, j in enumerate(gates):
                last = dve.scalar_tensor_tensor(res[:, j, :], sign[:, n, :], -1.0, mag[:, n, :],
                                                op0=ALU.add, op1=ALU.mult)
            last.then_inc(ready.sem, 1)


def make_identity(pool, tile, own, n):
    pool.memset(tile[:, :], 0.0).then_inc(own.sem, 1)
    own.wait(pool, n + 1)
    pool.affine_select(out=tile[:, :], in_=tile[:, :], compare_op=ALU.not_equal, fill=1.0, base=0,
                       pattern=[[-1, tile.shape[1]]], channel_multiplier=1).then_inc(own.sem, 1)
    return n + 2


def stage_qkv(nc, x, wqkvT, bqk, bv, mod_dram, qk_dram, v_dram):
    with ExitStack() as ctx:
        s = Scope(nc, ctx, "qkv_")
        x_sb = [s.sb(f"x{p}", [P, UT, D], FP32) for p in range(2)]
        wraw = s.sb("wraw", [P, DK, D], FP32)
        w_hi = [s.sb(f"w_hi{j}", [P, DK, D], F32R) for j in range(3)]
        w_lo = [s.sb(f"w_lo{j}", [P, DK, D], F32R) for j in range(3)]
        hT_hi = [s.sb(f"hT_hi{p}", [P, DK, UNIT], F32R) for p in range(2)]
        hT_lo = [s.sb(f"hT_lo{p}", [P, DK, UNIT], F32R) for p in range(2)]
        mod = s.sb("mod", [P, 2, D], FP32)
        bqk_sb = s.sb("bqk", [P, 2 * NG], FP32)
        bv_sb = s.sb("bv", [P, D], FP32)
        ident = s.sb("ident", [P, P], FP32)
        stats = s.sb("stats", [P, UT, 6], FP32)
        mv = s.sb("mv", [P, UT, 2], FP32)
        std = s.sb("std", [P, UT], FP32)
        rstd = s.sb("rstd", [P, UT], FP32)
        tmp = s.sb("tmp", [P, UT, 3], FP32)
        RING, BANKS = 4, 6
        out_hi = [s.sb(f"out_hi{n}", [P, UNIT], F32R) for n in range(RING)]
        out_lo = [s.sb(f"out_lo{n}", [P, UNIT], F32R) for n in range(RING)]
        out_v = [s.sb(f"out_v{n}", [P, D], FP32) for n in range(UT)]
        ps_t = [s.ps(f"ps_t{n}") for n in range(2)]
        ps_m = [s.ps(f"ps_m{n}") for n in range(BANKS)]

        w_loaded, w_hi_done, w_lo_done = s.sem("w_loaded"), s.sem("w_hi_done"), s.sem("w_lo_done")
        consts, pool_own, dve_own = s.sem("consts"), s.sem("pool_own"), s.sem("dve_own")
        x_in, mod_in = s.sems("x_in", 2), s.sem("mod_in")
        var_done, std_done, norm_done, h_done = s.sem("var"), s.sem("std"), s.sem("norm"), s.sem("h")
        mul_done = s.sem("mul")
        tr_done, hi_done, lo_done = s.sem("tr"), s.sem("hi"), s.sem("lo")
        mm_done, ehi_done, elo_done, ev_done = s.sem("mm"), s.sem("ehi"), s.sem("elo"), s.sem("ev")
        qk_out, v_out = s.sems("qk_out", RING), s.sems("v_out", UT)
        NQK = 2 * NG
        NM = NQK + UT
        block = ctx.enter_context(nc.Block())
        LAST = NB - 1

        def steps(eng, body):
            with eng.Fori(0, LAST) as b:
                for half in range(HALVES):
                    body(b, half, True)
            for half in range(HALVES):
                body(LAST, half, half + 1 < HALVES)

        @block.sync
        def _(sp):
            s.give_credit(sp)
            def load_x(b, half):
                src = x[bass.ds(b, 1), half * UNIT:(half + 1) * UNIT, :]
                sp.dma_start(x_sb[half][:, :, :], src.rearrange("o (t p) d -> p (o t) d", p=P)).then_inc(x_in[half].sem, 16)

            def load_mod(b):
                for m, j in enumerate((M_SA, M_CA)):
                    sp.dma_start(mod[:, m, :], mod_dram[bass.ds(b, 1), j, :].broadcast_to([P, D])).then_inc(mod_in.sem, 16)

            load_x(0, 0)
            load_mod(0)
            for j in range(3):
                if j:
                    w_lo_done.wait(sp, j)
                sp.dma_start(wraw[:, :, :], wqkvT[j].rearrange("(k p) n -> p k n", p=P)).then_inc(w_loaded.sem, 16)
            sp.dma_start(bqk_sb[:, :], bqk[:, :]).then_inc(consts.sem, 16)
            sp.dma_start(bv_sb[:, :], bv[:, :].broadcast_to([P, D])).then_inc(consts.sem, 16)
            load_x(0, 1)

            def body(b, half, more):
                u = b * HALVES + half
                if more or half == 0:
                    if not isinstance(b, int) or b < LAST:
                        tr_done.wait(sp, DK * (u + 1))
                        load_x(b + 1, half)
                        if half == 0:
                            h_done.wait(sp, UT * (u + 2))
                            load_mod(b + 1)
                for n in range(NQK):
                    elo_done.wait(sp, NQK * u + n + 1)
                    which, g = (QHI, n) if n < NG else (KHI, n - NG)
                    for part, tile in ((0, out_hi), (1, out_lo)):
                        dst = qk_dram[which + part, bass.ds(b * NG + g, 1), :, half * UNIT:(half + 1) * UNIT]
                        sp.dma_start(dst.rearrange("o p t -> (o p) t"), raw(tile[n % RING][:, :])).then_inc(qk_out[n % RING].sem, 16)
                for t in range(UT):
                    ev_done.wait(sp, UT * u + t + 1)
                    tok = half * UNIT + t * P
                    dst = v_dram[bass.ds(b * NG, NG), tok:tok + P, :]
                    sp.dma_start(dst.rearrange("g t j -> t g j"),
                                 out_v[t][:, :].rearrange("p (g j) -> p g j", g=NG)).then_inc(v_out[t].sem, 16)

            steps(sp, body)
            units = NB * HALVES
            for n in range(RING):
                qk_out[n].wait(sp, 32 * (NQK // RING) * units)
            for t in range(UT):
                v_out[t].wait(sp, 16 * units)

        @block.gpsimd
        def _(pool):
            make_identity(pool, ident, pool_own, 0)

            def modulate(u, half, b):
                mod_in.wait(pool, 32 * (b + 1))
                for t in range(UT):
                    norm_done.wait(pool, UT * u + t + 1)
                    xt = x_sb[half][:, t, :]
                    pool.tensor_tensor(xt, xt, mod[:, 1, :], ALU.mult).then_inc(mul_done.sem, 1)
                    mul_done.wait(pool, UT * u + t + 1)
                    pool.tensor_tensor(xt, xt, mod[:, 0, :], ALU.add).then_inc(h_done.sem, 1)

            modulate(0, 0, 0)

            def body(b, half, more):
                if more:
                    u = b * HALVES + half
                    modulate(u + 1, 1 - half, b + half)

            steps(pool, body)

        @block.scalar
        def _(act):
            for j in range(3):
                w_loaded.wait(act, 16 * (j + 1))
                act.activation(w_hi[j][:, :, :], wraw[:, :, :], ACT.Copy).then_inc(w_hi_done.sem, 1)
            consts.wait(act, 32)

            def root(u):
                var_done.wait(act, u + 1)
                act.activation(std[:, :], mv[:, :, 1], ACT.Sqrt).then_inc(std_done.sem, 1)

            root(0)

            def body(b, half, more):
                u = b * HALVES + half
                mm_done.wait(act, NM * (u - 1))
                for k in range(DK):
                    tr_done.wait(act, DK * u + k + 1)
                    act.activation(hT_hi[half][:, k, :], ps_t[k % 2][:, :], ACT.Copy).then_inc(hi_done.sem, 1)
                if more:
                    root(u + 1)
                for n in range(NQK):
                    mm_done.wait(act, NM * u + n + 1)
                    use = (NQK // RING) * u + n // RING
                    qk_out[n % RING].wait(act, 32 * use)
                    act.activation(out_hi[n % RING][:, :], ps_m[n % BANKS][:, :], ACT.Identity,
                                   bias=bqk_sb[:, n:n + 1]).then_inc(ehi_done.sem, 1)

            steps(act, body)

        @block.vector
        def _(dve):
            for j in range(3):
                w_hi_done.wait(dve, j + 1)
                dve.tensor_tensor(w_lo[j][:, :, :], wraw[:, :, :], raw(w_hi[j][:, :, :]), ALU.subtract).then_inc(w_lo_done.sem, 1)
            consts.wait(dve, 32)
            LINKS = 1 + STAT_LINKS + ROOT_LINKS

            def layernorm(u, half, b):
                chain = Chain(dve, dve_own, LINKS * u)
                x_in[half].wait(dve, 16 * (b + 1))
                for t in range(UT):
                    last = dve.bn_stats(stats[:, t, :], x_sb[half][:, t, :])
                chain.done(last)
                chain.wait()
                combine_stats(chain, stats, mv, tmp).then_inc(var_done.sem, 1)
                std_done.wait(dve, u + 1)
                var_done.wait(dve, u + 1)
                inverse_root(chain, rstd, std, mv[:, :, 1], tmp[:, :, 0])
                assert chain.n == LINKS
                for t in range(UT):
                    dve.tensor_scalar(x_sb[half][:, t, :], x_sb[half][:, t, :], mv[:, t, 0:1], rstd[:, t:t + 1],
                                      ALU.subtract, ALU.mult).then_inc(norm_done.sem, 1)

            layernorm(0, 0, 0)

            def body(b, half, more):
                u = b * HALVES + half
                for k in range(DK):
                    hi_done.wait(dve, DK * u + k + 1)
                    dve.tensor_tensor(hT_lo[half][:, k, :], ps_t[k % 2][:, :], raw(hT_hi[half][:, k, :]),
                                      ALU.subtract).then_inc(lo_done.sem, 1)
                if more:
                    layernorm(u + 1, 1 - half, b + half)
                for n in range(NQK):
                    ehi_done.wait(dve, NQK * u + n + 1)
                    dve.scalar_tensor_tensor(out_lo[n % RING][:, :], ps_m[n % BANKS][:, :], bqk_sb[:, n:n + 1],
                                             raw(out_hi[n % RING][:, :]), op0=ALU.add, op1=ALU.subtract).then_inc(elo_done.sem, 1)
                for t in range(UT):
                    mm_done.wait(dve, NM * u + NQK + t + 1)
                    v_out[t].wait(dve, 16 * u)
                    dve.tensor_tensor(out_v[t][:, :], ps_m[(NQK + t) % BANKS][:, :], bv_sb[:, :], ALU.add).then_inc(ev_done.sem, 1)

            steps(dve, body)

        @block.tensor
        def _(pe):
            pool_own.wait(pe, 2)

            def body(b, half, more):
                u = b * HALVES + half
                h_done.wait(pe, UT * (u + 1))
                for k in range(DK):
                    lo_done.wait(pe, DK * u + k - 1)
                    for t in range(UT):
                        last = pe.transpose(ps_t[k % 2][:, t * P:(t + 1) * P], x_sb[half][:, t, k * P:(k + 1) * P], ident[:, :])
                    last.then_inc(tr_done.sem, 1)
                w_lo_done.wait(pe, 3)
                lo_done.wait(pe, DK * (u + 1))
                for n in range(NM):
                    if n < BANKS:
                        if n < BANKS - UT:
                            elo_done.wait(pe, NQK * u - (BANKS - UT) + n + 1)
                        else:
                            ev_done.wait(pe, UT * u - UT + (n - (BANKS - UT)) + 1)
                    else:
                        elo_done.wait(pe, NQK * u + n - BANKS + 1)
                    for k in range(DK):
                        for a, c in ((0, 0), (0, 1), (1, 0)):
                            h_part = (hT_hi, hT_lo)[a][half]
                            if n < NQK:
                                w_part = (w_hi, w_lo)[c][n // NG]
                                last = pe.matmul(ps_m[n % BANKS][:, :], w_part[:, k, (n % NG) * P:(n % NG + 1) * P],
                                                 h_part[:, k, :], start=k == 0 and a + c == 0, stop=k == DK - 1 and a == 1)
                            else:
                                t = n - NQK
                                last = pe.matmul(ps_m[n % BANKS][:, :], h_part[:, k, t * P:(t + 1) * P],
                                                 (w_hi, w_lo)[c][2][:, k, :], start=k == 0 and a + c == 0, stop=k == DK - 1 and a == 1)
                    last.then_inc(mm_done.sem, 1)

            steps(pe, body)


def stage_attention(nc, qk_dram, v_dram, o_dram):
    STACK = 3 * HD
    ROWS = STACK + 2
    KT = S // P
    QH = S // UNIT
    GROUPS = NB * NG
    SLOT = 3
    NPT = 2 * GH
    with ExitStack() as ctx:
        s = Scope(nc, ctx, "att_")
        qs = [s.sb(f"qs{i}", [ROWS, GH, S], F32R) for i in range(SLOT)]
        ks = [s.sb(f"ks{i}", [ROWS, GH, S], F32R) for i in range(SLOT)]
        vs = [s.sb(f"vs{i}", [P, KT, P], FP32) for i in range(SLOT)]
        pt = [s.sb(f"pt{i}", [P, UNIT], FP32) for i in range(NPT)]
        total_sb = [s.sb(f"total{i}", [P, UNIT], FP32) for i in range(QH)]
        rec = [s.sb(f"rec{i}", [P, UNIT], FP32) for i in range(QH)]
        o32 = [s.sb(f"o32_{i}", [P, UNIT], FP32) for i in range(QH)]
        oT_hi = [s.sb(f"oT_hi{i}", [P, UNIT], F32R) for i in range(QH)]
        oT_lo = [s.sb(f"oT_lo{i}", [P, UNIT], F32R) for i in range(QH)]
        rowmax = s.sb("rowmax", [P, GH * KT], FP32)
        m_hi = s.sb("m_hi", [GH * KT, P], F32R)
        m_lo = s.sb("m_lo", [GH * KT, P], F32R)
        ones = s.sb("ones", [P, HD], FP32)
        ident = s.sb("ident", [P, P], FP32)
        ident16 = s.sb("ident16", [P, P], BF16)
        mask_q = s.sb("mask_q", [P, P], BF16)
        mask_k = s.sb("mask_k", [P, P], BF16)
        ps_s = [s.ps(f"ps_s{i}", (P, 2 * 512)) for i in range(2)]
        ps_p = [s.ps(f"ps_p{i}") for i in range(2)]
        ps_o, ps_sum = s.ps("ps_o"), s.ps("ps_sum")

        q_in, v_in, m_in = s.sems("q_in", SLOT), s.sems("v_in", SLOT), s.sems("m_in", SLOT)
        pool_own, consts, ln_done, rec_done, mark = (s.sem(n) for n in ("pool_own", "consts", "ln", "rec", "mark"))
        s_done, max_done = s.sem("s"), s.sem("max")
        mt_done, mhi_done, mlo_done = s.sem("mt"), s.sem("mhi"), s.sem("mlo")
        p_done, exp_done, pv_done = s.sem("p"), s.sem("exp"), s.sem("pv")
        o_free, ohi_done, olo_done = s.sem("o_free"), s.sem("ohi"), s.sem("olo")
        own_sem, t_free = s.sem("pool_links"), s.sem("t_free")
        o_out = s.sems("o_out", QH)
        block = ctx.enter_context(nc.Block())

        order1 = [(h, t) for a in range(KT // 2) for h in range(GH) for t in (KT - 1 - a, a)]
        HT = UNIT // P
        chunks = [(qh, kt) for qh in range(QH) for kt in
                  [0] + list(range(qh * HT + 1, (qh + 1) * HT)) + ([qh * HT] if qh else []) + list(range(1, qh * HT))]
        ENDS = [c for c in range(len(chunks)) if c + 1 == len(chunks) or chunks[c + 1][0] != chunks[c][0]]
        N1, NC = len(order1), len(chunks)
        NP = NC * GH
        TILES = [2, 3, 4, 4, 2, 3, 4, 4, 3, 3, 0, 0]
        TURN = NC - 2
        assert sorted(chunks) == [(qh, kt) for qh in range(QH) for kt in range((qh + 1) * HT)]
        assert sum(TILES) == N1 and not any(TILES[TURN:]) and len(TILES) == NC
        share = [sum(TILES[:c]) + -(-TILES[c] * h // GH) for c in range(NC) for h in range(GH)] + [N1]

        def after(c, h):
            return share[c * GH + h], share[c * GH + h + 1]

        class Group:
            def __init__(self, g, slot, use):
                self.g, self.slot, self.use = g, slot, use

            def ahead(self, n):
                slot = self.slot + n
                return Group(self.g + n, slot % SLOT, self.use + slot // SLOT)

        def steps(step):
            LOOPS = (GROUPS - 3) // SLOT - 1

            def run(eng):
                first = Group(0, 0, 0)
                step(first, None)
                step(first.ahead(1), first)
                with eng.Fori(0, LOOPS) as i:
                    for j in range(SLOT):
                        prev = Group(i * SLOT, 0, i).ahead(j + 1)
                        step(prev.ahead(1), prev)
                for g in range(LOOPS * SLOT + 1, GROUPS):
                    prev = first.ahead(g)
                    step(prev.ahead(1) if g + 1 < GROUPS else None, prev)
            return run

        def older(prev):
            if isinstance(prev.g, int) and prev.g == 0:
                return None
            return Group(prev.g - 1, (prev.slot - 1) % SLOT, None)

        @block.sync
        def _(sp):
            s.give_credit(sp)
            def load(G):
                for tile, parts in ((qs, (QHI, QHI, QLO)), (ks, (KHI, KLO, KHI))):
                    for r, part in enumerate(parts):
                        src = qk_dram[part, bass.ds(G.g, 1), :, :].rearrange("o (h d) t -> d (o h) t", d=HD)
                        sp.dma_start(raw(tile[G.slot][r * HD:(r + 1) * HD, :, :]), src).then_inc(q_in[G.slot].sem, 16)
                src = v_dram[bass.ds(G.g, 1), :, :].rearrange("o (k p) j -> p (o k) j", p=P)
                sp.dma_start(vs[G.slot][:, :, :], src).then_inc(v_in[G.slot].sem, 16)

            def store(group, qh):
                olo_done.wait(sp, QH * group.g + qh + 1)
                for part, tile in ((0, oT_hi), (1, oT_lo)):
                    dst = o_dram[part, bass.ds(group.g, 1), :, qh * UNIT:(qh + 1) * UNIT]
                    sp.dma_start(dst.rearrange("o p t -> (o p) t"), raw(tile[qh][:, :])).then_inc(o_out[qh].sem, 16)

            def step(cur, prev):
                if prev and cur and (not isinstance(cur.g, int) or cur.g + 1 < GROUPS):
                    if older(prev):
                        pv_done.wait(sp, NC * prev.g)
                        load(cur.ahead(1))
                    else:
                        load(cur.ahead(1))
                if prev and older(prev):
                    store(older(prev), QH - 1)
                if prev:
                    for qh in range(QH - 1):
                        store(prev, qh)
                if cur:
                    mlo_done.wait(sp, cur.g + 1)
                    for row, part in ((STACK, m_hi), (STACK + 1, m_lo)):
                        sp.dma_start(raw(qs[cur.slot][row:row + 1, :, :]).rearrange("o h (q t) -> o (h q) t", q=KT),
                                     raw(part[:, :])).then_inc(m_in[cur.slot].sem, 16)

            load(Group(0, 0, 0))
            load(Group(1, 1, 0))
            steps(step)(sp)
            store(Group(GROUPS - 1, None, None), QH - 1)
            for qh in range(QH):
                o_out[qh].wait(sp, 32 * GROUPS)

        @block.gpsimd
        def _(pool):
            n = make_identity(pool, ident, pool_own, 0)
            n = make_identity(pool, ident16, pool_own, n)
            pool.memset(mask_q[:, :], 0.0).then_inc(pool_own.sem, 1)
            pool.memset(mask_k[:, :], 0.0).then_inc(pool_own.sem, 1)
            pool.memset(ones[:, :], 1.0).then_inc(pool_own.sem, 1)
            pool_own.wait(pool, n + 3)
            pool.affine_select(out=mask_q[:, :], in_=mask_q[:, :], compare_op=ALU.is_ge, fill=MASKED, base=0,
                               pattern=[[-1, P]], channel_multiplier=1).then_inc(pool_own.sem, 1)
            pool.affine_select(out=mask_k[:, :], in_=mask_k[:, :], compare_op=ALU.is_ge, fill=MASKED, base=0,
                               pattern=[[1, P]], channel_multiplier=-1).then_inc(pool_own.sem, 1)
            for i in range(SLOT):
                pool_own.wait(pool, n + 5 + i)
                pool.memset(raw(ks[i][STACK:ROWS, :, :]), 1.0).then_inc(pool_own.sem, 1)
            pool_own.wait(pool, n + 5 + SLOT)
            pool.sem_inc(consts.sem, 1)
            LINKS = 3

            def step(cur, prev):
                if prev:
                    for qh in range(QH):
                        n = QH * prev.g + qh + 1
                        o_free.wait(pool, n)
                        pool.sem_inc(mark.sem, 1)
                        rec_done.wait(pool, n)
                        pool.tensor_tensor(total_sb[qh][:, :], total_sb[qh][:, :], rec[qh][:, :], ALU.mult)
                        pool.tensor_tensor(o32[qh][:, :], o32[qh][:, :], rec[qh][:, :], ALU.mult).then_inc(own_sem.sem, 1)
                        hold(pool, own_sem, LINKS * (n - 1) + 1, mark)
                        pool.tensor_scalar(total_sb[qh][:, :], total_sb[qh][:, :], -1.0, 2.0, ALU.mult, ALU.add).then_inc(own_sem.sem, 1)
                        own_sem.wait(pool, LINKS * (n - 1) + 2)
                        pool.tensor_tensor(o32[qh][:, :], o32[qh][:, :], total_sb[qh][:, :], ALU.mult).then_inc(own_sem.sem, 1)
                        o_out[qh].wait(pool, 32 * prev.g)
                        pool.sem_inc(mark.sem, 1)
                        hold(pool, own_sem, LINKS * (n - 1) + 3, mark)
                        pool.tensor_copy(oT_hi[qh][:, :], o32[qh][:, :]).then_inc(ohi_done.sem, 1)
                        ohi_done.wait(pool, n)
                        pool.tensor_tensor(oT_lo[qh][:, :], o32[qh][:, :], raw(oT_hi[qh][:, :]),
                                           ALU.subtract).then_inc(olo_done.sem, 1)

            steps(step)(pool)

        @block.scalar
        def _(act):
            act.preload_act_table_set("natural_log_exp_and_others")

            def take(group, qh, c):
                pv_done.wait(act, NC * group.g + c + 1)
                olo_done.wait(act, QH * group.g + qh - 1)
                act.activation(total_sb[qh][:, :], ps_sum[:, :], ACT.Copy).then_inc(t_free.sem, 1)

            def invert(group, qh, c):
                n = QH * group.g + qh + 1
                t_free.wait(act, n)
                act.activation(rec[qh][:, :], total_sb[qh][:, :], ACT.Ln).then_inc(ln_done.sem, 1)
                ln_done.wait(act, n)
                act.activation(rec[qh][:, :], rec[qh][:, :], ACT.Exp, scale=-1.0).then_inc(rec_done.sem, 1)


            def step(cur, prev):
                if not prev:
                    return

                def finish(c, h):
                    for back, at in ((1, GH - 1), (2, 1)):
                        e = (c - back) % NC
                        group = prev if c >= back else older(prev)
                        if h == at and e in ENDS and group:
                            (take if back == 1 else invert)(group, chunks[e][0], e)

                for c, (qh, kt) in enumerate(chunks):
                    col = max(kt * P - qh * UNIT, 0)
                    for h in range(GH):
                        n = c * GH + h
                        if h == 0:
                            pv_done.wait(act, NC * prev.g + c - 1)
                        p_done.wait(act, NP * prev.g + n + 1)
                        act.activation(pt[n % NPT][:, col:UNIT], ps_p[n % 2][:, col:UNIT], ACT.Exp,
                                       scale=float(HD) ** -0.5).then_inc(exp_done.sem, 1)
                        finish(c, h)

            steps(step)(act)
            last = Group(GROUPS - 1, None, None)
            take(last, QH - 1, NC - 1)
            invert(last, QH - 1, NC - 1)

        @block.vector
        def _(dve):

            def take(group, qh, c):
                pv_done.wait(dve, NC * group.g + c + 1)
                olo_done.wait(dve, QH * group.g + qh - 1)
                dve.tensor_copy(o32[qh][:, :], ps_o[:, :]).then_inc(o_free.sem, 1)

            def step(cur, prev):
                def maxima(lo, hi):
                    for i in range(lo, hi):
                        h, t = order1[i]
                        s_done.wait(dve, N1 * cur.g + i + 1)
                        dve.reduce_max(rowmax[:, h * KT + t:h * KT + t + 1], ps_s[i % 2][:, 0:(t + 1) * P],
                                       axis=AX.X).then_inc(max_done.sem, 1)

                def negate():
                    mt_done.wait(dve, cur.g + 1)
                    if prev:
                        m_in[prev.slot].wait(dve, 32 * (prev.use + 1))
                    top = ps_s[0][0:GH * KT, 0:P]
                    dve.tensor_scalar_mul(m_hi[:, :], top, -1.0).then_inc(mhi_done.sem, 1)
                    mhi_done.wait(dve, cur.g + 1)
                    dve.scalar_tensor_tensor(m_lo[:, :], top, -1.0, raw(m_hi[:, :]),
                                             op0=ALU.mult, op1=ALU.subtract).then_inc(mlo_done.sem, 1)

                if not prev:
                    maxima(0, N1)
                    negate()
                    return
                for c in range(NC):
                    if cur:
                        maxima(share[c * GH], share[c * GH + GH])
                        if c == TURN:
                            negate()
                    e = (c - 1) % NC
                    group = prev if c else older(prev)
                    if e in ENDS and group:
                        take(group, chunks[e][0], e)

            steps(step)(dve)
            take(Group(GROUPS - 1, None, None), QH - 1, NC - 1)

        @block.tensor
        def _(pe):
            consts.wait(pe, 1)

            def step(cur, prev):
                def scores(lo, hi):
                    for i in range(lo, hi):
                        h, t = order1[i]
                        max_done.wait(pe, N1 * cur.g + i - 1)
                        if i == 0 and prev:
                            mlo_done.wait(pe, cur.g)
                        top, bank = (t + 1) * P, ps_s[i % 2]
                        for c0 in range(0, top, 512):
                            c1 = min(c0 + 512, top)
                            pe.matmul(bank[:, c0:c1], qs[cur.slot][0:STACK, h, t * P:top],
                                      ks[cur.slot][0:STACK, h, c0:c1], start=True, stop=c1 < top)
                        pe.matmul(bank[:, t * P:top], ident16[:, :], mask_q[:, :], start=False, stop=True).then_inc(s_done.sem, 1)

                def accumulate(c, acc, lhs):
                    qh, kt = chunks[c]
                    col = max(kt * P - qh * UNIT, 0)
                    for h in range(GH):
                        last = pe.matmul(acc[h * HD:(h + 1) * HD, col:UNIT], lhs(h), pt[(c * GH + h) % NPT][:, col:UNIT],
                                         start=kt == 0, stop=c in ENDS)
                    return last

                def weigh(group, c):
                    qh, kt = chunks[c]
                    if kt == 0:
                        o_free.wait(pe, QH * group.g + qh)
                    exp_done.wait(pe, NP * group.g + (c + 1) * GH)
                    accumulate(c, ps_o, lambda h: vs[group.slot][:, kt, h * HD:(h + 1) * HD])

                def total(group, c):
                    qh, kt = chunks[c]
                    if kt == 0:
                        t_free.wait(pe, QH * group.g + qh)
                    accumulate(c, ps_sum, lambda h: ones[:, :]).then_inc(pv_done.sem, 1)

                def turn():
                    max_done.wait(pe, N1 * (cur.g + 1))
                    pe.transpose(ps_s[0][0:GH * KT, 0:P], rowmax[:, :], ident[:, :]).then_inc(mt_done.sem, 1)

                if cur:
                    q_in[cur.slot].wait(pe, 96 * (cur.use + 1))
                if not prev:
                    scores(0, N1)
                    turn()
                    return
                for c, (qh, kt) in enumerate(chunks):
                    col = max(kt * P - qh * UNIT, 0)
                    q0 = qh * UNIT + col
                    diag = kt * P >= qh * UNIT
                    if cur and c == TURN:
                        turn()
                    if c == 0:
                        m_in[prev.slot].wait(pe, 32 * (prev.use + 1))
                        v_in[prev.slot].wait(pe, 16 * (prev.use + 1))
                    for h in range(GH):
                        n = c * GH + h
                        exp_done.wait(pe, NP * prev.g + n - 1)
                        last = pe.matmul(ps_p[n % 2][:, col:UNIT], ks[prev.slot][:, h, kt * P:(kt + 1) * P],
                                         qs[prev.slot][:, h, q0:(qh + 1) * UNIT], start=True, stop=not diag)
                        if diag:
                            last = pe.matmul(ps_p[n % 2][:, col:col + P], ident16[:, :], mask_k[:, :], start=False, stop=True)
                        last.then_inc(p_done.sem, 1)
                        if cur:
                            scores(*after(c, h))
                        group = prev if c else older(prev)
                        if group and h == 1:
                            weigh(group, (c - 1) % NC)
                        if group and h == 2:
                            total(group, (c - 1) % NC)
                if not cur:
                    weigh(prev, NC - 1)
                    total(prev, NC - 1)

            steps(step)(pe)


def stage_project_route_shared(nc, x, o_dram, mod_dram, woT, bo, gateT, bias, upT, downT, h2_dram, info_dram, out):
    UP = HS // P
    RING = 4
    with ExitStack() as ctx:
        s = Scope(nc, ctx, "ffn_")
        wo_hi, wo_lo = s.sb("wo_hi", [P, DK, D], F32R), s.sb("wo_lo", [P, DK, D], F32R)
        up_hi, up_lo = s.sb("up_hi", [P, DK, HS], F32R), s.sb("up_lo", [P, DK, HS], F32R)
        dn_hi, dn_lo = s.sb("dn_hi", [P, UP, D], F32R), s.sb("dn_lo", [P, UP, D], F32R)
        gt_hi, gt_lo = s.sb("gt_hi", [P, DK, NE], F32R), s.sb("gt_lo", [P, DK, NE], F32R)
        o_hi, o_lo = s.sb("o_hi", [P, NG, UNIT], F32R), s.sb("o_lo", [P, NG, UNIT], F32R)
        x_sb = [s.sb(f"x{p}", [P, UT, D], FP32) for p in range(2)]
        h2 = s.sb("h2", [P, UT, D], FP32)
        hT_hi, hT_lo = s.sb("hT_hi", [P, DK, UNIT], F32R), s.sb("hT_lo", [P, DK, UNIT], F32R)
        a_hi, a_lo = s.sb("a_hi", [P, UP, UNIT], F32R), s.sb("a_lo", [P, UP, UNIT], F32R)
        relu = [s.sb(f"relu{i}", [P, UNIT], FP32) for i in range(2)]
        att = s.sb("att", [P, D], FP32)
        mod = s.sb("mod", [P, 3, D], FP32)
        gb = s.sb("gb", [P, D], FP32)
        bo_sb = s.sb("bo", [P, D], FP32)
        bias_sb = s.sb("bias", [P, NE], FP32)
        ident = s.sb("ident", [P, P], FP32)
        before = s.sb("before", [P, P], BF16)
        ones = s.sb("ones", [P, P], BF16)
        stats, tmp = s.sb("stats", [P, UT, 6], FP32), s.sb("tmp", [P, UT, 3], FP32)
        mv, std, rstd = s.sb("mv", [P, UT, 2], FP32), s.sb("std", [P, UT], FP32), s.sb("rstd", [P, UT], FP32)
        UG = UT * NGR
        score, biased = s.sb("score", [P, UT, NE], FP32), s.sb("biased", [P, UT, NE], FP32)
        masked = s.sb("masked", [P, UT, NE], FP32)
        pair_hi, pair_lo = s.sb("pair_hi", [P, UG, 2], FP32), s.sb("pair_lo", [P, UG, 2], FP32)
        grp = s.sb("grp", [P, 3, UG], FP32)
        ahead, ties = s.sb("ahead", [P, UG, NGR], FP32), s.sb("ties", [P, UG, NGR], FP32)
        earlier_i, earlier = s.sb("earlier_i", [P, NGR, NGR], I32), s.sb("earlier", [P, NGR, NGR], FP32)
        chosen = s.sb("chosen", [P, UG], I32)
        top, top_idx = s.sb("top", [P, UT, 8], FP32), s.sb("top_idx", [P, UT, 8], U32)
        expert = s.sb("expert", [P, UT, TOPK], FP32)
        iota_i, iota = s.sb("iota_i", [P, NE], I32), s.sb("iota", [P, NE], FP32)
        onehot, picked = s.sb("onehot", [P, UT, TOPK, NE], FP32), s.sb("picked", [P, UT, TOPK, NE], FP32)
        weight, den = s.sb("weight", [P, UT, TOPK], FP32), s.sb("den", [P, UT], FP32)
        sel, sel_acc = s.sb("sel", [P, UT, NE], BF16), s.sb("sel_acc", [P, NE], BF16)
        sel_sum = s.sb("sel_sum", [P, NE], FP32)
        place, over = s.sb("place", [P, UT, TOPK], FP32), s.sb("over", [P, UT, TOPK], FP32)
        tok_i, tok = s.sb("tok_i", [P, UT], I32), s.sb("tok", [P, UT], FP32)
        slot = [s.sb(f"slot{p}", [P, UT * TOPK], I32) for p in range(2)]
        info = [s.sb(f"info{p}", [P, UT * TOPK, 2], FP32) for p in range(2)]

        ps_t = [s.ps(f"ps_t{n}") for n in range(2)]
        ps_m = [s.ps(f"ps_m{n}") for n in range(RING)]
        ps_g, ps_pos = s.ps("ps_g"), s.ps("ps_pos")

        wraw = (h2, x_sb[1])
        w_in, w_hi_done, w_lo_done = s.sems("w_in", 2), s.sem("w_hi"), s.sem("w_lo")
        consts, pool_own, iotas, mark = s.sem("consts"), s.sem("pool_own"), s.sem("iotas"), s.sem("mark")
        o_in, x_in, mod_in, gb_in = s.sem("o_in"), s.sems("x_in", 2), s.sem("mod_in"), s.sem("gb_in")
        dve_own, var_done, std_done, norm_done = s.sem("dve_own"), s.sem("var"), s.sem("std"), s.sem("norm")
        mul_done, h_done = s.sem("mul"), s.sem("h")
        tr_done, hi_done, lo_done = s.sem("tr"), s.sem("hi"), s.sem("lo")
        gate_done, score_done, sel_done, pos_done = s.sem("gate"), s.sem("score"), s.sem("sel"), s.sem("pos")
        up_done, relu_done = s.sem("up"), s.sem("relu")
        sq_done, ahi_done, alo_done = s.sem("sq"), s.sem("ahi"), s.sem("alo")
        proj_done, att_done = s.sem("proj"), s.sem("att")
        down_done, fin_done, out_done = s.sem("down"), s.sem("fin"), s.sem("out")
        slot_done, slot_free = s.sem("slot"), s.sem("slot_free")
        h2_out, x_out, scattered = s.sem("h2_out"), s.sems("x_out", 2), s.sems("scattered", 2, credit=0)
        block = ctx.enter_context(nc.Block())
        LAST = NB - 1

        def steps(eng, body):
            with eng.Fori(0, LAST) as b:
                for half in range(HALVES):
                    body(b, half, True)
            for half in range(HALVES):
                body(LAST, half, half + 1 < HALVES)

        def piece(src, hi, lo, k0, k1):
            return src.rearrange("(k p) n -> p k n", p=P)[:, k0:k1, :], hi[:, k0:k1, :], lo[:, k0:k1, :]
        pieces = [piece(woT, wo_hi, wo_lo, 0, DK), piece(gateT, gt_hi, gt_lo, 0, DK)]
        pieces += [piece(upT, up_hi, up_lo, k, k + 2) for k in range(0, DK, 2)]
        pieces += [piece(downT, dn_hi, dn_lo, k, k + 4) for k in range(0, UP, 4)]
        NW = len(pieces)

        def raw_piece(n):
            k, w = pieces[n][1].shape[1:]
            return wraw[n % 2][:, :, :].rearrange("p a b -> p (a b)")[:, 0:k * w].rearrange("p (a b) -> p a b", a=k)

        @block.sync
        def _(sp):
            s.give_credit(sp)
            def load_o(b, half):
                for part, tile in ((0, o_hi), (1, o_lo)):
                    src = o_dram[part, bass.ds(b * NG, NG), :, half * UNIT:(half + 1) * UNIT]
                    sp.dma_start(raw(tile[:, :, :]), src.rearrange("g p t -> p g t")).then_inc(o_in.sem, 16)

            def load_x(b, half):
                src = x[bass.ds(b, 1), half * UNIT:(half + 1) * UNIT, :]
                sp.dma_start(x_sb[half][:, :, :], src.rearrange("o (t p) d -> p (o t) d", p=P)).then_inc(x_in[half].sem, 16)

            def load_mod(b):
                for m, j in enumerate((M_GA, M_CB, M_SB)):
                    sp.dma_start(mod[:, m, :], mod_dram[bass.ds(b, 1), j, :].broadcast_to([P, D])).then_inc(mod_in.sem, 16)

            def load_gb(b):
                sp.dma_start(gb[:, :], mod_dram[bass.ds(b, 1), M_GB, :].broadcast_to([P, D])).then_inc(gb_in.sem, 16)

            def store_h2(b, half):
                u = b * HALVES + half
                h_done.wait(sp, UT * (u + 1))
                dst = h2_dram[bass.ds(u * UNIT, UNIT), :]
                sp.dma_start(dst.rearrange("(t p) d -> p t d", p=P), h2[:, :, :]).then_inc(h2_out.sem, 16)

            load_o(0, 0)
            load_x(0, 0)
            load_mod(0)
            load_gb(0)
            sp.dma_start(bo_sb[:, :], bo[:, :].broadcast_to([P, D])).then_inc(consts.sem, 16)
            sp.dma_start(bias_sb[:, :], bias[:, :].broadcast_to([P, NE])).then_inc(consts.sem, 16)
            for n in range(NW):
                if n >= 2:
                    w_lo_done.wait(sp, n - 1)
                sp.dma_start(raw_piece(n), pieces[n][0]).then_inc(w_in[n % 2].sem, 16)
            w_lo_done.wait(sp, NW)
            load_x(0, 1)
            proj_done.wait(sp, UT)
            load_o(0, 1)
            store_h2(0, 0)

            def body(b, half, more):
                u = b * HALVES + half
                if more:
                    nb, nhalf = (b, 1) if half == 0 else (b + 1, 0)
                    if half == 0:
                        has_next2 = not (isinstance(b, int) and b == LAST)
                    else:
                        has_next2 = True
                    if has_next2:
                        proj_done.wait(sp, UT * (u + 2))
                        load_o(b + 1, half)
                    store_h2(nb, nhalf)
                    if half == 0 and has_next2:
                        load_mod(b + 1)
                out_done.wait(sp, UT * (u + 1))
                dst = out[bass.ds(u * UNIT, UNIT), :]
                sp.dma_start(dst.rearrange("(t p) d -> p t d", p=P), x_sb[half][:, :, :]).then_inc(x_out[half].sem, 16)
                if not (isinstance(b, int) and b == LAST):
                    x_out[half].wait(sp, 16 * (b + 1))
                    load_x(b + 1, half)
                    if half == 1:
                        load_gb(b + 1)
                hold(sp, scattered[half], 16 * UT * TOPK * (b + 1), slot_free)

            steps(sp, body)
            h2_out.wait(sp, 16 * NB * HALVES)
            for p in range(2):
                x_out[p].wait(sp, 16 * NB)
                scattered[p].wait(sp, 16 * UT * TOPK * NB)

        @block.gpsimd
        def _(pool):
            n = make_identity(pool, ident, pool_own, 0)
            pool.memset(ones[:, :], 1.0).then_inc(pool_own.sem, 1)
            pool.memset(before[:, :], 1.0).then_inc(pool_own.sem, 1)
            pool_own.wait(pool, n + 2)
            pool.affine_select(out=before[:, :], in_=before[:, :], compare_op=ALU.is_gt, fill=0.0, base=0,
                               pattern=[[1, P]], channel_multiplier=-1).then_inc(pool_own.sem, 1)
            pool.iota(earlier_i[:, :, :], pattern=[[1, NGR], [-1, NGR]], base=0, channel_multiplier=0)
            pool.iota(iota_i[:, :], pattern=[[1, NE]], base=0, channel_multiplier=0)
            pool.iota(tok_i[:, :], pattern=[[P, UT]], base=0, channel_multiplier=1).then_inc(iotas.sem, 1)

            def modulate(b, half):
                u = b * HALVES + half
                for t in range(UT):
                    norm_done.wait(pool, UT * u + t + 1)
                    ht = h2[:, t, :]
                    pool.tensor_tensor(ht, ht, mod[:, 1, :], ALU.mult).then_inc(mul_done.sem, 1)
                    mul_done.wait(pool, UT * u + t + 1)
                    pool.tensor_tensor(ht, ht, mod[:, 2, :], ALU.add).then_inc(h_done.sem, 1)

            modulate(0, 0)

            def body(b, half, more):
                u = b * HALVES + half
                if more:
                    modulate(*((b, 1) if half == 0 else (b + 1, 0)))
                hold(pool, slot_done, u + 1, mark)
                for j in range(UT * TOPK):
                    pool.indirect_dma_start(
                        info_dram[:, :], bass.IndirectOffsetOnAxis(slot[half][:, j:j + 1].bitcast(U32), 0),
                        info[half][:, j, :], None, bounds_check=SLOTS - 1, oob_is_err=False).then_inc(scattered[half].sem, 16)

            steps(pool, body)

        @block.scalar
        def _(act):
            for n in range(NW):
                w_in[n % 2].wait(act, 16 * (n // 2 + 1))
                act.activation(pieces[n][1], raw_piece(n), ACT.Copy).then_inc(w_hi_done.sem, 1)

            def root(u):
                var_done.wait(act, u + 1)
                act.activation(std[:, :], mv[:, :, 1], ACT.Sqrt).then_inc(std_done.sem, 1)

            root(0)

            def body(b, half, more):
                u = b * HALVES + half
                up_done.wait(act, UP * u)
                for k in range(DK):
                    tr_done.wait(act, DK * u + k + 1)
                    act.activation(hT_hi[:, k, :], ps_t[k % 2][:, :], ACT.Copy).then_inc(hi_done.sem, 1)
                down_done.wait(act, UT * u)

                def high(n):
                    sq_done.wait(act, UP * u + n + 1)
                    act.activation(a_hi[:, n, :], relu[n % 2][:, :], ACT.Copy).then_inc(ahi_done.sem, 1)

                for n in range(UP):
                    up_done.wait(act, UP * u + n + 1)
                    alo_done.wait(act, UP * u + n - 1)
                    act.activation(relu[n % 2][:, :], ps_m[n % RING][:, :], ACT.Relu).then_inc(relu_done.sem, 1)
                    if n:
                        high(n - 1)
                high(UP - 1)
                if more:
                    root(u + 1)
                gate_done.wait(act, u + 1)
                act.activation(score[:, :, :].rearrange("p t e -> p (t e)"), ps_g[:, 0:UT * NE], ACT.Sigmoid).then_inc(score_done.sem, 1)

            steps(act, body)

        @block.vector
        def _(dve):
            iotas.wait(dve, 1)
            dve.tensor_single_scalar(earlier[:, :, :], earlier_i[:, :, :], 0, op=ALU.is_gt)
            dve.tensor_copy(iota[:, :], iota_i[:, :])
            dve.tensor_copy(tok[:, :], tok_i[:, :])
            dve.memset(sel_acc[:, :], 0.0)
            dve.memset(sel_sum[:, :], 0.0)
            for n in range(NW):
                w_hi_done.wait(dve, n + 1)
                dve.tensor_tensor(pieces[n][2], raw_piece(n), raw(pieces[n][1]), ALU.subtract).then_inc(w_lo_done.sem, 1)
            consts.wait(dve, 32)
            LINKS = 2 * UT + 1 + STAT_LINKS + ROOT_LINKS

            def attend(b, half):
                u = b * HALVES + half
                chain = Chain(dve, dve_own, LINKS * u)
                xs = x_sb[half]
                x_in[half].wait(dve, 16 * (b + 1))
                mod_in.wait(dve, 48 * (b + 1))
                for t in range(UT):
                    proj_done.wait(dve, UT * u + t + 1)
                    dve.tensor_tensor(att[:, :], ps_m[t % RING][:, :], bo_sb[:, :], ALU.add).then_inc(att_done.sem, 1)
                    att_done.wait(dve, UT * u + t + 1)
                    chain.done(dve.tensor_tensor(att[:, :], att[:, :], mod[:, 0, :], ALU.mult))
                    chain.wait()
                    chain.done(dve.tensor_tensor(xs[:, t, :], xs[:, t, :], att[:, :], ALU.add))
                    chain.wait()
                    last = dve.bn_stats(stats[:, t, :], xs[:, t, :])
                chain.done(last)
                chain.wait()
                combine_stats(chain, stats, mv, tmp).then_inc(var_done.sem, 1)
                std_done.wait(dve, u + 1)
                var_done.wait(dve, u + 1)
                inverse_root(chain, rstd, std, mv[:, :, 1], tmp[:, :, 0])
                assert chain.n == LINKS
                tr_done.wait(dve, DK * u)
                h2_out.wait(dve, 16 * u)
                for t in range(UT):
                    dve.tensor_scalar(h2[:, t, :], xs[:, t, :], mv[:, t, 0:1], rstd[:, t:t + 1],
                                      ALU.subtract, ALU.mult).then_inc(norm_done.sem, 1)

            def groups(t):
                return t.rearrange("p (t g) -> p t g", t=UT)

            def choose(u):
                score_done.wait(dve, u + 1)
                dve.tensor_tensor(biased[:, :, :], score[:, :, :], bias_sb[:, :].unsqueeze(1).broadcast_to([P, UT, NE]), ALU.add)
                dve.drain()
                pairs = biased[:, :, :].rearrange("p t (g r) -> p (t g) r", r=EPG)
                dve.tensor_tensor(pair_hi[:, :, :], pairs[:, :, 0::2], pairs[:, :, 1::2], ALU.max)
                dve.tensor_tensor(pair_lo[:, :, :], pairs[:, :, 0::2], pairs[:, :, 1::2], ALU.min)
                dve.drain()
                best, second, third = (grp[:, i, :] for i in range(3))
                dve.tensor_tensor(best, pair_hi[:, :, 0], pair_hi[:, :, 1], ALU.max)
                dve.tensor_tensor(second, pair_hi[:, :, 0], pair_hi[:, :, 1], ALU.min)
                dve.tensor_tensor(third, pair_lo[:, :, 0], pair_lo[:, :, 1], ALU.max)
                dve.drain()
                dve.tensor_tensor(second, second, third, ALU.max)
                dve.drain()
                dve.tensor_tensor(best, best, second, ALU.add)
                dve.drain()
                other = groups(best).unsqueeze(2).broadcast_to([P, UT, NGR, NGR])
                own = groups(best).unsqueeze(3).broadcast_to([P, UT, NGR, NGR])
                four = lambda t: t[:, :, :].rearrange("p (t g) h -> p t g h", t=UT)
                dve.tensor_tensor(four(ahead), other, own, ALU.is_gt)
                dve.tensor_tensor(four(ties), other, own, ALU.is_equal)
                dve.drain()
                dve.tensor_tensor(four(ties), four(ties), earlier[:, :, :].unsqueeze(1).broadcast_to([P, UT, NGR, NGR]), ALU.mult)
                dve.drain()
                dve.tensor_tensor(ahead[:, :, :], ahead[:, :, :], ties[:, :, :], ALU.add)
                dve.drain()
                dve.tensor_reduce(grp[:, 2, :], ahead[:, :, :], axis=AX.X, op=ALU.add)
                dve.memset(masked[:, :, :], 0.0)
                dve.drain()
                dve.tensor_single_scalar(chosen[:, :], grp[:, 2, :], float(TOPG), op=ALU.is_lt)
                dve.drain()
                dve.copy_predicated(masked[:, :, :].rearrange("p t (g r) -> p (t g) r", r=EPG),
                                    chosen[:, :].unsqueeze(2).broadcast_to([P, UG, EPG]), pairs)
                dve.drain()
                for t in range(UT):
                    dve.max(top[:, t, :], masked[:, t, :])
                dve.drain()
                for t in range(UT):
                    dve.max_index(top_idx[:, t, :], top[:, t, :], masked[:, t, :])
                dve.drain()
                dve.tensor_copy(expert[:, :, :], top_idx[:, :, 0:TOPK])
                dve.drain()
                flat = lambda t: t[:, :, :, :].rearrange("p t k e -> p (t k) e")
                dve.tensor_tensor(flat(onehot), iota[:, :].unsqueeze(1).broadcast_to([P, UT * TOPK, NE]),
                                  expert[:, :, :].rearrange("p t k -> p (t k)").unsqueeze(2).broadcast_to([P, UT * TOPK, NE]),
                                  ALU.is_equal)
                dve.drain()
                with nc.allow_low_precision("0 or 1"):
                    dve.tensor_reduce(sel[:, :, :], onehot[:, :, :, :].rearrange("p t k e -> p t e k"), axis=AX.X, op=ALU.add).then_inc(sel_done.sem, 1)
                dve.tensor_tensor(picked[:, :, :, :], onehot[:, :, :, :], score[:, :, :].unsqueeze(2).broadcast_to([P, UT, TOPK, NE]), ALU.mult)
                dve.drain()
                dve.tensor_reduce(weight[:, :, :], picked[:, :, :, :], axis=AX.X, op=ALU.add)
                dve.drain()
                dve.tensor_reduce(den[:, :], weight[:, :, :], axis=AX.X, op=ALU.add)
                dve.drain()
                dve.tensor_scalar_add(den[:, :], den[:, :], 1e-20)
                dve.drain()
                dve.reciprocal(den[:, :], den[:, :])
                dve.drain()
                dve.tensor_scalar_mul(den[:, :], den[:, :], ROUTE_SCALE)

            def give_slots(u, b, half):
                slot_free.wait(dve, u - 1)
                pos_done.wait(dve, u + 1)
                dve.tensor_tensor(picked[:, :, :, :], onehot[:, :, :, :],
                                  ps_pos[:, 0:UT * NE].rearrange("p (t e) -> p t e", t=UT).unsqueeze(2).broadcast_to([P, UT, TOPK, NE]), ALU.mult)
                pairs = info[half][:, :, :].rearrange("p (t k) c -> p t k c", t=UT)
                dve.tensor_tensor(pairs[:, :, :, 1], weight[:, :, :], den[:, :].unsqueeze(2).broadcast_to([P, UT, TOPK]), ALU.mult)
                dve.tensor_copy(pairs[:, :, :, 0], tok[:, :].unsqueeze(2).broadcast_to([P, UT, TOPK]))
                dve.tensor_reduce(sel_sum[:, :], sel[:, :, :].rearrange("p t e -> p e t"), axis=AX.X, op=ALU.add)
                dve.drain()
                dve.tensor_tensor(sel_acc[:, :], sel_acc[:, :], sel_sum[:, :], ALU.add)
                dve.tensor_reduce(place[:, :, :], picked[:, :, :, :], axis=AX.X, op=ALU.add)
                dve.tensor_scalar_add(tok[:, :], tok[:, :], float(UNIT))
                dve.drain()
                dve.tensor_scalar(over[:, :, :], place[:, :, :], float(CAP), float(SLOTS), ALU.is_ge, ALU.mult)
                dve.scalar_tensor_tensor(place[:, :, :], expert[:, :, :], float(CAP), place[:, :, :], op0=ALU.mult, op1=ALU.add)
                dve.drain()
                dve.tensor_tensor(slot[half][:, :].rearrange("p (t k) -> p t k", t=UT), place[:, :, :], over[:, :, :], ALU.add).then_inc(slot_done.sem, 1)

            attend(0, 0)

            def body(b, half, more):
                u = b * HALVES + half
                for k in range(DK):
                    hi_done.wait(dve, DK * u + k + 1)
                    dve.tensor_tensor(hT_lo[:, k, :], ps_t[k % 2][:, :], raw(hT_hi[:, k, :]), ALU.subtract).then_inc(lo_done.sem, 1)

                def low(n):
                    ahi_done.wait(dve, UP * u + n + 1)
                    dve.tensor_tensor(a_lo[:, n, :], relu[n % 2][:, :], raw(a_hi[:, n, :]), ALU.subtract).then_inc(alo_done.sem, 1)

                for n in range(UP):
                    relu_done.wait(dve, UP * u + n + 1)
                    dve.tensor_tensor(relu[n % 2][:, :], relu[n % 2][:, :], relu[n % 2][:, :], ALU.mult).then_inc(sq_done.sem, 1)
                    if n:
                        low(n - 1)
                low(UP - 1)
                if more:
                    attend(*((b, 1) if half == 0 else (b + 1, 0)))
                choose(u)
                gb_in.wait(dve, 16 * (b + 1))
                for t in range(UT):
                    down_done.wait(dve, UT * u + t + 1)
                    if t:
                        out_done.wait(dve, UT * u + t)
                    dve.tensor_tensor(att[:, :], ps_m[t % RING][:, :], gb[:, :], ALU.mult).then_inc(fin_done.sem, 1)
                    fin_done.wait(dve, UT * u + t + 1)
                    dve.tensor_tensor(x_sb[half][:, t, :], x_sb[half][:, t, :], att[:, :], ALU.add).then_inc(out_done.sem, 1)
                give_slots(u, b, half)

            steps(dve, body)

        @block.tensor
        def _(pe):
            THREE = ((0, 0), (0, 1), (1, 0))

            def exact(bank, pairs):
                for i, (a, c) in enumerate(pairs):
                    for j, (m, n) in enumerate(THREE):
                        last = pe.matmul(bank, a[m], c[n], start=i + j == 0, stop=i + 1 == len(pairs) and j == 2)
                return last

            def project(b, half, free):
                u = b * HALVES + half
                o_in.wait(pe, 32 * (u + 1))
                for t in range(UT):
                    free(t)
                    cols = slice(t * P, (t + 1) * P)
                    exact(ps_m[t % RING][:, :], [((o_hi[:, g, cols], o_lo[:, g, cols]), (wo_hi[:, g, :], wo_lo[:, g, :]))
                                                 for g in range(NG)]).then_inc(proj_done.sem, 1)

            pool_own.wait(pe, 5)
            w_lo_done.wait(pe, 1)
            project(0, 0, lambda t: None)
            w_lo_done.wait(pe, NW)

            def body(b, half, more):
                u = b * HALVES + half
                h_done.wait(pe, UT * (u + 1))
                for k in range(DK):
                    lo_done.wait(pe, DK * u + k - 1)
                    for t in range(UT):
                        last = pe.transpose(ps_t[k % 2][:, t * P:(t + 1) * P], h2[:, t, k * P:(k + 1) * P], ident[:, :])
                    last.then_inc(tr_done.sem, 1)
                lo_done.wait(pe, DK * (u + 1))
                score_done.wait(pe, u)
                for t in range(UT):
                    cols = slice(t * P, (t + 1) * P)
                    last = exact(ps_g[:, t * NE:(t + 1) * NE], [((hT_hi[:, k, cols], hT_lo[:, k, cols]), (gt_hi[:, k, :], gt_lo[:, k, :]))
                                                               for k in range(DK)])
                last.then_inc(gate_done.sem, 1)
                for n in range(UP):
                    if n < RING:
                        fin_done.wait(pe, UT * (u - 1) + n + 1)
                    else:
                        relu_done.wait(pe, UP * u + n - RING + 1)
                    cols = slice(n * P, (n + 1) * P)
                    exact(ps_m[n % RING][:, :], [((up_hi[:, k, cols], up_lo[:, k, cols]), (hT_hi[:, k, :], hT_lo[:, k, :]))
                                                 for k in range(DK)]).then_inc(up_done.sem, 1)
                if more:
                    project(*((b, 1) if half == 0 else (b + 1, 0)), lambda t: relu_done.wait(pe, UP * u + UP - RING + t + 1))
                alo_done.wait(pe, UP * (u + 1))
                for t in range(UT):
                    if more:
                        att_done.wait(pe, UT * (u + 1) + t + 1)
                    else:
                        relu_done.wait(pe, UP * (u + 1))
                    cols = slice(t * P, (t + 1) * P)
                    exact(ps_m[t % RING][:, :], [((a_hi[:, n, cols], a_lo[:, n, cols]), (dn_hi[:, n, :], dn_lo[:, n, :]))
                                                 for n in range(UP)]).then_inc(down_done.sem, 1)
                sel_done.wait(pe, u + 1)
                slot_done.wait(pe, u)
                for t in range(UT):
                    bank = ps_pos[:, t * NE:(t + 1) * NE]
                    pe.matmul(bank, before[:, :], sel[:, t, :], start=True, stop=False)
                    for t2 in range(t):
                        pe.matmul(bank, ones[:, :], sel[:, t2, :], start=False, stop=False)
                    last = pe.matmul(bank, ones[:, :], sel_acc[:, :], start=False, stop=True)
                last.then_inc(pos_done.sem, 1)

            steps(pe, body)


def stage_experts(nc, e_upT, e_downT, h2_dram, mod_dram, info_dram, out):
    J, HT = CAP // P, HID // P
    with ExitStack() as ctx:
        s = Scope(nc, ctx, "exp_")
        two = range(2)
        upr, dnr = ([s.sb(f"{n}{p}", sh, FP32) for p in two] for n, sh in (("upr", [P, DK, HID]), ("dnr", [P, HT, D])))
        up_hi, up_lo = ([s.sb(f"{n}{p}", [P, DK, HID], F32R) for p in two] for n in ("up_hi", "up_lo"))
        dn_hi, dn_lo = ([s.sb(f"{n}{p}", [P, HT, D], F32R) for p in two] for n in ("dn_hi", "dn_lo"))
        info = [s.sb(f"info{p}", [P, J, 2], FP32) for p in two]
        tok = [s.sb(f"tok{p}", [P, J], I32) for p in two]
        row = [s.sb(f"row{p}", [P, J], I32) for p in two]
        xg = [s.sb(f"xg{p}", [P, J, D], FP32) for p in two]
        gbg = [s.sb(f"gbg{p}", [P, J, D], FP32) for p in two]
        xT_hi, xT_lo = ([s.sb(f"{n}{p}", [P, DK, CAP], F32R) for p in two] for n in ("xT_hi", "xT_lo"))
        relu = s.sb("relu", [P, HT, CAP], FP32)
        a_hi, a_lo = s.sb("a_hi", [P, HT, CAP], F32R), s.sb("a_lo", [P, HT, CAP], F32R)
        y = [s.sb(f"y{p}", [P, J, D], FP32) for p in two]
        ident = s.sb("ident", [P, P], FP32)
        ps_t = [s.ps(f"ps_t{n}") for n in range(2)]
        ps_u = [s.ps(f"ps_u{n}") for n in range(HT)]
        ps_y = [s.ps(f"ps_y{n}") for n in range(2 * J)]

        w_in, info_in = s.sems("w_in", 2), s.sems("info_in", 2)
        pool_own, mark = s.sem("pool_own"), s.sem("mark")
        tok_done, row_done = s.sem("tok"), s.sem("row")
        x_in, added = s.sems("x_in", 2, credit=0), s.sem("added", credit=0)
        all_added = s.sem("all_added")
        whi_done, wlo_done, dlo_done = s.sem("whi"), s.sem("wlo"), s.sem("dlo")
        tr_done, xhi_done, xlo_done = s.sem("tr"), s.sem("xhi"), s.sem("xlo")
        up_done, relu_done, sq_done = s.sem("up"), s.sem("relu"), s.sem("sq")
        ahi_done, alo_done = s.sem("ahi"), s.sem("alo")
        dn_done, y_done = s.sem("dn"), s.sem("y")
        block = ctx.enter_context(nc.Block())

        def steps(eng, body):
            with eng.Fori(0, NE // 2) as i:
                for p in two:
                    body(i * 2 + p, p, i)

        @block.sync
        def _(sp):
            s.give_credit(sp)
            def body(e, p, i):
                wlo_done.wait(sp, e - 1)
                dlo_done.wait(sp, e - 1)
                sp.dma_start(upr[p][:, :, :], e_upT[bass.ds(e, 1), :, :].rearrange("o (k p) n -> p (o k) n", p=P)).then_inc(w_in[p].sem, 16)
                sp.dma_start(dnr[p][:, :, :], e_downT[bass.ds(e, 1), :, :].rearrange("o (k p) n -> p (o k) n", p=P)).then_inc(w_in[p].sem, 16)
                y_done.wait(sp, J * (e - 1))
                sp.dma_start(info[p][:, :, :], info_dram[bass.ds(e * CAP, CAP), :].rearrange("(j p) c -> p j c", p=P)).then_inc(info_in[p].sem, 16)

            def relay(e):
                hold(sp, added, 16 * J * (e + 1), all_added)

            for e in two:
                body(e, e, 0)
            with sp.Fori(1, NE // 2) as i:
                for p in two:
                    body(i * 2 + p, p, i)
                    relay(i * 2 + p - 2)
            for e in (NE - 2, NE - 1):
                relay(e)

        @block.gpsimd
        def _(pool):
            make_identity(pool, ident, pool_own, 0)

            def body(e, p, i):
                hold(pool, row_done, e + 1, mark)
                xlo_done.wait(pool, 2 * (e - 1))
                pool.sem_inc(mark.sem, 1)
                y_done.wait(pool, J * (e - 1))
                pool.sem_inc(mark.sem, 1)
                for j in range(J):
                    pool.indirect_dma_start(xg[p][:, j, :], None, h2_dram[:, :],
                                            bass.IndirectOffsetOnAxis(tok[p][:, j:j + 1].bitcast(U32), 0)).then_inc(x_in[p].sem, 16)
                    pool.indirect_dma_start(gbg[p][:, j, :], None, mod_dram.rearrange("b m d -> (b m) d"),
                                            bass.IndirectOffsetOnAxis(row[p][:, j:j + 1].bitcast(U32), 0)).then_inc(x_in[p].sem, 16)
                dn_done.wait(pool, J * (e - 1))
                pool.sem_inc(mark.sem, 1)
                whi_done.wait(pool, 2 * (e + 1))
                pool.tensor_tensor(dn_lo[p][:, :, :], dnr[p][:, :, :], raw(dn_hi[p][:, :, :]), ALU.subtract).then_inc(dlo_done.sem, 1)

            def add(e, p):
                y_done.wait(pool, J * (e + 1))
                pool.sem_inc(mark.sem, 1)
                if not isinstance(e, int) or e:
                    hold(pool, added, 16 * J * e, mark)
                for j in range(J):
                    pool.indirect_dma_start(out[:, :], bass.IndirectOffsetOnAxis(tok[p][:, j:j + 1].bitcast(U32), 0),
                                            y[p][:, j, :], None, compute_op=ALU.add).then_inc(added.sem, 16)

            body(0, 0, 0)
            body(1, 1, 0)
            add(0, 0)
            with pool.Fori(1, NE // 2) as i:
                for p in two:
                    body(i * 2 + p, p, i)
                    add(i * 2 + p - 1, 1 - p)
            add(NE - 1, 1)

        @block.scalar
        def _(act):
            def weights(e, p, i):
                w_in[p].wait(act, 32 * (i + 1))
                dn_done.wait(act, J * (e - 1))
                act.activation(up_hi[p][:, :, :], upr[p][:, :, :], ACT.Copy).then_inc(whi_done.sem, 1)
                act.activation(dn_hi[p][:, :, :], dnr[p][:, :, :], ACT.Copy).then_inc(whi_done.sem, 1)

            def body(e, p, i, more=True):
                if more:
                    weights(e + 1, 1 - p, i + p)
                for n in range(2):
                    tr_done.wait(act, 2 * e + n + 1)
                    act.activation(xT_hi[p][:, 2 * n:2 * n + 2, :].rearrange("p k c -> p (k c)"), ps_t[n][:, :], ACT.Copy).then_inc(xhi_done.sem, 1)
                for n in range(HT):
                    up_done.wait(act, HT * e + n + 1)
                    if n == 0:
                        alo_done.wait(act, e)
                    act.activation(relu[:, n, :], ps_u[n][:, 0:CAP], ACT.Relu).then_inc(relu_done.sem, 1)
                sq_done.wait(act, e + 1)
                act.activation(a_hi[:, :, :], relu[:, :, :], ACT.Copy).then_inc(ahi_done.sem, 1)

            weights(0, 0, 0)
            with act.Fori(0, NE // 2 - 1) as i:
                for p in two:
                    body(i * 2 + p, p, i)
            body(NE - 2, 0, NE // 2 - 1)
            body(NE - 1, 1, NE // 2 - 1, more=False)

        @block.vector
        def _(dve):

            def tokens(e, p, i):
                info_in[p].wait(dve, 16 * (i + 1))
                all_added.wait(dve, e - 1)
                dve.tensor_copy(tok[p][:, :], info[p][:, :, 0]).then_inc(tok_done.sem, 1)
                tok_done.wait(dve, e + 1)
                dve.tensor_single_scalar(row[p][:, :], tok[p][:, :], S.bit_length() - 1, op=ALU.logical_shift_right)
                dve.drain()
                dve.tensor_scalar(row[p][:, :], row[p][:, :], 6.0, float(M_GB), ALU.mult, ALU.add).then_inc(row_done.sem, 1)
                whi_done.wait(dve, 2 * e + 1)
                dve.tensor_tensor(up_lo[p][:, :, :], upr[p][:, :, :], raw(up_hi[p][:, :, :]), ALU.subtract).then_inc(wlo_done.sem, 1)

            def body(e, p, i, more=True):
                if more:
                    tokens(e + 1, 1 - p, i + p)
                for n in range(2):
                    xhi_done.wait(dve, 2 * e + n + 1)
                    dve.tensor_tensor(xT_lo[p][:, 2 * n:2 * n + 2, :].rearrange("p k c -> p (k c)"), ps_t[n][:, :],
                                      raw(xT_hi[p][:, 2 * n:2 * n + 2, :]).rearrange("p k c -> p (k c)"), ALU.subtract).then_inc(xlo_done.sem, 1)
                relu_done.wait(dve, HT * (e + 1))
                dve.tensor_tensor(relu[:, :, :], relu[:, :, :], relu[:, :, :], ALU.mult).then_inc(sq_done.sem, 1)
                ahi_done.wait(dve, e + 1)
                dve.tensor_tensor(a_lo[:, :, :], relu[:, :, :], raw(a_hi[:, :, :]), ALU.subtract).then_inc(alo_done.sem, 1)
                x_in[p].wait(dve, 64 * (i + 1))
                for j in range(J):
                    dn_done.wait(dve, J * e + j + 1)
                    dve.scalar_tensor_tensor(y[p][:, j, :], ps_y[p * J + j][:, :], info[p][:, j, 1:2], gbg[p][:, j, :],
                                             op0=ALU.mult, op1=ALU.mult).then_inc(y_done.sem, 1)

            tokens(0, 0, 0)
            with dve.Fori(0, NE // 2 - 1) as i:
                for p in two:
                    body(i * 2 + p, p, i)
            body(NE - 2, 0, NE // 2 - 1)
            body(NE - 1, 1, NE // 2 - 1, more=False)

        @block.tensor
        def _(pe):
            THREE = ((0, 0), (0, 1), (1, 0))
            pool_own.wait(pe, 2)

            def body(e, p, i):
                x_in[p].wait(pe, 64 * (i + 1))
                for n in range(2):
                    xlo_done.wait(pe, 2 * (e - 1) + n + 1)
                    for k in (2 * n, 2 * n + 1):
                        for j in range(J):
                            col = (k % 2) * CAP + j * P
                            last = pe.transpose(ps_t[n][:, col:col + P], xg[p][:, j, k * P:(k + 1) * P], ident[:, :])
                    last.then_inc(tr_done.sem, 1)
                xlo_done.wait(pe, 2 * (e + 1))
                wlo_done.wait(pe, e + 1)
                relu_done.wait(pe, HT * e)
                for n in range(HT):
                    for k in range(DK):
                        for a, c in THREE:
                            last = pe.matmul(ps_u[n][:, 0:CAP], (up_hi, up_lo)[a][p][:, k, n * P:(n + 1) * P],
                                             (xT_hi, xT_lo)[c][p][:, k, :], start=k + a + c == 0, stop=k == DK - 1 and a == 1)
                    last.then_inc(up_done.sem, 1)
                alo_done.wait(pe, e + 1)
                dlo_done.wait(pe, e + 1)
                y_done.wait(pe, J * (e - 1))
                for j in range(J):
                    for n in range(HT):
                        for a, c in THREE:
                            last = pe.matmul(ps_y[p * J + j][:, :], (a_hi, a_lo)[a][:, n, j * P:(j + 1) * P],
                                             (dn_hi, dn_lo)[c][p][:, n, :], start=n + a + c == 0, stop=n == HT - 1 and a == 1)
                    last.then_inc(dn_done.sem, 1)

            steps(pe, body)


def build(nc, x, cT, wmod, wqkvT, bqk, bv, woT, bo, gateT, bias, sh_upT, sh_downT, e_upT, e_downT, out):
    mod_dram = nc.dram_tensor("mod_rows", [NB + 1, 6, D], FP32, kind="Internal").ap()
    qk_dram = nc.dram_tensor("qk_parts", [4, NB * NG, P, S], FP32, kind="Internal").ap()
    v_dram = nc.dram_tensor("v_rows", [NB * NG, S, P], FP32, kind="Internal").ap()
    o_dram = nc.dram_tensor("o_parts", [2, NB * NG, P, S], FP32, kind="Internal").ap()
    h2_dram = nc.dram_tensor("h2_rows", [T + CAP, D], FP32, kind="Internal").ap()
    info_dram = nc.dram_tensor("slot_info", [SLOTS, 2], FP32, kind="Internal").ap()
    stage_modulation(nc, cT, wmod, mod_dram, h2_dram, info_dram, out)
    stage_qkv(nc, x, wqkvT, bqk, bv, mod_dram, qk_dram, v_dram)
    stage_attention(nc, qk_dram, v_dram, o_dram)
    stage_project_route_shared(nc, x, o_dram, mod_dram, woT, bo, gateT, bias, sh_upT, sh_downT, h2_dram, info_dram, out)
    stage_experts(nc, e_upT, e_downT, h2_dram, mod_dram, info_dram, out)


def kernel(L0_attn_x, L0_attn_w_q, L0_attn_b_q, L0_attn_w_k, L0_attn_b_k, L0_attn_w_v, L0_attn_b_v, L0_attn_w_o,
           L0_attn_b_o, L0_ffn_gate_w, L0_ffn_bias_corr, L0_ffn_up_w, L0_ffn_down_w, L0_ffn_shared_up_w,
           L0_ffn_shared_down_w, L0_c, L0_wmod):
    import concourse.bacc as bacc
    from concourse.bass_utils import run_bass_kernel_spmd

    a = np.asarray
    arrays = {
        "x": a(L0_attn_x),
        "cT": a(L0_c).T,
        "wmod": a(L0_wmod),
        "wqkvT": np.stack([a(w).T for w in (L0_attn_w_q, L0_attn_w_k, L0_attn_w_v)]),
        "bqk": np.concatenate([a(b).reshape(NG, P).T for b in (L0_attn_b_q, L0_attn_b_k)], axis=1),
        "bv": a(L0_attn_b_v).reshape(1, D),
        "woT": a(L0_attn_w_o).T,
        "bo": a(L0_attn_b_o).reshape(1, D),
        "gateT": a(L0_ffn_gate_w).T,
        "bias": a(L0_ffn_bias_corr).reshape(1, NE),
        "sh_upT": a(L0_ffn_shared_up_w).T,
        "sh_downT": a(L0_ffn_shared_down_w).T,
        "e_upT": a(L0_ffn_up_w).transpose(0, 2, 1),
        "e_downT": a(L0_ffn_down_w).transpose(0, 2, 1),
    }
    arrays = {n: np.ascontiguousarray(v) for n, v in arrays.items()}
    nc = bacc.Bacc("TRN2", target_bir_lowering=False, num_devices=1)
    args = [nc.dram_tensor(n, v.shape, mybir.dt.from_np(v.dtype), kind="ExternalInput").ap() for n, v in arrays.items()]
    out = nc.dram_tensor("out", (T + CAP, D), FP32, kind="ExternalOutput").ap()
    build(nc, *args, out)
    r = run_bass_kernel_spmd(nc, [arrays], core_ids=[0])
    return r.results[0]["out"][:T].reshape(NB, S, D)
```

```python
import numpy as np
import concourse.bass as bass
from concourse import mybir
from contextlib import ExitStack

FP32 = mybir.dt.float32
F32R = mybir.dt.float32r
BF16 = mybir.dt.bfloat16
I32 = mybir.dt.int32
U32 = mybir.dt.uint32
ALU = mybir.AluOpType
ACT = mybir.ActivationFunctionType
AX = mybir.AxisListType

P = 128
NB, S, D = 8, 1024, 512
T = NB * S
DK = D // P
HD = 32
NG = D // P
GH = P // HD
UNIT = 512
UT = UNIT // P
HALVES = S // UNIT
NE, NGR, EPG = 32, 8, 4
TOPG, TOPK = 4, 4
HID, HS, CAP = 256, 1024, 256
ROUTE_SCALE = 2.5
EPS = 1e-5
MASKED = -1.0e30
QHI, QLO, KHI, KLO = range(4)
SLOTS = NE * CAP
M_SA, M_CA, M_GA, M_SB, M_CB, M_GB = range(6)


def raw(ap):
    return ap.bitcast(FP32)


class Chain:

    def __init__(self, eng, sem, base):
        self.eng, self.sem, self.base, self.n = eng, sem, base, 0

    def done(self, ins):
        self.n += 1
        ins.then_inc(self.sem.sem, 1)

    def wait(self):
        self.sem.wait(self.eng, self.base + self.n)


class Sem:

    def __init__(self, sem, credit):
        self.sem, self.credit = sem, credit

    def wait(self, eng, value):
        low = value if isinstance(value, int) else value.min_val
        if isinstance(value, int) and value <= 0:
            return
        assert isinstance(value, int) or low + self.credit > 0, (self.sem, low)
        eng.wait_ge(self.sem, value + self.credit)


def hold(eng, sem, value, mark):
    sem.wait(eng, value)
    eng.sem_inc(mark.sem, 1)


class Scope:

    def __init__(self, nc, ctx, prefix, credit=16):
        self.nc, self.ctx, self.prefix, self.credit, self.all = nc, ctx, prefix, credit, []

    def sb(self, name, shape, dt):
        return self.ctx.enter_context(self.nc.sbuf_tensor(self.prefix + name, shape, dt))

    def ps(self, name, shape=(P, 512), dt=FP32):
        return self.ctx.enter_context(self.nc.psum_tensor(self.prefix + name, list(shape), dt))

    def sem(self, name, credit=None):
        sem = Sem(self.ctx.enter_context(self.nc.semaphore(self.prefix + name)),
                  self.credit if credit is None else credit)
        self.all.append(sem)
        return sem

    def sems(self, name, n, credit=None):
        return [self.sem(f"{name}{i}", credit) for i in range(n)]

    def give_credit(self, eng):
        for sem in self.all:
            if sem.credit:
                eng.sem_inc(sem.sem, sem.credit)


STAT_LINKS, ROOT_LINKS = 2, 5


def combine_stats(chain, stats, mv, tmp):
    dve = chain.eng
    total, diff, m2 = tmp[:, :, 0], tmp[:, :, 1], tmp[:, :, 2]
    dve.tensor_tensor(total, stats[:, :, 1], stats[:, :, 4], ALU.add)
    dve.tensor_tensor(diff, stats[:, :, 1], stats[:, :, 4], ALU.subtract)
    chain.done(dve.tensor_tensor(m2, stats[:, :, 2], stats[:, :, 5], ALU.add))
    chain.wait()
    dve.tensor_scalar_mul(mv[:, :, 0], total, 0.5)
    dve.tensor_scalar(m2, m2, 1.0 / D, EPS, ALU.mult, ALU.add)
    chain.done(dve.scalar_tensor_tensor(diff, diff, 0.25, diff, op0=ALU.mult, op1=ALU.mult))
    chain.wait()
    return dve.tensor_tensor(mv[:, :, 1], m2, diff, ALU.add)


def inverse_root(chain, rstd, std, var, y):
    dve = chain.eng
    r = rstd[:, :]
    for op in (lambda: dve.reciprocal(r, std[:, :]),
               lambda: dve.tensor_tensor(y, r, r, ALU.mult),
               lambda: dve.tensor_tensor(y, y, var, ALU.mult),
               lambda: dve.tensor_scalar(y, y, -0.5, 1.5, ALU.mult, ALU.add),
               lambda: dve.tensor_tensor(r, r, y, ALU.mult)):
        chain.done(op())
        chain.wait()


def stage_modulation(nc, cT, wmod, mod_dram, h2_dram, info_dram, out):
    with ExitStack() as ctx:
        s = Scope(nc, ctx, "mod_", credit=0)
        c_sb = s.sb("c", [P, DK, NB], FP32)
        sig = s.sb("sig", [P, DK, NB], FP32)
        silu = s.sb("silu", [P, DK, NB], FP32)
        w_sb = s.sb("w", [P, DK, 6 * D], FP32)
        res = s.sb("res", [NB, 6, D], FP32)
        sign = s.sb("sign", [NB, 2, D], FP32)
        mag = s.sb("mag", [NB, 2, D], FP32)
        ps = [s.ps(f"ps{j}", (NB, D)) for j in range(6)]
        SP_TILES = SLOTS // P
        zero = s.sb("zero", [P, D], FP32)
        pad_i = s.sb("pad_i", [P, SP_TILES], I32)
        info = s.sb("info", [P, SP_TILES, 2], FP32)
        pool_own, info_done = s.sem("pool_own"), s.sem("info")
        loaded, sig_done, silu_done = s.sem("loaded"), s.sem("sig"), s.sem("silu")
        mm, own, ready, stored = s.sem("mm"), s.sem("own"), s.sem("ready"), s.sem("stored")
        gates = (M_GA, M_GB)
        ORDER = gates + (M_SA, M_CA, M_SB, M_CB)
        w_in = s.sems("w_in", 2)
        block = ctx.enter_context(nc.Block())

        @block.sync
        def _(sp):
            sp.dma_start(c_sb[:, :, :], cT.rearrange("(k p) b -> p k b", p=P)).then_inc(loaded.sem, 16)
            for n, j in enumerate(ORDER):
                cols = slice(j * D, (j + 1) * D)
                sp.dma_start(w_sb[:, :, cols], wmod[:, cols].rearrange("(k p) n -> p k n", p=P)).then_inc(w_in[n >= 2].sem, 16)
            info_done.wait(sp, 1)
            for r in range(CAP // P):
                sp.dma_start(h2_dram[T + r * P:T + (r + 1) * P, :], zero[:, :]).then_inc(stored.sem, 16)
                sp.dma_start(out[T + r * P:T + (r + 1) * P, :], zero[:, :]).then_inc(stored.sem, 16)
            sp.dma_start(info_dram.rearrange("(n p) c -> p n c", p=P), info[:, :, :]).then_inc(stored.sem, 16)
            sp.dma_start(mod_dram[NB:NB + 1, :, :].rearrange("b j d -> (b j) d"), zero[0:6, :]).then_inc(stored.sem, 16)
            ready.wait(sp, 1)
            sp.dma_start(mod_dram[0:NB, :, :], res[:, :, :]).then_inc(stored.sem, 16)
            stored.wait(sp, 16 * (2 * CAP // P + 3))

        @block.gpsimd
        def _(pool):
            pool.memset(zero[:, :], 0.0)
            pool.memset(info[:, :, :], 0.0)
            pool.iota(pad_i[:, :], pattern=[[0, NE], [P, CAP // P]], base=T, channel_multiplier=1).then_inc(pool_own.sem, 1)
            pool_own.wait(pool, 1)
            pool.tensor_copy(info[:, :, 0], pad_i[:, :]).then_inc(info_done.sem, 1)

        @block.scalar
        def _(act):
            loaded.wait(act, 16)
            act.activation(sig[:, :, :], c_sb[:, :, :], ACT.Sigmoid).then_inc(sig_done.sem, 1)

        @block.tensor
        def _(pe):
            silu_done.wait(pe, 1)
            for n, j in enumerate(ORDER):
                w_in[n >= 2].wait(pe, 64 if n >= 2 else 32)
                for k in range(DK):
                    last = pe.matmul(ps[j][:, :], silu[:, k, :], w_sb[:, k, j * D:(j + 1) * D],
                                     start=k == 0, stop=k == DK - 1)
                last.then_inc(mm.sem, 1)

        @block.vector
        def _(dve):
            chain = Chain(dve, own, 0)
            sig_done.wait(dve, 1)
            dve.tensor_tensor(silu[:, :, :], c_sb[:, :, :], sig[:, :, :], ALU.mult).then_inc(silu_done.sem, 1)
            for n, j in enumerate(gates):
                mm.wait(dve, n + 1)
                last = dve.tensor_copy(res[:, j, :], ps[j][:, :])
            chain.done(last)
            chain.wait()
            for n, j in enumerate(gates):
                dve.tensor_scalar(sign[:, n, :], res[:, j, :], 0.0, 2.0, ALU.is_ge, ALU.mult)
                last = dve.tensor_scalar(mag[:, n, :], res[:, j, :], -1.0, 0.25, ALU.mult, ALU.max)
            chain.done(last)
            chain.wait()
            for n, j in enumerate(gates):
                last = dve.tensor_tensor(mag[:, n, :], mag[:, n, :], res[:, j, :], ALU.max)
            chain.done(last)
            chain.wait()
            for n, j in enumerate(gates):
                dve.scalar_tensor_tensor(res[:, j, :], sign[:, n, :], -1.0, mag[:, n, :], op0=ALU.add, op1=ALU.mult)
            for n, j in enumerate(ORDER[2:]):
                mm.wait(dve, n + 3)
                if j in (M_CA, M_CB):
                    last = dve.tensor_scalar_add(res[:, j, :], ps[j][:, :], 1.0)
                else:
                    last = dve.tensor_copy(res[:, j, :], ps[j][:, :])
            last.then_inc(ready.sem, 1)


def make_identity(pool, tile, own, n):
    pool.memset(tile[:, :], 0.0).then_inc(own.sem, 1)
    own.wait(pool, n + 1)
    pool.affine_select(out=tile[:, :], in_=tile[:, :], compare_op=ALU.not_equal, fill=1.0, base=0,
                       pattern=[[-1, tile.shape[1]]], channel_multiplier=1).then_inc(own.sem, 1)
    return n + 2


def stage_qkv(nc, x, wqkvT, bqk, bv, mod_dram, qk_dram, v_dram):
    with ExitStack() as ctx:
        s = Scope(nc, ctx, "qkv_")
        x_sb = [s.sb(f"x{p}", [P, UT, D], FP32) for p in range(2)]
        wraw = [s.sb(f"wraw{j}", [P, DK, D], FP32) for j in range(3)]
        w_hi = [s.sb(f"w_hi{j}", [P, DK, D], F32R) for j in range(3)]
        w_lo = [s.sb(f"w_lo{j}", [P, DK, D], F32R) for j in range(3)]
        hT_hi = [s.sb(f"hT_hi{p}", [P, DK, UNIT], F32R) for p in range(2)]
        hT_lo = [s.sb(f"hT_lo{p}", [P, DK, UNIT], F32R) for p in range(2)]
        mod = s.sb("mod", [P, 2, D], FP32)
        bqk_sb = s.sb("bqk", [P, 2 * NG], FP32)
        bv_sb = s.sb("bv", [P, D], FP32)
        ident = s.sb("ident", [P, P], FP32)
        stats = s.sb("stats", [P, UT, 6], FP32)
        mv = s.sb("mv", [P, UT, 2], FP32)
        std = s.sb("std", [P, UT], FP32)
        rstd = s.sb("rstd", [P, UT], FP32)
        tmp = s.sb("tmp", [P, UT, 3], FP32)
        RING, BANKS = 4, 6
        out_hi = [s.sb(f"out_hi{n}", [P, UNIT], F32R) for n in range(RING)]
        out_lo = [s.sb(f"out_lo{n}", [P, UNIT], F32R) for n in range(RING)]
        out_v = [s.sb(f"out_v{n}", [P, D], FP32) for n in range(UT)]
        ps_t = [s.ps(f"ps_t{n}") for n in range(2)]
        ps_m = [s.ps(f"ps_m{n}") for n in range(BANKS)]

        w_in, w_hi_done, w_lo_done = s.sems("w_in", 3), s.sem("w_hi_done"), s.sem("w_lo_done")
        consts, pool_own, dve_own = s.sem("consts"), s.sem("pool_own"), s.sem("dve_own")
        x_in, mod_in = s.sems("x_in", 2), s.sem("mod_in")
        var_done, std_done, norm_done, h_done = s.sem("var"), s.sem("std"), s.sem("norm"), s.sem("h")
        mul_done = s.sem("mul")
        tr_done, hi_done, lo_done = s.sem("tr"), s.sem("hi"), s.sem("lo")
        mm_done, ehi_done, elo_done, ev_done = s.sem("mm"), s.sem("ehi"), s.sem("elo"), s.sem("ev")
        qk_out, v_out = s.sems("qk_out", RING), s.sems("v_out", UT)
        NQK = 2 * NG
        NM = NQK + UT
        block = ctx.enter_context(nc.Block())
        LAST = NB - 1

        def steps(eng, body):
            with eng.Fori(0, LAST) as b:
                for half in range(HALVES):
                    body(b, half, True)
            for half in range(HALVES):
                body(LAST, half, half + 1 < HALVES)

        @block.sync
        def _(sp):
            s.give_credit(sp)
            def load_x(b, half):
                src = x[bass.ds(b, 1), half * UNIT:(half + 1) * UNIT, :]
                sp.dma_start(x_sb[half][:, :, :], src.rearrange("o (t p) d -> p (o t) d", p=P)).then_inc(x_in[half].sem, 16)

            def load_mod(b):
                for m, j in enumerate((M_SA, M_CA)):
                    sp.dma_start(mod[:, m, :], mod_dram[bass.ds(b, 1), j, :].broadcast_to([P, D])).then_inc(mod_in.sem, 16)

            load_x(0, 0)
            load_mod(0)
            for j in range(3):
                sp.dma_start(wraw[j][:, :, :], wqkvT[j].rearrange("(k p) n -> p k n", p=P)).then_inc(w_in[j].sem, 16)
            sp.dma_start(bqk_sb[:, :], bqk[:, :]).then_inc(consts.sem, 16)
            sp.dma_start(bv_sb[:, :], bv[:, :].broadcast_to([P, D])).then_inc(consts.sem, 16)
            load_x(0, 1)

            def body(b, half, more):
                u = b * HALVES + half
                if more or half == 0:
                    if not isinstance(b, int) or b < LAST:
                        tr_done.wait(sp, DK * (u + 1))
                        load_x(b + 1, half)
                        if half == 0:
                            h_done.wait(sp, UT * (u + 2))
                            load_mod(b + 1)
                for n in range(NQK):
                    elo_done.wait(sp, NQK * u + n + 1)
                    which, g = (QHI, n) if n < NG else (KHI, n - NG)
                    for part, tile in ((0, out_hi), (1, out_lo)):
                        dst = qk_dram[which + part, bass.ds(b * NG + g, 1), :, half * UNIT:(half + 1) * UNIT]
                        sp.dma_start(dst.rearrange("o p t -> (o p) t"), raw(tile[n % RING][:, :])).then_inc(qk_out[n % RING].sem, 16)
                for t in range(UT):
                    ev_done.wait(sp, UT * u + t + 1)
                    tok = half * UNIT + t * P
                    dst = v_dram[bass.ds(b * NG, NG), tok:tok + P, :]
                    sp.dma_start(dst.rearrange("g t j -> t g j"),
                                 out_v[t][:, :].rearrange("p (g j) -> p g j", g=NG)).then_inc(v_out[t].sem, 16)

            steps(sp, body)
            units = NB * HALVES
            for n in range(RING):
                qk_out[n].wait(sp, 32 * (NQK // RING) * units)
            for t in range(UT):
                v_out[t].wait(sp, 16 * units)

        @block.gpsimd
        def _(pool):
            make_identity(pool, ident, pool_own, 0)

            def modulate(u, half, b):
                mod_in.wait(pool, 32 * (b + 1))
                for t in range(UT):
                    norm_done.wait(pool, UT * u + t + 1)
                    xt = x_sb[half][:, t, :]
                    pool.tensor_tensor(xt, xt, mod[:, 1, :], ALU.mult).then_inc(mul_done.sem, 1)
                    mul_done.wait(pool, UT * u + t + 1)
                    pool.tensor_tensor(xt, xt, mod[:, 0, :], ALU.add).then_inc(h_done.sem, 1)

            modulate(0, 0, 0)

            def body(b, half, more):
                if more:
                    u = b * HALVES + half
                    modulate(u + 1, 1 - half, b + half)

            steps(pool, body)

        @block.scalar
        def _(act):
            def high_weights(j):
                w_in[j].wait(act, 16)
                act.activation(w_hi[j][:, :, :], wraw[j][:, :, :], ACT.Copy).then_inc(w_hi_done.sem, 1)


            def root(u):
                var_done.wait(act, u + 1)
                act.activation(std[:, :], mv[:, :, 1], ACT.Sqrt).then_inc(std_done.sem, 1)

            def turn(u, half):
                for k in range(DK):
                    tr_done.wait(act, DK * u + k + 1)
                    act.activation(hT_hi[half][:, k, :], ps_t[k % 2][:, :], ACT.Copy).then_inc(hi_done.sem, 1)

            root(0)
            for j in range(3):
                high_weights(j)
            turn(0, 0)
            consts.wait(act, 32)

            def body(b, half, more):
                u = b * HALVES + half
                if more:
                    root(u + 1)
                for n in range(NQK):
                    mm_done.wait(act, NM * u + n + 1)
                    use = (NQK // RING) * u + n // RING
                    qk_out[n % RING].wait(act, 32 * use)
                    act.activation(out_hi[n % RING][:, :], ps_m[n % BANKS][:, :], ACT.Identity,
                                   bias=bqk_sb[:, n:n + 1]).then_inc(ehi_done.sem, 1)
                if more:
                    turn(u + 1, 1 - half)

            steps(act, body)

        @block.vector
        def _(dve):
            LINKS = 1 + STAT_LINKS + ROOT_LINKS

            def layernorm(u, half, b):
                chain = Chain(dve, dve_own, LINKS * u)
                x_in[half].wait(dve, 16 * (b + 1))
                for t in range(UT):
                    last = dve.bn_stats(stats[:, t, :], x_sb[half][:, t, :])
                chain.done(last)
                chain.wait()
                combine_stats(chain, stats, mv, tmp).then_inc(var_done.sem, 1)
                std_done.wait(dve, u + 1)
                var_done.wait(dve, u + 1)
                inverse_root(chain, rstd, std, mv[:, :, 1], tmp[:, :, 0])
                assert chain.n == LINKS
                for t in range(UT):
                    dve.tensor_scalar(x_sb[half][:, t, :], x_sb[half][:, t, :], mv[:, t, 0:1], rstd[:, t:t + 1],
                                      ALU.subtract, ALU.mult).then_inc(norm_done.sem, 1)

            def low_turned(u, half, k):
                hi_done.wait(dve, DK * u + k + 1)
                dve.tensor_tensor(hT_lo[half][:, k, :], ps_t[k % 2][:, :], raw(hT_hi[half][:, k, :]),
                                  ALU.subtract).then_inc(lo_done.sem, 1)

            layernorm(0, 0, 0)
            for j in range(3):
                w_hi_done.wait(dve, j + 1)
                dve.tensor_tensor(w_lo[j][:, :, :], wraw[j][:, :, :], raw(w_hi[j][:, :, :]), ALU.subtract).then_inc(w_lo_done.sem, 1)
            for k in range(DK):
                low_turned(0, 0, k)
            consts.wait(dve, 32)

            def body(b, half, more):
                u = b * HALVES + half
                if more:
                    layernorm(u + 1, 1 - half, b + half)
                for n in range(NQK):
                    ehi_done.wait(dve, NQK * u + n + 1)
                    dve.scalar_tensor_tensor(out_lo[n % RING][:, :], ps_m[n % BANKS][:, :], bqk_sb[:, n:n + 1],
                                             raw(out_hi[n % RING][:, :]), op0=ALU.add, op1=ALU.subtract).then_inc(elo_done.sem, 1)
                for t in range(UT):
                    if more:
                        low_turned(u + 1, 1 - half, t)
                    mm_done.wait(dve, NM * u + NQK + t + 1)
                    v_out[t].wait(dve, 16 * u)
                    dve.tensor_tensor(out_v[t][:, :], ps_m[(NQK + t) % BANKS][:, :], bv_sb[:, :], ALU.add).then_inc(ev_done.sem, 1)

            steps(dve, body)

        @block.tensor
        def _(pe):
            pool_own.wait(pe, 2)

            def turn(u, half, k):
                h_done.wait(pe, UT * (u + 1))
                lo_done.wait(pe, DK * u + k - 1)
                for t in range(UT):
                    last = pe.transpose(ps_t[k % 2][:, t * P:(t + 1) * P], x_sb[half][:, t, k * P:(k + 1) * P], ident[:, :])
                last.then_inc(tr_done.sem, 1)

            for k in range(DK):
                turn(0, 0, k)
            w_lo_done.wait(pe, 3)

            def body(b, half, more):
                u = b * HALVES + half
                lo_done.wait(pe, DK * (u + 1))
                for n in range(NM):
                    if n < BANKS:
                        if n < BANKS - UT:
                            elo_done.wait(pe, NQK * u - (BANKS - UT) + n + 1)
                        else:
                            ev_done.wait(pe, UT * u - UT + (n - (BANKS - UT)) + 1)
                    else:
                        elo_done.wait(pe, NQK * u + n - BANKS + 1)
                    for k in range(DK):
                        for a, c in ((0, 0), (0, 1), (1, 0)):
                            h_part = (hT_hi, hT_lo)[a][half]
                            if n < NQK:
                                w_part = (w_hi, w_lo)[c][n // NG]
                                last = pe.matmul(ps_m[n % BANKS][:, :], w_part[:, k, (n % NG) * P:(n % NG + 1) * P],
                                                 h_part[:, k, :], start=k == 0 and a + c == 0, stop=k == DK - 1 and a == 1)
                            else:
                                t = n - NQK
                                last = pe.matmul(ps_m[n % BANKS][:, :], h_part[:, k, t * P:(t + 1) * P],
                                                 (w_hi, w_lo)[c][2][:, k, :], start=k == 0 and a + c == 0, stop=k == DK - 1 and a == 1)
                    last.then_inc(mm_done.sem, 1)
                    if more and NM - 1 > n >= NQK - 1:
                        turn(u + 1, 1 - half, n - (NQK - 1))

            steps(pe, body)


def stage_attention(nc, qk_dram, v_dram, o_dram):
    STACK = 3 * HD
    ROWS = STACK + 2
    KT = S // P
    QH = S // UNIT
    GROUPS = NB * NG
    SLOT = 3
    NPT = 2 * GH
    with ExitStack() as ctx:
        s = Scope(nc, ctx, "att_")
        qs = [s.sb(f"qs{i}", [ROWS, GH, S], F32R) for i in range(SLOT)]
        ks = [s.sb(f"ks{i}", [ROWS, GH, S], F32R) for i in range(SLOT)]
        vs = [s.sb(f"vs{i}", [P, KT, P], FP32) for i in range(SLOT)]
        pt = [s.sb(f"pt{i}", [P, UNIT], FP32) for i in range(NPT)]
        total_sb = [s.sb(f"total{i}", [P, UNIT], FP32) for i in range(QH)]
        rec = [s.sb(f"rec{i}", [P, UNIT], FP32) for i in range(QH)]
        o32 = [s.sb(f"o32_{i}", [P, UNIT], FP32) for i in range(QH)]
        oT_hi = [s.sb(f"oT_hi{i}", [P, UNIT], F32R) for i in range(QH)]
        oT_lo = [s.sb(f"oT_lo{i}", [P, UNIT], F32R) for i in range(QH)]
        rowmax = s.sb("rowmax", [P, GH * KT], FP32)
        m_hi = s.sb("m_hi", [GH * KT, P], F32R)
        m_lo = s.sb("m_lo", [GH * KT, P], F32R)
        ones = s.sb("ones", [P, HD], FP32)
        ident = s.sb("ident", [P, P], FP32)
        ident16 = s.sb("ident16", [P, P], BF16)
        mask_q = s.sb("mask_q", [P, P], BF16)
        mask_k = s.sb("mask_k", [P, P], BF16)
        ps_s = [s.ps(f"ps_s{i}", (P, 2 * 512)) for i in range(2)]
        ps_p = [s.ps(f"ps_p{i}") for i in range(2)]
        ps_o, ps_sum = s.ps("ps_o"), s.ps("ps_sum")

        q_in, v_in, m_in = s.sems("q_in", SLOT), s.sems("v_in", SLOT), s.sems("m_in", SLOT)
        pool_own, consts, ln_done, rec_done, mark = (s.sem(n) for n in ("pool_own", "consts", "ln", "rec", "mark"))
        s_done, max_done = s.sem("s"), s.sem("max")
        mt_done, mhi_done, mlo_done = s.sem("mt"), s.sem("mhi"), s.sem("mlo")
        p_done, exp_done, pv_done = s.sem("p"), s.sem("exp"), s.sem("pv")
        o_free, ohi_done, olo_done = s.sem("o_free"), s.sem("ohi"), s.sem("olo")
        own_sem, t_free = s.sem("pool_links"), s.sem("t_free")
        o_out = s.sems("o_out", QH)
        block = ctx.enter_context(nc.Block())

        order1 = [(h, t) for a in range(KT // 2) for h in range(GH) for t in (KT - 1 - a, a)]
        HT = UNIT // P
        chunks = [(qh, kt) for qh in range(QH) for kt in
                  [0] + list(range(qh * HT + 1, (qh + 1) * HT)) + ([qh * HT] if qh else []) + list(range(1, qh * HT))]
        ENDS = [c for c in range(len(chunks)) if c + 1 == len(chunks) or chunks[c + 1][0] != chunks[c][0]]
        N1, NC = len(order1), len(chunks)
        NP = NC * GH
        TILES = [2, 3, 4, 4, 2, 3, 4, 4, 3, 3, 0, 0]
        TURN = NC - 2
        assert sorted(chunks) == [(qh, kt) for qh in range(QH) for kt in range((qh + 1) * HT)]
        assert sum(TILES) == N1 and not any(TILES[TURN:]) and len(TILES) == NC
        share = [sum(TILES[:c]) + -(-TILES[c] * h // GH) for c in range(NC) for h in range(GH)] + [N1]

        def after(c, h):
            return share[c * GH + h], share[c * GH + h + 1]

        class Group:
            def __init__(self, g, slot, use):
                self.g, self.slot, self.use = g, slot, use

            def ahead(self, n):
                slot = self.slot + n
                return Group(self.g + n, slot % SLOT, self.use + slot // SLOT)

        def steps(step):
            LOOPS = (GROUPS - 3) // SLOT - 1

            def run(eng):
                first = Group(0, 0, 0)
                step(first, None)
                step(first.ahead(1), first)
                with eng.Fori(0, LOOPS) as i:
                    for j in range(SLOT):
                        prev = Group(i * SLOT, 0, i).ahead(j + 1)
                        step(prev.ahead(1), prev)
                for g in range(LOOPS * SLOT + 1, GROUPS):
                    prev = first.ahead(g)
                    step(prev.ahead(1) if g + 1 < GROUPS else None, prev)
            return run

        def older(prev):
            if isinstance(prev.g, int) and prev.g == 0:
                return None
            return Group(prev.g - 1, (prev.slot - 1) % SLOT, None)

        @block.sync
        def _(sp):
            s.give_credit(sp)
            def load(G):
                for tile, parts in ((qs, (QHI, QHI, QLO)), (ks, (KHI, KLO, KHI))):
                    for r, part in enumerate(parts):
                        src = qk_dram[part, bass.ds(G.g, 1), :, :].rearrange("o (h d) t -> d (o h) t", d=HD)
                        sp.dma_start(raw(tile[G.slot][r * HD:(r + 1) * HD, :, :]), src).then_inc(q_in[G.slot].sem, 16)
                src = v_dram[bass.ds(G.g, 1), :, :].rearrange("o (k p) j -> p (o k) j", p=P)
                sp.dma_start(vs[G.slot][:, :, :], src).then_inc(v_in[G.slot].sem, 16)

            def store(group, qh):
                olo_done.wait(sp, QH * group.g + qh + 1)
                for part, tile in ((0, oT_hi), (1, oT_lo)):
                    dst = o_dram[part, bass.ds(group.g, 1), :, qh * UNIT:(qh + 1) * UNIT]
                    sp.dma_start(dst.rearrange("o p t -> (o p) t"), raw(tile[qh][:, :])).then_inc(o_out[qh].sem, 16)

            def step(cur, prev):
                if prev and cur and (not isinstance(cur.g, int) or cur.g + 1 < GROUPS):
                    if older(prev):
                        pv_done.wait(sp, NC * prev.g)
                        load(cur.ahead(1))
                    else:
                        load(cur.ahead(1))
                if prev and older(prev):
                    store(older(prev), QH - 1)
                if prev:
                    for qh in range(QH - 1):
                        store(prev, qh)
                if cur:
                    mlo_done.wait(sp, cur.g + 1)
                    for row, part in ((STACK, m_hi), (STACK + 1, m_lo)):
                        sp.dma_start(raw(qs[cur.slot][row:row + 1, :, :]).rearrange("o h (q t) -> o (h q) t", q=KT),
                                     raw(part[:, :])).then_inc(m_in[cur.slot].sem, 16)

            load(Group(0, 0, 0))
            load(Group(1, 1, 0))
            steps(step)(sp)
            store(Group(GROUPS - 1, None, None), QH - 1)
            for qh in range(QH):
                o_out[qh].wait(sp, 32 * GROUPS)

        @block.gpsimd
        def _(pool):
            n = make_identity(pool, ident, pool_own, 0)
            n = make_identity(pool, ident16, pool_own, n)
            pool.memset(mask_q[:, :], 0.0).then_inc(pool_own.sem, 1)
            pool.memset(mask_k[:, :], 0.0).then_inc(pool_own.sem, 1)
            pool.memset(ones[:, :], 1.0).then_inc(pool_own.sem, 1)
            pool_own.wait(pool, n + 3)
            pool.affine_select(out=mask_q[:, :], in_=mask_q[:, :], compare_op=ALU.is_ge, fill=MASKED, base=0,
                               pattern=[[-1, P]], channel_multiplier=1).then_inc(pool_own.sem, 1)
            pool.affine_select(out=mask_k[:, :], in_=mask_k[:, :], compare_op=ALU.is_ge, fill=MASKED, base=0,
                               pattern=[[1, P]], channel_multiplier=-1).then_inc(pool_own.sem, 1)
            for i in range(SLOT):
                pool_own.wait(pool, n + 5 + i)
                pool.memset(raw(ks[i][STACK:ROWS, :, :]), 1.0).then_inc(pool_own.sem, 1)
            pool_own.wait(pool, n + 5 + SLOT)
            pool.sem_inc(consts.sem, 1)
            LINKS = 3

            def step(cur, prev):
                if prev:
                    for qh in range(QH):
                        n = QH * prev.g + qh + 1
                        o_free.wait(pool, n)
                        pool.sem_inc(mark.sem, 1)
                        rec_done.wait(pool, n)
                        pool.tensor_tensor(total_sb[qh][:, :], total_sb[qh][:, :], rec[qh][:, :], ALU.mult)
                        pool.tensor_tensor(o32[qh][:, :], o32[qh][:, :], rec[qh][:, :], ALU.mult).then_inc(own_sem.sem, 1)
                        hold(pool, own_sem, LINKS * (n - 1) + 1, mark)
                        pool.tensor_scalar(total_sb[qh][:, :], total_sb[qh][:, :], -1.0, 2.0, ALU.mult, ALU.add).then_inc(own_sem.sem, 1)
                        own_sem.wait(pool, LINKS * (n - 1) + 2)
                        pool.tensor_tensor(o32[qh][:, :], o32[qh][:, :], total_sb[qh][:, :], ALU.mult).then_inc(own_sem.sem, 1)
                        o_out[qh].wait(pool, 32 * prev.g)
                        pool.sem_inc(mark.sem, 1)
                        hold(pool, own_sem, LINKS * (n - 1) + 3, mark)
                        pool.tensor_copy(oT_hi[qh][:, :], o32[qh][:, :]).then_inc(ohi_done.sem, 1)
                        ohi_done.wait(pool, n)
                        pool.tensor_tensor(oT_lo[qh][:, :], o32[qh][:, :], raw(oT_hi[qh][:, :]),
                                           ALU.subtract).then_inc(olo_done.sem, 1)

            steps(step)(pool)

        @block.scalar
        def _(act):
            act.preload_act_table_set("natural_log_exp_and_others")

            def take(group, qh, c):
                pv_done.wait(act, NC * group.g + c + 1)
                olo_done.wait(act, QH * group.g + qh - 1)
                act.activation(total_sb[qh][:, :], ps_sum[:, :], ACT.Copy).then_inc(t_free.sem, 1)

            def invert(group, qh, c):
                n = QH * group.g + qh + 1
                t_free.wait(act, n)
                act.activation(rec[qh][:, :], total_sb[qh][:, :], ACT.Ln).then_inc(ln_done.sem, 1)
                ln_done.wait(act, n)
                act.activation(rec[qh][:, :], rec[qh][:, :], ACT.Exp, scale=-1.0).then_inc(rec_done.sem, 1)


            def step(cur, prev):
                if not prev:
                    return

                def finish(c, h):
                    for back, at in ((1, GH - 1), (2, 1)):
                        e = (c - back) % NC
                        group = prev if c >= back else older(prev)
                        if h == at and e in ENDS and group:
                            (take if back == 1 else invert)(group, chunks[e][0], e)

                for c, (qh, kt) in enumerate(chunks):
                    col = max(kt * P - qh * UNIT, 0)
                    for h in range(GH):
                        n = c * GH + h
                        if h == 0:
                            pv_done.wait(act, NC * prev.g + c - 1)
                        p_done.wait(act, NP * prev.g + n + 1)
                        act.activation(pt[n % NPT][:, col:UNIT], ps_p[n % 2][:, col:UNIT], ACT.Exp,
                                       scale=float(HD) ** -0.5).then_inc(exp_done.sem, 1)
                        finish(c, h)

            steps(step)(act)
            last = Group(GROUPS - 1, None, None)
            take(last, QH - 1, NC - 1)
            invert(last, QH - 1, NC - 1)

        @block.vector
        def _(dve):

            def take(group, qh, c):
                pv_done.wait(dve, NC * group.g + c + 1)
                olo_done.wait(dve, QH * group.g + qh - 1)
                dve.tensor_copy(o32[qh][:, :], ps_o[:, :]).then_inc(o_free.sem, 1)

            def step(cur, prev):
                def maxima(lo, hi):
                    for i in range(lo, hi):
                        h, t = order1[i]
                        s_done.wait(dve, N1 * cur.g + i + 1)
                        dve.reduce_max(rowmax[:, h * KT + t:h * KT + t + 1], ps_s[i % 2][:, 0:(t + 1) * P],
                                       axis=AX.X).then_inc(max_done.sem, 1)

                def negate():
                    mt_done.wait(dve, cur.g + 1)
                    if prev:
                        m_in[prev.slot].wait(dve, 32 * (prev.use + 1))
                    top = ps_s[0][0:GH * KT, 0:P]
                    dve.tensor_scalar_mul(m_hi[:, :], top, -1.0).then_inc(mhi_done.sem, 1)
                    mhi_done.wait(dve, cur.g + 1)
                    dve.scalar_tensor_tensor(m_lo[:, :], top, -1.0, raw(m_hi[:, :]),
                                             op0=ALU.mult, op1=ALU.subtract).then_inc(mlo_done.sem, 1)

                if not prev:
                    maxima(0, N1)
                    negate()
                    return
                for c in range(NC):
                    if cur:
                        maxima(share[c * GH], share[c * GH + GH])
                        if c == TURN:
                            negate()
                    e = (c - 1) % NC
                    group = prev if c else older(prev)
                    if e in ENDS and group:
                        take(group, chunks[e][0], e)

            steps(step)(dve)
            take(Group(GROUPS - 1, None, None), QH - 1, NC - 1)

        @block.tensor
        def _(pe):
            consts.wait(pe, 1)

            def step(cur, prev):
                def scores(lo, hi):
                    for i in range(lo, hi):
                        h, t = order1[i]
                        max_done.wait(pe, N1 * cur.g + i - 1)
                        if i == 0 and prev:
                            mlo_done.wait(pe, cur.g)
                        top, bank = (t + 1) * P, ps_s[i % 2]
                        for c0 in range(0, top, 512):
                            c1 = min(c0 + 512, top)
                            pe.matmul(bank[:, c0:c1], qs[cur.slot][0:STACK, h, t * P:top],
                                      ks[cur.slot][0:STACK, h, c0:c1], start=True, stop=c1 < top)
                        pe.matmul(bank[:, t * P:top], ident16[:, :], mask_q[:, :], start=False, stop=True).then_inc(s_done.sem, 1)

                def accumulate(c, acc, lhs):
                    qh, kt = chunks[c]
                    col = max(kt * P - qh * UNIT, 0)
                    for h in range(GH):
                        last = pe.matmul(acc[h * HD:(h + 1) * HD, col:UNIT], lhs(h), pt[(c * GH + h) % NPT][:, col:UNIT],
                                         start=kt == 0, stop=c in ENDS)
                    return last

                def weigh(group, c):
                    qh, kt = chunks[c]
                    if kt == 0:
                        o_free.wait(pe, QH * group.g + qh)
                    exp_done.wait(pe, NP * group.g + (c + 1) * GH)
                    accumulate(c, ps_o, lambda h: vs[group.slot][:, kt, h * HD:(h + 1) * HD])

                def total(group, c):
                    qh, kt = chunks[c]
                    if kt == 0:
                        t_free.wait(pe, QH * group.g + qh)
                    accumulate(c, ps_sum, lambda h: ones[:, :]).then_inc(pv_done.sem, 1)

                def turn():
                    max_done.wait(pe, N1 * (cur.g + 1))
                    pe.transpose(ps_s[0][0:GH * KT, 0:P], rowmax[:, :], ident[:, :]).then_inc(mt_done.sem, 1)

                if cur:
                    q_in[cur.slot].wait(pe, 96 * (cur.use + 1))
                if not prev:
                    scores(0, N1)
                    turn()
                    return
                for c, (qh, kt) in enumerate(chunks):
                    col = max(kt * P - qh * UNIT, 0)
                    q0 = qh * UNIT + col
                    diag = kt * P >= qh * UNIT
                    if cur and c == TURN:
                        turn()
                    if c == 0:
                        m_in[prev.slot].wait(pe, 32 * (prev.use + 1))
                        v_in[prev.slot].wait(pe, 16 * (prev.use + 1))
                    for h in range(GH):
                        n = c * GH + h
                        exp_done.wait(pe, NP * prev.g + n - 1)
                        last = pe.matmul(ps_p[n % 2][:, col:UNIT], ks[prev.slot][:, h, kt * P:(kt + 1) * P],
                                         qs[prev.slot][:, h, q0:(qh + 1) * UNIT], start=True, stop=not diag)
                        if diag:
                            last = pe.matmul(ps_p[n % 2][:, col:col + P], ident16[:, :], mask_k[:, :], start=False, stop=True)
                        last.then_inc(p_done.sem, 1)
                        if cur:
                            scores(*after(c, h))
                        group = prev if c else older(prev)
                        if group and h == 1:
                            weigh(group, (c - 1) % NC)
                        if group and h == 3:
                            total(group, (c - 1) % NC)
                if not cur:
                    weigh(prev, NC - 1)
                    total(prev, NC - 1)

            steps(step)(pe)


def stage_project_route_shared(nc, x, o_dram, mod_dram, woT, bo, gateT, bias, upT, downT, h2_dram, info_dram, out):
    UP = HS // P
    RING, RELU = 4, 2
    with ExitStack() as ctx:
        s = Scope(nc, ctx, "ffn_")
        wo_hi, wo_lo = s.sb("wo_hi", [P, DK, D], F32R), s.sb("wo_lo", [P, DK, D], F32R)
        up_hi, up_lo = s.sb("up_hi", [P, DK, HS], F32R), s.sb("up_lo", [P, DK, HS], F32R)
        dn_hi, dn_lo = s.sb("dn_hi", [P, UP, D], F32R), s.sb("dn_lo", [P, UP, D], F32R)
        gt_raw = s.sb("gt_raw", [P, DK * NE], FP32)
        gt_hi, gt_lo = s.sb("gt_hi", [P, DK, NE], F32R), s.sb("gt_lo", [P, DK, NE], F32R)
        o_hi, o_lo = s.sb("o_hi", [P, NG, UNIT], F32R), s.sb("o_lo", [P, NG, UNIT], F32R)
        x_sb = [s.sb(f"x{p}", [P, UT, D], FP32) for p in range(2)]
        h2 = s.sb("h2", [P, UT, D], FP32)
        hT_hi, hT_lo = s.sb("hT_hi", [P, DK, UNIT], F32R), s.sb("hT_lo", [P, DK, UNIT], F32R)
        a_hi, a_lo = s.sb("a_hi", [P, UP, UNIT], F32R), s.sb("a_lo", [P, UP, UNIT], F32R)
        relu = [s.sb(f"relu{n}", [P, UNIT], FP32) for n in range(RELU)]
        att = s.sb("att", [P, D], FP32)
        mod = s.sb("mod", [P, 3, D], FP32)
        gb = s.sb("gb", [P, D], FP32)
        bo_sb = s.sb("bo", [P, D], FP32)
        bias_sb = s.sb("bias", [P, NE], FP32)
        ident = s.sb("ident", [P, P], FP32)
        before = s.sb("before", [P, P], BF16)
        ones = s.sb("ones", [P, P], BF16)
        stats, tmp = s.sb("stats", [P, UT, 6], FP32), s.sb("tmp", [P, UT, 3], FP32)
        mv, std, rstd = s.sb("mv", [P, UT, 2], FP32), s.sb("std", [P, UT], FP32), s.sb("rstd", [P, UT], FP32)
        UG = UT * NGR
        score, biased = s.sb("score", [P, UT, NE], FP32), s.sb("biased", [P, UT, NE], FP32)
        masked = s.sb("masked", [P, UT, NE], FP32)
        pair_hi, pair_lo = s.sb("pair_hi", [P, UG, 2], FP32), s.sb("pair_lo", [P, UG, 2], FP32)
        grp = s.sb("grp", [P, 3, UG], FP32)
        ahead, ties = s.sb("ahead", [P, UG, NGR], FP32), s.sb("ties", [P, UG, NGR], FP32)
        earlier_i, earlier = s.sb("earlier_i", [P, NGR, NGR], I32), s.sb("earlier", [P, NGR, NGR], FP32)
        chosen = s.sb("chosen", [P, UG], I32)
        top, top_idx = s.sb("top", [P, UT, 8], FP32), s.sb("top_idx", [P, UT, 8], U32)
        expert = s.sb("expert", [P, UT, TOPK], FP32)
        iota_i, iota = s.sb("iota_i", [P, NE], I32), s.sb("iota", [P, NE], FP32)
        onehot, picked = s.sb("onehot", [P, UT, TOPK, NE], FP32), s.sb("picked", [P, UT, TOPK, NE], FP32)
        weight, den = s.sb("weight", [P, UT, TOPK], FP32), s.sb("den", [P, UT], FP32)
        sel, sel_acc = s.sb("sel", [P, UT, NE], BF16), s.sb("sel_acc", [P, NE], BF16)
        sel_sum = s.sb("sel_sum", [P, NE], FP32)
        place, over = s.sb("place", [P, UT, TOPK], FP32), s.sb("over", [P, UT, TOPK], FP32)
        tok_i, tok = s.sb("tok_i", [P, UT], I32), s.sb("tok", [P, UT], FP32)
        slot = [s.sb(f"slot{p}", [P, UT * TOPK], I32) for p in range(2)]
        info = [s.sb(f"info{p}", [P, UT * TOPK, 2], FP32) for p in range(2)]

        ps_t = [s.ps(f"ps_t{n}") for n in range(2)]
        ps_m = [s.ps(f"ps_m{n}") for n in range(RING)]
        ps_g, ps_pos = s.ps("ps_g"), s.ps("ps_pos")

        half_tiles = [t[:, n:n + 2, :].rearrange("p a b -> p (a b)") for t in (x_sb[1], h2) for n in (0, 2)]
        x_lower, x_upper, h_lower, h_upper = range(4)
        PLACES = (x_lower, x_upper, 4, h_lower, h_upper) + 3 * (x_lower, x_upper)
        wraw = half_tiles + [gt_raw[:, :]]
        w_in, w_hi_done, w_lo_done = s.sems("w_in", len(wraw)), s.sem("w_hi"), s.sem("w_lo")
        consts, pool_own, iotas, mark = s.sem("consts"), s.sem("pool_own"), s.sem("iotas"), s.sem("mark")
        o_in, x_in, mod_in, gb_in = s.sem("o_in"), s.sems("x_in", 2), s.sem("mod_in"), s.sem("gb_in")
        dve_own, var_done, std_done, norm_done = s.sem("dve_own"), s.sem("var"), s.sem("std"), s.sem("norm")
        mul_done, h_done = s.sem("mul"), s.sem("h")
        tr_done, hi_done, lo_done = s.sem("tr"), s.sem("hi"), s.sem("lo")
        gate_done, score_done, sel_done, pos_done = s.sem("gate"), s.sem("score"), s.sem("sel"), s.sem("pos")
        up_done, relu_done = s.sem("up"), s.sem("relu")
        sq_done, ahi_done, alo_done = s.sem("sq"), s.sem("ahi"), s.sem("alo")
        proj_done, att_done = s.sem("proj"), s.sem("att")
        chosen_done = s.sem("chosen")
        down_done, fin_done, out_done = s.sem("down"), s.sem("fin"), s.sem("out")
        slot_done, slot_free = s.sem("slot"), s.sem("slot_free")
        h2_out, x_out, scattered = s.sem("h2_out"), s.sems("x_out", 2), s.sems("scattered", 2, credit=0)
        block = ctx.enter_context(nc.Block())
        LAST = NB - 1
        CHOICE_STEPS = 4
        TURNS = ((), (0,), (1, 2, 3), ())

        def steps(eng, body):
            for half in range(HALVES):
                body(0, half, True)
            with eng.Fori(1, LAST) as b:
                for half in range(HALVES):
                    body(b, half, True)
            for half in range(HALVES):
                body(LAST, half, half + 1 < HALVES)

        def pieces_of(src, hi, lo, rows):
            src = src.rearrange("(k p) n -> p k n", p=P)
            return [tuple(t[:, k:k + rows, :] for t in (src, hi, lo)) for k in range(0, hi.shape[1], rows)]
        parts = [pieces_of(woT, wo_hi, wo_lo, 2), pieces_of(gateT, gt_hi, gt_lo, DK),
                 pieces_of(upT, up_hi, up_lo, 1), pieces_of(downT, dn_hi, dn_lo, 2)]
        pieces = sum(parts, [])
        NW, NW_UP, NW_H = len(pieces), sum(map(len, parts[:3])), 5

        def raw_piece(n):
            k, w = pieces[n][1].shape[1:]
            return wraw[PLACES[n]][:, 0:k * w].rearrange("p (a b) -> p a b", a=k)

        @block.sync
        def _(sp):
            s.give_credit(sp)
            def load_o(b, half):
                for part, tile in ((0, o_hi), (1, o_lo)):
                    src = o_dram[part, bass.ds(b * NG, NG), :, half * UNIT:(half + 1) * UNIT]
                    sp.dma_start(raw(tile[:, :, :]), src.rearrange("g p t -> p g t")).then_inc(o_in.sem, 16)

            def load_x(b, half):
                src = x[bass.ds(b, 1), half * UNIT:(half + 1) * UNIT, :]
                sp.dma_start(x_sb[half][:, :, :], src.rearrange("o (t p) d -> p (o t) d", p=P)).then_inc(x_in[half].sem, 16)

            def load_mod(b):
                for m, j in enumerate((M_GA, M_CB, M_SB)):
                    sp.dma_start(mod[:, m, :], mod_dram[bass.ds(b, 1), j, :].broadcast_to([P, D])).then_inc(mod_in.sem, 16)

            def load_gb(b):
                sp.dma_start(gb[:, :], mod_dram[bass.ds(b, 1), M_GB, :].broadcast_to([P, D])).then_inc(gb_in.sem, 16)

            def store_h2(b, half):
                u = b * HALVES + half
                h_done.wait(sp, UT * (u + 1))
                dst = h2_dram[bass.ds(u * UNIT, UNIT), :]
                sp.dma_start(dst.rearrange("(t p) d -> p t d", p=P), h2[:, :, :]).then_inc(h2_out.sem, 16)

            def load_w(n):
                before = [m for m in range(n) if PLACES[m] == PLACES[n]]
                if before:
                    w_lo_done.wait(sp, before[-1] + 1)
                sp.dma_start(raw_piece(n), pieces[n][0]).then_inc(w_in[PLACES[n]].sem, 16)

            for n in range(3):
                load_w(n)
            load_o(0, 0)
            load_x(0, 0)
            sp.dma_start(bo_sb[:, :], bo[:, :].broadcast_to([P, D])).then_inc(consts.sem, 16)
            sp.dma_start(bias_sb[:, :], bias[:, :].broadcast_to([P, NE])).then_inc(consts.sem, 16)
            load_mod(0)
            for n in range(3, NW):
                load_w(n)
            load_gb(0)
            w_lo_done.wait(sp, NW)
            load_x(0, 1)
            proj_done.wait(sp, UT)
            load_o(0, 1)
            store_h2(0, 0)

            def body(b, half, more):
                u = b * HALVES + half
                if more:
                    nb, nhalf = (b, 1) if half == 0 else (b + 1, 0)
                    if half == 0:
                        has_next2 = not (isinstance(b, int) and b == LAST)
                    else:
                        has_next2 = True
                    if has_next2:
                        proj_done.wait(sp, UT * (u + 2))
                        load_o(b + 1, half)
                    store_h2(nb, nhalf)
                    if half == 0 and has_next2:
                        load_mod(b + 1)
                if not more:
                    hold(sp, scattered[half], 16 * UT * TOPK * b, slot_free)
                out_done.wait(sp, UT * (u + 1))
                dst = out[bass.ds(u * UNIT, UNIT), :]
                sp.dma_start(dst.rearrange("(t p) d -> p t d", p=P), x_sb[half][:, :, :]).then_inc(x_out[half].sem, 16)
                if not (isinstance(b, int) and b == LAST):
                    x_out[half].wait(sp, 16 * (b + 1))
                    load_x(b + 1, half)
                    if half == 1:
                        load_gb(b + 1)
                if more and (not isinstance(b, int) or b):
                    hold(sp, scattered[half], 16 * UT * TOPK * b, slot_free)

            steps(sp, body)
            h2_out.wait(sp, 16 * NB * HALVES)
            for p in range(2):
                x_out[p].wait(sp, 16 * NB)
                scattered[p].wait(sp, 16 * UT * TOPK * NB)

        @block.gpsimd
        def _(pool):
            n = make_identity(pool, ident, pool_own, 0)
            pool.memset(ones[:, :], 1.0).then_inc(pool_own.sem, 1)
            pool.memset(before[:, :], 1.0).then_inc(pool_own.sem, 1)
            pool_own.wait(pool, n + 2)
            pool.affine_select(out=before[:, :], in_=before[:, :], compare_op=ALU.is_gt, fill=0.0, base=0,
                               pattern=[[1, P]], channel_multiplier=-1).then_inc(pool_own.sem, 1)
            pool.iota(earlier_i[:, :, :], pattern=[[1, NGR], [-1, NGR]], base=0, channel_multiplier=0)
            pool.iota(iota_i[:, :], pattern=[[1, NE]], base=0, channel_multiplier=0)
            pool.iota(tok_i[:, :], pattern=[[P, UT]], base=0, channel_multiplier=1).then_inc(iotas.sem, 1)

            def modulate(b, half):
                u = b * HALVES + half
                for t in range(UT):
                    norm_done.wait(pool, UT * u + t + 1)
                    ht = h2[:, t, :]
                    pool.tensor_tensor(ht, ht, mod[:, 1, :], ALU.mult).then_inc(mul_done.sem, 1)
                    mul_done.wait(pool, UT * u + t + 1)
                    pool.tensor_tensor(ht, ht, mod[:, 2, :], ALU.add).then_inc(h_done.sem, 1)

            modulate(0, 0)

            def body(b, half, more):
                u = b * HALVES + half
                if more:
                    modulate(*((b, 1) if half == 0 else (b + 1, 0)))
                if not isinstance(u, int) or u:
                    scatter(u - 1, 1 - half)

            def scatter(u, half):
                hold(pool, slot_done, u + 1, mark)
                for j in range(UT * TOPK):
                    pool.indirect_dma_start(
                        info_dram[:, :], bass.IndirectOffsetOnAxis(slot[half][:, j:j + 1].bitcast(U32), 0),
                        info[half][:, j, :], None, bounds_check=SLOTS - 1, oob_is_err=False).then_inc(scattered[half].sem, 16)

            steps(pool, body)
            scatter(NB * HALVES - 1, 1)

        @block.scalar
        def _(act):
            def high_weights(n0, n1):
                for n in range(n0, n1):
                    w_in[PLACES[n]].wait(act, 16 * PLACES[:n + 1].count(PLACES[n]))
                    act.activation(pieces[n][1], raw_piece(n), ACT.Copy).then_inc(w_hi_done.sem, 1)

            high_weights(0, NW_UP)

            def root(u):
                var_done.wait(act, u + 1)
                act.activation(std[:, :], mv[:, :, 1], ACT.Sqrt).then_inc(std_done.sem, 1)

            def turn(u):
                for t in range(UT):
                    tr_done.wait(act, UT * u + t + 1)
                    act.activation(hT_hi[:, :, t * P:(t + 1) * P], ps_t[t % 2][:, :].rearrange("p (k c) -> p k c", k=DK), ACT.Copy).then_inc(hi_done.sem, 1)

            root(0)
            turn(0)
            high_weights(NW_UP, NW)

            def body(b, half, more):
                u = b * HALVES + half
                down_done.wait(act, UT * u)

                def square(n):
                    relu_done.wait(act, UP * u + n + 1)
                    act.activation(relu[n % RELU][:, :], relu[n % RELU][:, :], ACT.Square).then_inc(sq_done.sem, 1)

                def high(n):
                    sq_done.wait(act, UP * u + n + 1)
                    act.activation(a_hi[:, n, :], relu[n % RELU][:, :], ACT.Copy).then_inc(ahi_done.sem, 1)

                for n in range(UP):
                    up_done.wait(act, UP * u + n + 1)
                    alo_done.wait(act, UP * u + n + 1 - RELU if n >= RELU else UP * u)
                    act.activation(relu[n % RELU][:, :], ps_m[n % RING][:, :], ACT.Relu).then_inc(relu_done.sem, 1)
                    if n:
                        high(n - 1)
                    square(n)
                high(UP - 1)
                gate_done.wait(act, u + 1)
                chosen_done.wait(act, u)
                act.activation(score[:, :, :].rearrange("p t e -> p (t e)"), ps_g[:, 0:UT * NE], ACT.Sigmoid).then_inc(score_done.sem, 1)
                if more:
                    root(u + 1)
                    turn(u + 1)

            steps(act, body)

        @block.vector
        def _(dve):
            iotas.wait(dve, 1)
            dve.tensor_single_scalar(earlier[:, :, :], earlier_i[:, :, :], 0, op=ALU.is_gt)
            dve.tensor_copy(iota[:, :], iota_i[:, :])
            dve.tensor_copy(tok[:, :], tok_i[:, :])
            dve.memset(sel_acc[:, :], 0.0)
            dve.memset(sel_sum[:, :], 0.0)
            def low_weights(n0, n1):
                for n in range(n0, n1):
                    w_hi_done.wait(dve, n + 1)
                    dve.tensor_tensor(pieces[n][2], raw_piece(n), raw(pieces[n][1]), ALU.subtract).then_inc(w_lo_done.sem, 1)

            low_weights(0, NW_H)
            consts.wait(dve, 32)
            LINKS = 2 * UT + 1 + STAT_LINKS + ROOT_LINKS

            def attend(b, half):
                u = b * HALVES + half
                chain = Chain(dve, dve_own, LINKS * u)
                xs = x_sb[half]
                x_in[half].wait(dve, 16 * (b + 1))
                mod_in.wait(dve, 48 * (b + 1))
                for t in range(UT):
                    proj_done.wait(dve, UT * u + t + 1)
                    dve.tensor_tensor(att[:, :], ps_m[t % RING][:, :], bo_sb[:, :], ALU.add).then_inc(att_done.sem, 1)
                    att_done.wait(dve, UT * u + t + 1)
                    chain.done(dve.tensor_tensor(att[:, :], att[:, :], mod[:, 0, :], ALU.mult))
                    chain.wait()
                    chain.done(dve.tensor_tensor(xs[:, t, :], xs[:, t, :], att[:, :], ALU.add))
                    chain.wait()
                    last = dve.bn_stats(stats[:, t, :], xs[:, t, :])
                chain.done(last)
                chain.wait()
                combine_stats(chain, stats, mv, tmp).then_inc(var_done.sem, 1)
                std_done.wait(dve, u + 1)
                var_done.wait(dve, u + 1)
                inverse_root(chain, rstd, std, mv[:, :, 1], tmp[:, :, 0])
                assert chain.n == LINKS
                tr_done.wait(dve, UT * u)
                h2_out.wait(dve, 16 * u)
                for t in range(UT):
                    dve.tensor_scalar(h2[:, t, :], xs[:, t, :], mv[:, t, 0:1], rstd[:, t:t + 1],
                                      ALU.subtract, ALU.mult).then_inc(norm_done.sem, 1)

            def groups(t):
                return t.rearrange("p (t g) -> p t g", t=UT)

            def choose(u):
                score_done.wait(dve, u + 1)
                dve.tensor_tensor(biased[:, :, :], score[:, :, :], bias_sb[:, :].unsqueeze(1).broadcast_to([P, UT, NE]), ALU.add)
                dve.drain()
                yield
                pairs = biased[:, :, :].rearrange("p t (g r) -> p (t g) r", r=EPG)
                dve.tensor_tensor(pair_hi[:, :, :], pairs[:, :, 0::2], pairs[:, :, 1::2], ALU.max)
                dve.tensor_tensor(pair_lo[:, :, :], pairs[:, :, 0::2], pairs[:, :, 1::2], ALU.min)
                dve.drain()
                yield
                best, second, third = (grp[:, i, :] for i in range(3))
                dve.tensor_tensor(best, pair_hi[:, :, 0], pair_hi[:, :, 1], ALU.max)
                dve.tensor_tensor(second, pair_hi[:, :, 0], pair_hi[:, :, 1], ALU.min)
                dve.tensor_tensor(third, pair_lo[:, :, 0], pair_lo[:, :, 1], ALU.max)
                dve.drain()
                yield
                dve.tensor_tensor(second, second, third, ALU.max)
                dve.drain()
                yield
                dve.tensor_tensor(best, best, second, ALU.add)
                dve.drain()
                yield
                other = groups(best).unsqueeze(2).broadcast_to([P, UT, NGR, NGR])
                own = groups(best).unsqueeze(3).broadcast_to([P, UT, NGR, NGR])
                four = lambda t: t[:, :, :].rearrange("p (t g) h -> p t g h", t=UT)
                dve.tensor_tensor(four(ahead), other, own, ALU.is_gt)
                dve.tensor_tensor(four(ties), other, own, ALU.is_equal)
                dve.drain()
                yield
                dve.tensor_tensor(four(ties), four(ties), earlier[:, :, :].unsqueeze(1).broadcast_to([P, UT, NGR, NGR]), ALU.mult)
                dve.drain()
                yield
                dve.tensor_tensor(ahead[:, :, :], ahead[:, :, :], ties[:, :, :], ALU.add)
                dve.drain()
                yield
                dve.tensor_reduce(grp[:, 2, :], ahead[:, :, :], axis=AX.X, op=ALU.add)
                dve.memset(masked[:, :, :], 0.0)
                dve.drain()
                yield
                dve.tensor_single_scalar(chosen[:, :], grp[:, 2, :], float(TOPG), op=ALU.is_lt)
                dve.drain()
                yield
                dve.copy_predicated(masked[:, :, :].rearrange("p t (g r) -> p (t g) r", r=EPG),
                                    chosen[:, :].unsqueeze(2).broadcast_to([P, UG, EPG]), pairs)
                dve.drain()
                yield
                for t in range(UT):
                    dve.max(top[:, t, :], masked[:, t, :])
                dve.drain()
                yield
                for t in range(UT):
                    dve.max_index(top_idx[:, t, :], top[:, t, :], masked[:, t, :])
                dve.drain()
                yield
                dve.tensor_copy(expert[:, :, :], top_idx[:, :, 0:TOPK])
                dve.drain()
                yield
                flat = lambda t: t[:, :, :, :].rearrange("p t k e -> p (t k) e")
                dve.tensor_tensor(flat(onehot), iota[:, :].unsqueeze(1).broadcast_to([P, UT * TOPK, NE]),
                                  expert[:, :, :].rearrange("p t k -> p (t k)").unsqueeze(2).broadcast_to([P, UT * TOPK, NE]),
                                  ALU.is_equal)
                dve.drain()
                yield
                with nc.allow_low_precision("0 or 1"):
                    dve.tensor_reduce(sel[:, :, :], onehot[:, :, :, :].rearrange("p t k e -> p t e k"), axis=AX.X, op=ALU.add).then_inc(sel_done.sem, 1)
                dve.tensor_tensor(picked[:, :, :, :], onehot[:, :, :, :], score[:, :, :].unsqueeze(2).broadcast_to([P, UT, TOPK, NE]), ALU.mult)
                dve.drain()
                yield
                dve.tensor_reduce(weight[:, :, :], picked[:, :, :, :], axis=AX.X, op=ALU.add)
                dve.drain()
                yield
                dve.tensor_reduce(den[:, :], weight[:, :, :], axis=AX.X, op=ALU.add)
                dve.drain()
                yield
                dve.tensor_scalar_add(den[:, :], den[:, :], 1e-20)
                dve.drain()
                yield
                dve.reciprocal(den[:, :], den[:, :])
                dve.drain()
                yield
                dve.tensor_scalar_mul(den[:, :], den[:, :], ROUTE_SCALE).then_inc(chosen_done.sem, 1)

            def give_slots(u, half):
                slot_free.wait(dve, u - 1)
                pos_done.wait(dve, u + 1)
                chosen_done.wait(dve, u + 1)
                dve.tensor_tensor(picked[:, :, :, :], onehot[:, :, :, :],
                                  ps_pos[:, 0:UT * NE].rearrange("p (t e) -> p t e", t=UT).unsqueeze(2).broadcast_to([P, UT, TOPK, NE]), ALU.mult)
                pairs = info[half][:, :, :].rearrange("p (t k) c -> p t k c", t=UT)
                dve.tensor_tensor(pairs[:, :, :, 1], weight[:, :, :], den[:, :].unsqueeze(2).broadcast_to([P, UT, TOPK]), ALU.mult)
                dve.tensor_copy(pairs[:, :, :, 0], tok[:, :].unsqueeze(2).broadcast_to([P, UT, TOPK]))
                dve.tensor_reduce(sel_sum[:, :], sel[:, :, :].rearrange("p t e -> p e t"), axis=AX.X, op=ALU.add)
                dve.drain()
                dve.tensor_tensor(sel_acc[:, :], sel_acc[:, :], sel_sum[:, :], ALU.add)
                dve.tensor_reduce(place[:, :, :], picked[:, :, :, :], axis=AX.X, op=ALU.add)
                dve.tensor_scalar_add(tok[:, :], tok[:, :], float(UNIT))
                dve.drain()
                dve.tensor_scalar(over[:, :, :], place[:, :, :], float(CAP), float(SLOTS), ALU.is_ge, ALU.mult)
                dve.scalar_tensor_tensor(place[:, :, :], expert[:, :, :], float(CAP), place[:, :, :], op0=ALU.mult, op1=ALU.add)
                dve.drain()
                dve.tensor_tensor(slot[half][:, :].rearrange("p (t k) -> p t k", t=UT), place[:, :, :], over[:, :, :], ALU.add).then_inc(slot_done.sem, 1)

            def low_turned(u, t):
                hi_done.wait(dve, UT * u + t + 1)
                cols = slice(t * P, (t + 1) * P)
                dve.tensor_tensor(hT_lo[:, :, cols], ps_t[t % 2][:, :].rearrange("p (k c) -> p k c", k=DK),
                                  raw(hT_hi[:, :, cols]), ALU.subtract).then_inc(lo_done.sem, 1)

            attend(0, 0)
            low_weights(NW_H, NW_UP)
            for t in range(UT):
                low_turned(0, t)
            low_weights(NW_UP, NW)

            def body(b, half, more):
                u = b * HALVES + half
                choosing = choose(u - 1) if not isinstance(u, int) or u else iter(())
                for n in range(UP):
                    ahi_done.wait(dve, UP * u + n + 1)
                    dve.tensor_tensor(a_lo[:, n, :], relu[n % RELU][:, :], raw(a_hi[:, n, :]), ALU.subtract).then_inc(alo_done.sem, 1)
                    for _ in range(CHOICE_STEPS):
                        next(choosing, None)
                for _ in choosing:
                    pass
                if more:
                    attend(*((b, 1) if half == 0 else (b + 1, 0)))
                else:
                    give_slots(u - 1, 1 - half)
                    for _ in choose(u):
                        pass
                gb_in.wait(dve, 16 * (b + 1))
                for t in range(UT):
                    down_done.wait(dve, UT * u + t + 1)
                    if t:
                        out_done.wait(dve, UT * u + t)
                    dve.tensor_tensor(att[:, :], ps_m[t % RING][:, :], gb[:, :], ALU.mult).then_inc(fin_done.sem, 1)
                    fin_done.wait(dve, UT * u + t + 1)
                    dve.tensor_tensor(x_sb[half][:, t, :], x_sb[half][:, t, :], att[:, :], ALU.add).then_inc(out_done.sem, 1)
                    if more:
                        for t2 in TURNS[t]:
                            low_turned(u + 1, t2)
                    elif t == 1:
                        give_slots(u, half)
                if more and (not isinstance(u, int) or u):
                    give_slots(u - 1, 1 - half)

            steps(dve, body)

        @block.tensor
        def _(pe):
            THREE = ((0, 0), (0, 1), (1, 0))

            def exact(bank, pairs):
                for i, (a, c) in enumerate(pairs):
                    for j, (m, n) in enumerate(THREE):
                        last = pe.matmul(bank, a[m], c[n], start=i + j == 0, stop=i + 1 == len(pairs) and j == 2)
                return last

            def project(b, half, free):
                u = b * HALVES + half
                o_in.wait(pe, 32 * (u + 1))
                for t in range(UT):
                    free(t)
                    cols = slice(t * P, (t + 1) * P)
                    exact(ps_m[t % RING][:, :], [((o_hi[:, g, cols], o_lo[:, g, cols]), (wo_hi[:, g, :], wo_lo[:, g, :]))
                                                 for g in range(NG)]).then_inc(proj_done.sem, 1)

            pool_own.wait(pe, 5)
            w_lo_done.wait(pe, 2)
            project(0, 0, lambda t: None)
            def turn(u, t):
                h_done.wait(pe, UT * u + t + 1)
                lo_done.wait(pe, UT * u + t - 1)
                for k in range(DK):
                    last = pe.transpose(ps_t[t % 2][:, k * P:(k + 1) * P], h2[:, t, k * P:(k + 1) * P], ident[:, :])
                last.then_inc(tr_done.sem, 1)

            def places(u):
                sel_done.wait(pe, u + 1)
                slot_done.wait(pe, u)
                for t in range(UT):
                    bank = ps_pos[:, t * NE:(t + 1) * NE]
                    pe.matmul(bank, before[:, :], sel[:, t, :], start=True, stop=False)
                    for t2 in range(t):
                        pe.matmul(bank, ones[:, :], sel[:, t2, :], start=False, stop=False)
                    last = pe.matmul(bank, ones[:, :], sel_acc[:, :], start=False, stop=True)
                last.then_inc(pos_done.sem, 1)

            for t in range(UT):
                turn(0, t)

            def body(b, half, more):
                u = b * HALVES + half
                first = isinstance(u, int) and u == 0
                lo_done.wait(pe, UT * (u + 1))
                if first:
                    w_lo_done.wait(pe, NW_UP)
                score_done.wait(pe, u)
                for t in range(UT):
                    cols = slice(t * P, (t + 1) * P)
                    last = exact(ps_g[:, t * NE:(t + 1) * NE], [((hT_hi[:, k, cols], hT_lo[:, k, cols]), (gt_hi[:, k, :], gt_lo[:, k, :]))
                                                               for k in range(DK)])
                last.then_inc(gate_done.sem, 1)
                for n in range(UP):
                    if n < RING:
                        fin_done.wait(pe, UT * (u - 1) + n + 1)
                    else:
                        relu_done.wait(pe, UP * u + n - RING + 1)
                    cols = slice(n * P, (n + 1) * P)
                    exact(ps_m[n % RING][:, :], [((up_hi[:, k, cols], up_lo[:, k, cols]), (hT_hi[:, k, :], hT_lo[:, k, :]))
                                                 for k in range(DK)]).then_inc(up_done.sem, 1)
                if more:
                    project(*((b, 1) if half == 0 else (b + 1, 0)), lambda t: relu_done.wait(pe, UP * u + UP - RING + t + 1))
                if not first:
                    places(u - 1)
                alo_done.wait(pe, UP * (u + 1))
                if first:
                    w_lo_done.wait(pe, NW)
                for t in range(UT):
                    if more:
                        att_done.wait(pe, UT * (u + 1) + t + 1)
                    else:
                        relu_done.wait(pe, UP * (u + 1))
                    cols = slice(t * P, (t + 1) * P)
                    exact(ps_m[t % RING][:, :], [((a_hi[:, n, cols], a_lo[:, n, cols]), (dn_hi[:, n, :], dn_lo[:, n, :]))
                                                 for n in range(UP)]).then_inc(down_done.sem, 1)
                    if more:
                        for t2 in TURNS[t]:
                            turn(u + 1, t2)
                    elif t == 1:
                        places(u)

            steps(pe, body)


def stage_experts(nc, e_upT, e_downT, h2_dram, mod_dram, info_dram, out):
    J, HT = CAP // P, HID // P
    AHEAD, R = 2, 4
    NK = NB + 1
    with ExitStack() as ctx:
        s = Scope(nc, ctx, "exp_")
        two, ring = range(2), range(R)
        upr, dnr = ([s.sb(f"{n}{p}", sh, FP32) for p in two] for n, sh in (("upr", [P, DK, HID]), ("dnr", [P, HT, D])))
        up_hi, up_lo = ([s.sb(f"{n}{p}", [P, DK, HID], F32R) for p in two] for n in ("up_hi", "up_lo"))
        dn_hi, dn_lo = ([s.sb(f"{n}{p}", [P, HT, D], F32R) for p in two] for n in ("dn_hi", "dn_lo"))
        info = s.sb("info", [P, NE * J, 2], FP32)
        tok_all = s.sb("tok_all", [P, NE * J], I32)
        batch_i = s.sb("batch_i", [P, NE * J], I32)
        batch = s.sb("batch", [P, NE * J], FP32)
        iota_i, iota = s.sb("iota_i", [P, NK], I32), s.sb("iota", [P, NK], FP32)
        tok_get = [s.sb(f"tok_get{r}", [P, J], I32) for r in ring]
        tok_add = [s.sb(f"tok_add{r}", [P, J], I32) for r in ring]
        weight = [s.sb(f"weight{r}", [P, J], FP32) for r in ring]
        onehot = s.sb("onehot", [P, J, NK], FP32)
        onehotT = [s.sb(f"onehotT{p}", [NK, CAP], F32R) for p in two]
        gb = s.sb("gb", [NK, D], FP32)
        gb_hi, gb_lo = s.sb("gb_hi", [NK, D], F32R), s.sb("gb_lo", [NK, D], F32R)
        gate = s.sb("gate", [P, J, D], FP32)
        xg = [s.sb(f"xg{r}", [P, J, D], FP32) for r in ring]
        xT_hi, xT_lo = ([s.sb(f"{n}{p}", [P, DK, CAP], F32R) for p in two] for n in ("xT_hi", "xT_lo"))
        relu = s.sb("relu", [P, HT, CAP], FP32)
        a_hi, a_lo = ([s.sb(f"{n}{p}", [P, HT, CAP], F32R) for p in two] for n in ("a_hi", "a_lo"))
        y = [s.sb(f"y{p}", [P, J, D], FP32) for p in two]
        ident = s.sb("ident", [P, P], FP32)
        ps_t = [s.ps(f"ps_t{n}") for n in range(2)]
        ps_u, ps_o = s.ps("ps_u"), s.ps("ps_o", (NK, CAP))
        ps_y, ps_g = ([s.ps(f"{n}{j}") for j in range(J)] for n in ("ps_y", "ps_g"))

        w_in = s.sems("w_in", 2)
        consts, pool_own, iota_done = s.sem("consts"), s.sem("pool_own"), s.sem("iota")
        x_in, added = s.sems("x_in", R, credit=0), s.sem("added", credit=0)
        mark, dve_mark, added_seen = s.sem("mark"), s.sem("dve_mark"), s.sem("added_seen")
        slots_done, gb_hi_done, gb_done = s.sem("slots"), s.sem("gb_hi"), s.sem("gb")
        get_done, aux_done = s.sem("get"), s.sem("aux")
        uphi_done, dnhi_done, uplo_done, dnlo_done = s.sem("uphi"), s.sem("dnhi"), s.sem("uplo"), s.sem("dnlo")
        tr_done, xhi_done, xlo_done = s.sem("tr"), s.sem("xhi"), s.sem("xlo")
        up_done, relu_done, sq_done = s.sem("up"), s.sem("relu"), s.sem("sq")
        ahi_done, alo_done = s.sem("ahi"), s.sem("alo")
        ot_done, oht_done, gate_done = s.sem("ot"), s.sem("oht"), s.sem("gate")
        y_mm, g_mm, y_done = s.sem("y_mm"), s.sem("g_mm"), s.sem("y")
        block = ctx.enter_context(nc.Block())

        def live(e):
            return not isinstance(e, int) or 0 <= e < NE

        def steps(eng, body):
            for e in range(-AHEAD, 0):
                body(e, R + e, -1)
            with eng.Fori(0, NE // R - 1) as i:
                for r in ring:
                    body(i * R + r, r, i)
            for r in ring:
                body(NE - R + r, r, NE // R - 1)

        @block.sync
        def _(sp):
            s.give_credit(sp)
            sp.dma_start(info[:, :, :], info_dram.rearrange("(n p) c -> p n c", p=P)).then_inc(consts.sem, 16)
            sp.dma_start(gb[:, :], mod_dram[:, M_GB, :]).then_inc(consts.sem, 16)

            def load(e, p):
                uplo_done.wait(sp, e - 1)
                dnlo_done.wait(sp, e - 1)
                sp.dma_start(upr[p][:, :, :], e_upT[bass.ds(e, 1), :, :].rearrange("o (k p) n -> p (o k) n", p=P)).then_inc(w_in[p].sem, 16)
                sp.dma_start(dnr[p][:, :, :], e_downT[bass.ds(e, 1), :, :].rearrange("o (k p) n -> p (o k) n", p=P)).then_inc(w_in[p].sem, 16)

            for e in two:
                load(e, e)
            with sp.Fori(1, NE // 2) as i:
                for p in two:
                    load(i * 2 + p, p)

        @block.gpsimd
        def _(pool):
            make_identity(pool, ident, pool_own, 0)
            pool.iota(iota_i[:, :], pattern=[[1, NK]], base=0, channel_multiplier=0).then_inc(iota_done.sem, 1)

            def gather(e, slot):
                hold(pool, get_done, e + 1, mark)
                for j in range(J):
                    pool.indirect_dma_start(xg[slot][:, j, :], None, h2_dram[:, :],
                                            bass.IndirectOffsetOnAxis(tok_get[slot][:, j:j + 1].bitcast(U32), 0)).then_inc(x_in[slot].sem, 16)

            def add(e, r):
                if not isinstance(e, int) or e:
                    hold(pool, added, 16 * J * e, added_seen)
                hold(pool, y_done, J * (e + 1), mark)
                for j in range(J):
                    pool.indirect_dma_start(out[:, :], bass.IndirectOffsetOnAxis(tok_add[r][:, j:j + 1].bitcast(U32), 0),
                                            y[r % 2][:, j, :], None, compute_op=ALU.add).then_inc(added.sem, 16)

            def body(e, r):
                if not isinstance(e, int) or e + R < NE:
                    gather(e + R, r)
                add(e, r)

            for n in ring:
                gather(n, n)
            body(0, 0)
            with pool.Fori(0, NE // R - 2) as i:
                for r in ring:
                    body(i * R + r + 1, (r + 1) % R)
            for e in range(NE - 2 * R + 1, NE):
                body(e, e % R)
            added.wait(pool, 16 * J * NE)

        @block.scalar
        def _(act):
            consts.wait(act, 32)
            act.activation(gb_hi[:, :], gb[:, :], ACT.Copy).then_inc(gb_hi_done.sem, 1)

            def body(e, r, i):
                half = i * (R // 2)
                if live(e + 2):
                    w_in[r % 2].wait(act, 32 * (half + (r + 2) // 2 + 1))
                    up_done.wait(act, e + 1)
                    act.activation(up_hi[r % 2][:, :, :], upr[r % 2][:, :, :], ACT.Copy).then_inc(uphi_done.sem, 1)
                if live(e + 1):
                    q = (r + 1) % 2
                    y_mm.wait(act, J * e)
                    act.activation(dn_hi[q][:, :, :], dnr[q][:, :, :], ACT.Copy).then_inc(dnhi_done.sem, 1)
                if live(e + 2):
                    for n in range(2):
                        tr_done.wait(act, 2 * (e + 2) + n + 1)
                        act.activation(xT_hi[r % 2][:, 2 * n:2 * n + 2, :].rearrange("p k c -> p (k c)"), ps_t[n][:, :], ACT.Copy).then_inc(xhi_done.sem, 1)
                if live(e + 1):
                    up_done.wait(act, e + 2)
                    alo_done.wait(act, e + 1)
                    act.activation(relu[:, :, :].rearrange("p n c -> p (n c)"), ps_u[:, :], ACT.Relu).then_inc(relu_done.sem, 1)
                    sq_done.wait(act, e + 2)
                    act.activation(a_hi[q][:, :, :], relu[:, :, :], ACT.Copy).then_inc(ahi_done.sem, 1)
                if live(e):
                    y_done.wait(act, J * e)
                    for j in range(J):
                        g_mm.wait(act, J * e + j + 1)
                        act.activation(gate[:, j, :], ps_g[j][:, :], ACT.Copy).then_inc(gate_done.sem, 1)
                if live(e + 1):
                    ot_done.wait(act, e + 2)
                    act.activation(onehotT[q][:, :], ps_o[:, :], ACT.Copy).then_inc(oht_done.sem, 1)

            steps(act, body)

        @block.vector
        def _(dve):
            consts.wait(dve, 32)
            dve.tensor_copy(tok_all[:, :], info[:, :, 0])
            iota_done.wait(dve, 1)
            dve.tensor_copy(iota[:, :], iota_i[:, :])
            dve.drain()
            dve.tensor_single_scalar(batch_i[:, :], tok_all[:, :], S.bit_length() - 1, op=ALU.logical_shift_right)
            for r in ring:
                dve.tensor_copy(tok_get[r][:, :], tok_all[:, r * J:(r + 1) * J]).then_inc(get_done.sem, 1)
            dve.drain()
            dve.tensor_copy(batch[:, :], batch_i[:, :]).then_inc(slots_done.sem, 1)
            gb_hi_done.wait(dve, 1)
            dve.tensor_tensor(gb_lo[:, :], gb[:, :], raw(gb_hi[:, :]), ALU.subtract).then_inc(gb_done.sem, 1)
            slots_done.wait(dve, 1)

            def body(e, r, i):
                if live(e + 1):
                    n, q = (r + 1) % R, (r + 1) % 2
                    cols = bass.ds((e + 1) * J, J)
                    hold(dve, added_seen, e - 3, dve_mark)
                    dve.tensor_copy(tok_add[n][:, :], tok_all[:, cols])
                    dve.tensor_copy(weight[n][:, :], info[:, cols, 1])
                    ot_done.wait(dve, e + 1)
                    dve.tensor_tensor(onehot[:, :, :], batch[:, cols].unsqueeze(2).broadcast_to([P, J, NK]),
                                      iota[:, :].unsqueeze(1).broadcast_to([P, J, NK]), ALU.is_equal).then_inc(aux_done.sem, 1)
                if live(e) and live(e + R):
                    hold(dve, tr_done, 2 * (e + 1), dve_mark)
                    dve.tensor_copy(tok_get[r][:, :], tok_all[:, bass.ds((e + R) * J, J)]).then_inc(get_done.sem, 1)
                if live(e + 2):
                    uphi_done.wait(dve, e + 3)
                    dve.tensor_tensor(up_lo[r % 2][:, :, :], upr[r % 2][:, :, :], raw(up_hi[r % 2][:, :, :]), ALU.subtract).then_inc(uplo_done.sem, 1)
                if live(e + 1):
                    dnhi_done.wait(dve, e + 2)
                    dve.tensor_tensor(dn_lo[q][:, :, :], dnr[q][:, :, :], raw(dn_hi[q][:, :, :]), ALU.subtract).then_inc(dnlo_done.sem, 1)
                if live(e + 2):
                    for n in range(2):
                        xhi_done.wait(dve, 2 * (e + 2) + n + 1)
                        dve.tensor_tensor(xT_lo[r % 2][:, 2 * n:2 * n + 2, :].rearrange("p k c -> p (k c)"), ps_t[n][:, :],
                                          raw(xT_hi[r % 2][:, 2 * n:2 * n + 2, :]).rearrange("p k c -> p (k c)"), ALU.subtract).then_inc(xlo_done.sem, 1)
                if live(e + 1):
                    relu_done.wait(dve, e + 2)
                    dve.tensor_tensor(relu[:, :, :], relu[:, :, :], relu[:, :, :], ALU.mult).then_inc(sq_done.sem, 1)
                    ahi_done.wait(dve, e + 2)
                    dve.tensor_tensor(a_lo[q][:, :, :], relu[:, :, :], raw(a_hi[q][:, :, :]), ALU.subtract).then_inc(alo_done.sem, 1)
                if live(e):
                    added_seen.wait(dve, e - 1)
                    gate_done.wait(dve, J * (e + 1))
                    for j in range(J):
                        y_mm.wait(dve, J * e + j + 1)
                        dve.scalar_tensor_tensor(y[r % 2][:, j, :], ps_y[j][:, :], weight[r][:, j:j + 1], gate[:, j, :],
                                                 op0=ALU.mult, op1=ALU.mult).then_inc(y_done.sem, 1)

            steps(dve, body)

        @block.tensor
        def _(pe):
            THREE = ((0, 0), (0, 1), (1, 0))
            pool_own.wait(pe, 2)
            gb_done.wait(pe, 1)

            def body(e, r, i):
                p, q = r % 2, (r + 1) % 2
                if live(e + 2):
                    slot = (r + 2) % R
                    x_in[slot].wait(pe, 16 * J * (i + (r + 2) // R + 1))
                    for n in range(2):
                        xlo_done.wait(pe, 2 * (e + 1) + n + 1)
                        for k in (2 * n, 2 * n + 1):
                            for j in range(J):
                                col = (k % 2) * CAP + j * P
                                last = pe.transpose(ps_t[n][:, col:col + P], xg[slot][:, j, k * P:(k + 1) * P], ident[:, :])
                        last.then_inc(tr_done.sem, 1)
                if live(e + 1):
                    xlo_done.wait(pe, 2 * (e + 2))
                    uplo_done.wait(pe, e + 2)
                    relu_done.wait(pe, e + 1)
                    for n in range(HT):
                        for k in range(DK):
                            for a, c in THREE:
                                last = pe.matmul(ps_u[:, n * CAP:(n + 1) * CAP], (up_hi, up_lo)[a][q][:, k, n * P:(n + 1) * P],
                                                 (xT_hi, xT_lo)[c][q][:, k, :], start=k + a + c == 0, stop=k == DK - 1 and a == 1)
                    last.then_inc(up_done.sem, 1)
                if live(e):
                    oht_done.wait(pe, e + 1)
                    gate_done.wait(pe, J * e)
                    for j in range(J):
                        for half in (gb_hi, gb_lo):
                            last = pe.matmul(ps_g[j][:, :], onehotT[p][:, j * P:(j + 1) * P], half[:, :], start=half is gb_hi, stop=half is gb_lo)
                        last.then_inc(g_mm.sem, 1)
                    alo_done.wait(pe, e + 1)
                    dnlo_done.wait(pe, e + 1)
                    y_done.wait(pe, J * e)
                    for j in range(J):
                        for n in range(HT):
                            for a, c in THREE:
                                last = pe.matmul(ps_y[j][:, :], (a_hi, a_lo)[a][p][:, n, j * P:(j + 1) * P],
                                                 (dn_hi, dn_lo)[c][p][:, n, :], start=n + a + c == 0, stop=n == HT - 1 and a == 1)
                        last.then_inc(y_mm.sem, 1)
                if live(e + 1):
                    aux_done.wait(pe, e + 2)
                    oht_done.wait(pe, e + 1)
                    for j in range(J):
                        last = pe.transpose(ps_o[:, j * P:(j + 1) * P], onehot[:, j, :], ident[:, :])
                    last.then_inc(ot_done.sem, 1)

            steps(pe, body)


def build(nc, x, cT, wmod, wqkvT, bqk, bv, woT, bo, gateT, bias, sh_upT, sh_downT, e_upT, e_downT, out):
    mod_dram = nc.dram_tensor("mod_rows", [NB + 1, 6, D], FP32, kind="Internal").ap()
    qk_dram = nc.dram_tensor("qk_parts", [4, NB * NG, P, S], FP32, kind="Internal").ap()
    v_dram = nc.dram_tensor("v_rows", [NB * NG, S, P], FP32, kind="Internal").ap()
    o_dram = nc.dram_tensor("o_parts", [2, NB * NG, P, S], FP32, kind="Internal").ap()
    h2_dram = nc.dram_tensor("h2_rows", [T + CAP, D], FP32, kind="Internal").ap()
    info_dram = nc.dram_tensor("slot_info", [SLOTS, 2], FP32, kind="Internal").ap()
    stage_modulation(nc, cT, wmod, mod_dram, h2_dram, info_dram, out)
    stage_qkv(nc, x, wqkvT, bqk, bv, mod_dram, qk_dram, v_dram)
    stage_attention(nc, qk_dram, v_dram, o_dram)
    stage_project_route_shared(nc, x, o_dram, mod_dram, woT, bo, gateT, bias, sh_upT, sh_downT, h2_dram, info_dram, out)
    stage_experts(nc, e_upT, e_downT, h2_dram, mod_dram, info_dram, out)


def kernel(L0_attn_x, L0_attn_w_q, L0_attn_b_q, L0_attn_w_k, L0_attn_b_k, L0_attn_w_v, L0_attn_b_v, L0_attn_w_o,
           L0_attn_b_o, L0_ffn_gate_w, L0_ffn_bias_corr, L0_ffn_up_w, L0_ffn_down_w, L0_ffn_shared_up_w,
           L0_ffn_shared_down_w, L0_c, L0_wmod):
    import concourse.bacc as bacc
    from concourse.bass_utils import run_bass_kernel_spmd

    a = np.asarray
    arrays = {
        "x": a(L0_attn_x),
        "cT": a(L0_c).T,
        "wmod": a(L0_wmod),
        "wqkvT": np.stack([a(w).T for w in (L0_attn_w_q, L0_attn_w_k, L0_attn_w_v)]),
        "bqk": np.concatenate([a(b).reshape(NG, P).T for b in (L0_attn_b_q, L0_attn_b_k)], axis=1),
        "bv": a(L0_attn_b_v).reshape(1, D),
        "woT": a(L0_attn_w_o).T,
        "bo": a(L0_attn_b_o).reshape(1, D),
        "gateT": a(L0_ffn_gate_w).T,
        "bias": a(L0_ffn_bias_corr).reshape(1, NE),
        "sh_upT": a(L0_ffn_shared_up_w).T,
        "sh_downT": a(L0_ffn_shared_down_w).T,
        "e_upT": a(L0_ffn_up_w).transpose(0, 2, 1),
        "e_downT": a(L0_ffn_down_w).transpose(0, 2, 1),
    }
    arrays = {n: np.ascontiguousarray(v) for n, v in arrays.items()}
    nc = bacc.Bacc("TRN2", target_bir_lowering=False, num_devices=1)
    args = [nc.dram_tensor(n, v.shape, mybir.dt.from_np(v.dtype), kind="ExternalInput").ap() for n, v in arrays.items()]
    out = nc.dram_tensor("out", (T + CAP, D), FP32, kind="ExternalOutput").ap()
    build(nc, *args, out)
    r = run_bass_kernel_spmd(nc, [arrays], core_ids=[0])
    return r.results[0]["out"][:T].reshape(NB, S, D)
```
